# Optimizing a Trainium2 kernel written in Bass

```python
import numpy as np
import jax
import jax.numpy as jnp

def _softmax(x, axis=-1):
    return jax.nn.softmax(x, axis=axis)

def _gelu(x):
    return jax.nn.gelu(x, approximate=True)

def _silu(x):
    return jax.nn.silu(x)

def _sigmoid(x):
    return jax.nn.sigmoid(x)

def _layernorm(x, axis=-1, eps=1e-05):
    m = jnp.mean(x, axis=axis, keepdims=True)
    v = jnp.var(x, axis=axis, keepdims=True)
    return (x - m) / jnp.sqrt(v + eps)

def _scatter_add(tgt, idx, src, axis=0):
    return tgt.at[idx].add(src)

def _segment_sum(src, seg, n):
    return jax.ops.segment_sum(src, seg, n)
kernel_name = 'mk_recurrent_d2_jaxref_r8_426724'

def setup_inputs(seed: int=0):
    np.random.seed(seed)
    _w = jnp.asarray

    def _L0_attn_setup():
        import jax, jax.numpy as jnp
        import numpy as np
        import math
        D_MODEL = 128
        N_HEADS = 16
        D_K = D_MODEL // N_HEADS
        MAX_REL = 32
        key = jax.random.key(seed)
        ks = jax.random.split(key, 8)
        B, S = (8, 128)
        x = jax.random.normal(ks[0], (B, S, D_MODEL), dtype=jnp.float32)
        scale = 1.0 / math.sqrt(D_MODEL)
        Wq = jax.random.normal(ks[1], (D_MODEL, D_MODEL), dtype=jnp.float32) * scale
        Wk = jax.random.normal(ks[2], (D_MODEL, D_MODEL), dtype=jnp.float32) * scale
        Wv = jax.random.normal(ks[3], (D_MODEL, D_MODEL), dtype=jnp.float32) * scale
        Wo = jax.random.normal(ks[4], (D_MODEL, D_MODEL), dtype=jnp.float32) * scale
        b_o = jnp.zeros((D_MODEL,), dtype=jnp.float32)
        rel_k_emb = jax.random.normal(ks[5], (2 * MAX_REL + 1, D_K), dtype=jnp.float32) * 0.02
        rel_v_emb = jax.random.normal(ks[6], (2 * MAX_REL + 1, D_K), dtype=jnp.float32) * 0.02
        return {'x': x, 'Wq': Wq, 'Wk': Wk, 'Wv': Wv, 'Wo': Wo, 'b_o': b_o, 'rel_k_emb': rel_k_emb, 'rel_v_emb': rel_v_emb}
    _L0_attn_in = _L0_attn_setup()

    def _L0_ffn_setup():
        import jax, jax.numpy as jnp
        import numpy as np
        N_HEAD = 16
        NUM_EXPERTS = 8
        TOP_K = 2
        LN_EPS = 1e-05

        def _layernorm(x, g, b):
            mu = jnp.mean(x, axis=-1, keepdims=True)
            var = jnp.mean(jnp.square(x - mu), axis=-1, keepdims=True)
            return (x - mu) * jax.lax.rsqrt(var + LN_EPS) * g + b

        def _attention(h, Wq, bq, Wk, bk, Wv, bv, Wp, bp):
            B, T, D = h.shape
            hd = D // N_HEAD

            def split(z):
                return z.reshape(B, T, N_HEAD, hd).transpose(0, 2, 1, 3)
            q = split(h @ Wq + bq)
            k = split(h @ Wk + bk)
            v = split(h @ Wv + bv)
            att = jnp.einsum('bhqd,bhkd->bhqk', q, k) / jnp.sqrt(jnp.float32(hd))
            causal = jnp.tril(jnp.ones((T, T), bool))
            att = jnp.where(causal, att, -jnp.inf)
            att = jax.nn.softmax(att, axis=-1)
            y = jnp.einsum('bhqk,bhkd->bhqd', att, v)
            y = y.transpose(0, 2, 1, 3).reshape(B, T, D)
            return y @ Wp + bp

        def _token_moe(h, gate_W, gate_b, exp_W1, exp_b1, exp_W2, exp_b2):
            B, T, D = h.shape
            flat = h.reshape(-1, D)
            N = flat.shape[0]
            logits = flat @ gate_W + gate_b
            top_v, top_i = jax.lax.top_k(logits, TOP_K)
            w = jax.nn.softmax(top_v, axis=-1)
            w_full = jnp.zeros((N, NUM_EXPERTS), flat.dtype)
            w_full = w_full.at[jnp.arange(N)[:, None], top_i].add(w)
            out = jnp.zeros_like(flat)
            for e in range(NUM_EXPERTS):
                mid = jax.nn.gelu(flat @ exp_W1[e] + exp_b1[e], approximate=False)
                y_e = mid @ exp_W2[e] + exp_b2[e]
                out = out + w_full[:, e:e + 1] * y_e
            return out.reshape(B, T, D)
        key = jax.random.key(seed)
        B, T, D = (8, 128, 128)
        H = 4 * D
        E = NUM_EXPERTS
        ks = jax.random.split(key, 24)
        s = 0.02
        inp = {'x': jax.random.normal(ks[0], (B, T, D), jnp.float32), 'ln1_g': jnp.ones((D,), jnp.float32), 'ln1_b': jnp.zeros((D,), jnp.float32), 'ln2_g': jnp.ones((D,), jnp.float32), 'ln2_b': jnp.zeros((D,), jnp.float32), 'Wq': jax.random.normal(ks[1], (D, D), jnp.float32) * s, 'bq': jnp.zeros((D,), jnp.float32), 'Wk': jax.random.normal(ks[2], (D, D), jnp.float32) * s, 'bk': jnp.zeros((D,), jnp.float32), 'Wv': jax.random.normal(ks[3], (D, D), jnp.float32) * s, 'bv': jnp.zeros((D,), jnp.float32), 'Wp': jax.random.normal(ks[4], (D, D), jnp.float32) * s, 'bp': jnp.zeros((D,), jnp.float32), 'gate_W': jax.random.normal(ks[5], (D, E), jnp.float32) * s, 'gate_b': jnp.zeros((E,), jnp.float32), 'exp_W1': jax.random.normal(ks[6], (E, D, H), jnp.float32) * s, 'exp_b1': jnp.zeros((E, H), jnp.float32), 'exp_W2': jax.random.normal(ks[7], (E, H, D), jnp.float32) * s, 'exp_b2': jnp.zeros((E, D), jnp.float32)}
        return inp
    _L0_ffn_in = _L0_ffn_setup()

    def _L1_attn_setup():
        import jax, jax.numpy as jnp
        import numpy as np
        B, T, D = (1, 256, 128)
        H, DH, DV, DF = (16, 64, 64, 512)
        EPS_LN = 1e-05
        EPS_DEN = 1e-06

        def _layernorm(x, g, b):
            m = jnp.mean(x, axis=-1, keepdims=True)
            v = jnp.mean((x - m) ** 2, axis=-1, keepdims=True)
            return (x - m) / jnp.sqrt(v + EPS_LN) * g + b

        def _phi(x):
            return jax.nn.elu(x) + 1.0

        def _linear_attention(x, Wq, Wk, Wv, Wo):
            b, t, d = x.shape
            Q = _phi((x @ Wq).reshape(b, t, H, DH)).transpose(0, 2, 1, 3)
            K = _phi((x @ Wk).reshape(b, t, H, DH)).transpose(0, 2, 1, 3)
            V = (x @ Wv).reshape(b, t, H, DV).transpose(0, 2, 1, 3)
            KV = jnp.einsum('bhti,bhtj->bhtij', K, V)
            S = jnp.cumsum(KV, axis=2)
            z = jnp.cumsum(K, axis=2)
            num = jnp.einsum('bhti,bhtij->bhtj', Q, S)
            den = jnp.maximum(jnp.einsum('bhti,bhti->bht', Q, z), EPS_DEN)[..., None]
            out = (num / den).transpose(0, 2, 1, 3).reshape(b, t, H * DV)
            return out @ Wo
        key = jax.random.key(seed)
        ks = jax.random.split(key, 8)
        s = 0.02
        return {'x': jax.random.normal(ks[0], (B, T, D), dtype=jnp.float32), 'ln1_g': jnp.ones((D,), jnp.float32), 'ln1_b': jnp.zeros((D,), jnp.float32), 'Wq': jax.random.normal(ks[1], (D, H * DH), jnp.float32) * s, 'Wk': jax.random.normal(ks[2], (D, H * DH), jnp.float32) * s, 'Wv': jax.random.normal(ks[3], (D, H * DV), jnp.float32) * s, 'Wo': jax.random.normal(ks[4], (H * DV, D), jnp.float32) * s, 'ln2_g': jnp.ones((D,), jnp.float32), 'ln2_b': jnp.zeros((D,), jnp.float32), 'Wf1': jax.random.normal(ks[5], (D, DF), jnp.float32) * s, 'Wf2': jax.random.normal(ks[6], (DF, D), jnp.float32) * s}
    _L1_attn_in = _L1_attn_setup()

    def _L1_ffn_setup():
        import jax, jax.numpy as jnp
        import numpy as np
        B, C, D, O = (4, 512, 128, 128)
        PROJ = 32
        RANKS = [1, 2, 4, 8]
        E = len(RANKS)
        CLAMP_MAX = float(np.log(1.0 / 0.01))

        def _l2norm(v, axis):
            return v / jnp.maximum(jnp.linalg.norm(v, axis=axis, keepdims=True), 1e-12)
        key = jax.random.key(seed)
        ks = jax.random.split(key, 16)
        inp = {'x': jax.random.normal(ks[0], (B, C, D), dtype=jnp.float32), 'W': jax.random.normal(ks[1], (O, D), dtype=jnp.float32) / np.sqrt(D), 'Wp': jax.random.normal(ks[2], (PROJ, D), dtype=jnp.float32) / np.sqrt(D), 'bp': jnp.zeros((PROJ,), dtype=jnp.float32), 'sim': jax.random.normal(ks[3], (PROJ, E), dtype=jnp.float32) * 0.01, 'temp': jnp.full((1,), np.log(1.0 / 0.5), dtype=jnp.float32)}
        for i, r in enumerate(RANKS):
            inp[f'Wd{i}'] = jax.random.normal(ks[4 + 2 * i], (r, D), dtype=jnp.float32) / r
            inp[f'Wu{i}'] = jax.random.normal(ks[5 + 2 * i], (O, r), dtype=jnp.float32) * 0.01
        return inp
    _L1_ffn_in = _L1_ffn_setup()
    _d = {'L0_attn_x': _L0_attn_in['x'], 'L0_attn_Wq': _L0_attn_in['Wq'], 'L0_attn_Wk': _L0_attn_in['Wk'], 'L0_attn_Wv': _L0_attn_in['Wv'], 'L0_attn_Wo': _L0_attn_in['Wo'], 'L0_attn_b_o': _L0_attn_in['b_o'], 'L0_attn_rel_k_emb': _L0_attn_in['rel_k_emb'], 'L0_attn_rel_v_emb': _L0_attn_in['rel_v_emb'], 'L0_ffn_ln1_g': _L0_ffn_in['ln1_g'], 'L0_ffn_ln1_b': _L0_ffn_in['ln1_b'], 'L0_ffn_ln2_g': _L0_ffn_in['ln2_g'], 'L0_ffn_ln2_b': _L0_ffn_in['ln2_b'], 'L0_ffn_Wq': _L0_ffn_in['Wq'], 'L0_ffn_bq': _L0_ffn_in['bq'], 'L0_ffn_Wk': _L0_ffn_in['Wk'], 'L0_ffn_bk': _L0_ffn_in['bk'], 'L0_ffn_Wv': _L0_ffn_in['Wv'], 'L0_ffn_bv': _L0_ffn_in['bv'], 'L0_ffn_Wp': _L0_ffn_in['Wp'], 'L0_ffn_bp': _L0_ffn_in['bp'], 'L0_ffn_gate_W': _L0_ffn_in['gate_W'], 'L0_ffn_gate_b': _L0_ffn_in['gate_b'], 'L0_ffn_exp_W1': _L0_ffn_in['exp_W1'], 'L0_ffn_exp_b1': _L0_ffn_in['exp_b1'], 'L0_ffn_exp_W2': _L0_ffn_in['exp_W2'], 'L0_ffn_exp_b2': _L0_ffn_in['exp_b2'], 'L1_attn_ln1_g': _L1_attn_in['ln1_g'], 'L1_attn_ln1_b': _L1_attn_in['ln1_b'], 'L1_attn_Wq': _L1_attn_in['Wq'], 'L1_attn_Wk': _L1_attn_in['Wk'], 'L1_attn_Wv': _L1_attn_in['Wv'], 'L1_attn_Wo': _L1_attn_in['Wo'], 'L1_attn_ln2_g': _L1_attn_in['ln2_g'], 'L1_attn_ln2_b': _L1_attn_in['ln2_b'], 'L1_attn_Wf1': _L1_attn_in['Wf1'], 'L1_attn_Wf2': _L1_attn_in['Wf2'], 'L1_ffn_W': _L1_ffn_in['W'], 'L1_ffn_Wp': _L1_ffn_in['Wp'], 'L1_ffn_bp': _L1_ffn_in['bp'], 'L1_ffn_sim': _L1_ffn_in['sim'], 'L1_ffn_temp': _L1_ffn_in['temp'], 'L1_ffn_Wd0': _L1_ffn_in['Wd0'], 'L1_ffn_Wu0': _L1_ffn_in['Wu0'], 'L1_ffn_Wd1': _L1_ffn_in['Wd1'], 'L1_ffn_Wu1': _L1_ffn_in['Wu1'], 'L1_ffn_Wd2': _L1_ffn_in['Wd2'], 'L1_ffn_Wu2': _L1_ffn_in['Wu2'], 'L1_ffn_Wd3': _L1_ffn_in['Wd3'], 'L1_ffn_Wu3': _L1_ffn_in['Wu3']}
    _x0 = _d['L0_attn_x']
    _d['L0_attn_x'] = jax.random.normal(jax.random.fold_in(jax.random.key(seed), 1), (2, 1024, 128), dtype=_x0.dtype)
    del _x0
    return _d

def reference(L0_attn_x, L0_attn_Wq, L0_attn_Wk, L0_attn_Wv, L0_attn_Wo, L0_attn_b_o, L0_attn_rel_k_emb, L0_attn_rel_v_emb, L0_ffn_ln1_g, L0_ffn_ln1_b, L0_ffn_ln2_g, L0_ffn_ln2_b, L0_ffn_Wq, L0_ffn_bq, L0_ffn_Wk, L0_ffn_bk, L0_ffn_Wv, L0_ffn_bv, L0_ffn_Wp, L0_ffn_bp, L0_ffn_gate_W, L0_ffn_gate_b, L0_ffn_exp_W1, L0_ffn_exp_b1, L0_ffn_exp_W2, L0_ffn_exp_b2, L1_attn_ln1_g, L1_attn_ln1_b, L1_attn_Wq, L1_attn_Wk, L1_attn_Wv, L1_attn_Wo, L1_attn_ln2_g, L1_attn_ln2_b, L1_attn_Wf1, L1_attn_Wf2, L1_ffn_W, L1_ffn_Wp, L1_ffn_bp, L1_ffn_sim, L1_ffn_temp, L1_ffn_Wd0, L1_ffn_Wu0, L1_ffn_Wd1, L1_ffn_Wu1, L1_ffn_Wd2, L1_ffn_Wu2, L1_ffn_Wd3, L1_ffn_Wu3):

    def _L0_attn_ref(x, Wq, Wk, Wv, Wo, b_o, rel_k_emb, rel_v_emb):
        import jax, jax.numpy as jnp
        import numpy as np
        import math
        D_MODEL = 128
        N_HEADS = 16
        D_K = D_MODEL // N_HEADS
        MAX_REL = 32
        B, S, D = x.shape
        H, dk = (N_HEADS, D_K)
        inv_sqrt_dk = 1.0 / math.sqrt(dk)
        Q = (x @ Wq.T).reshape(B, S, H, dk)
        K = (x @ Wk.T).reshape(B, S, H, dk)
        V = (x @ Wv.T).reshape(B, S, H, dk)
        pos = jnp.arange(S)
        rel_idx = jnp.clip(pos[None, :] - pos[:, None], -MAX_REL, MAX_REL) + MAX_REL
        rel_k = rel_k_emb[rel_idx]
        rel_v = rel_v_emb[rel_idx]
        scores = jnp.einsum('bihd,bjhd->bhij', Q, K) * inv_sqrt_dk
        scores = scores + jnp.einsum('bihd,ijd->bhij', Q, rel_k) * inv_sqrt_dk
        attn = jax.nn.softmax(scores, axis=-1)
        ctx = jnp.einsum('bhij,bjhd->bihd', attn, V)
        ctx = ctx + jnp.einsum('bhij,ijd->bihd', attn, rel_v)
        ctx = ctx.reshape(B, S, D)
        out = ctx @ Wo.T + b_o
        return out

    def _L0_ffn_ref(x, ln1_g, ln1_b, ln2_g, ln2_b, Wq, bq, Wk, bk, Wv, bv, Wp, bp, gate_W, gate_b, exp_W1, exp_b1, exp_W2, exp_b2):
        import jax, jax.numpy as jnp
        import numpy as np
        N_HEAD = 16
        NUM_EXPERTS = 8
        TOP_K = 2
        LN_EPS = 1e-05

        def _layernorm(x, g, b):
            mu = jnp.mean(x, axis=-1, keepdims=True)
            var = jnp.mean(jnp.square(x - mu), axis=-1, keepdims=True)
            return (x - mu) * jax.lax.rsqrt(var + LN_EPS) * g + b

        def _attention(h, Wq, bq, Wk, bk, Wv, bv, Wp, bp):
            B, T, D = h.shape
            hd = D // N_HEAD

            def split(z):
                return z.reshape(B, T, N_HEAD, hd).transpose(0, 2, 1, 3)
            q = split(h @ Wq + bq)
            k = split(h @ Wk + bk)
            v = split(h @ Wv + bv)
            att = jnp.einsum('bhqd,bhkd->bhqk', q, k) / jnp.sqrt(jnp.float32(hd))
            causal = jnp.tril(jnp.ones((T, T), bool))
            att = jnp.where(causal, att, -jnp.inf)
            att = jax.nn.softmax(att, axis=-1)
            y = jnp.einsum('bhqk,bhkd->bhqd', att, v)
            y = y.transpose(0, 2, 1, 3).reshape(B, T, D)
            return y @ Wp + bp

        def _token_moe(h, gate_W, gate_b, exp_W1, exp_b1, exp_W2, exp_b2):
            B, T, D = h.shape
            flat = h.reshape(-1, D)
            N = flat.shape[0]
            logits = flat @ gate_W + gate_b
            top_v, top_i = jax.lax.top_k(logits, TOP_K)
            w = jax.nn.softmax(top_v, axis=-1)
            w_full = jnp.zeros((N, NUM_EXPERTS), flat.dtype)
            w_full = w_full.at[jnp.arange(N)[:, None], top_i].add(w)
            out = jnp.zeros_like(flat)
            for e in range(NUM_EXPERTS):
                mid = jax.nn.gelu(flat @ exp_W1[e] + exp_b1[e], approximate=False)
                y_e = mid @ exp_W2[e] + exp_b2[e]
                out = out + w_full[:, e:e + 1] * y_e
            return out.reshape(B, T, D)
        x = x + _attention(_layernorm(x, ln1_g, ln1_b), Wq, bq, Wk, bk, Wv, bv, Wp, bp)
        x = x + _token_moe(_layernorm(x, ln2_g, ln2_b), gate_W, gate_b, exp_W1, exp_b1, exp_W2, exp_b2)
        return x

    def _L1_attn_ref(x, ln1_g, ln1_b, Wq, Wk, Wv, Wo, ln2_g, ln2_b, Wf1, Wf2):
        import jax, jax.numpy as jnp
        import numpy as np
        B, T, D = (1, 256, 128)
        H, DH, DV, DF = (16, 64, 64, 512)
        EPS_LN = 1e-05
        EPS_DEN = 1e-06

        def _layernorm(x, g, b):
            m = jnp.mean(x, axis=-1, keepdims=True)
            v = jnp.mean((x - m) ** 2, axis=-1, keepdims=True)
            return (x - m) / jnp.sqrt(v + EPS_LN) * g + b

        def _phi(x):
            return jax.nn.elu(x) + 1.0

        def _linear_attention(x, Wq, Wk, Wv, Wo):
            b, t, d = x.shape
            Q = _phi((x @ Wq).reshape(b, t, H, DH)).transpose(0, 2, 1, 3)
            K = _phi((x @ Wk).reshape(b, t, H, DH)).transpose(0, 2, 1, 3)
            V = (x @ Wv).reshape(b, t, H, DV).transpose(0, 2, 1, 3)
            KV = jnp.einsum('bhti,bhtj->bhtij', K, V)
            S = jnp.cumsum(KV, axis=2)
            z = jnp.cumsum(K, axis=2)
            num = jnp.einsum('bhti,bhtij->bhtj', Q, S)
            den = jnp.maximum(jnp.einsum('bhti,bhti->bht', Q, z), EPS_DEN)[..., None]
            out = (num / den).transpose(0, 2, 1, 3).reshape(b, t, H * DV)
            return out @ Wo
        x = x + _linear_attention(_layernorm(x, ln1_g, ln1_b), Wq, Wk, Wv, Wo)
        h = _layernorm(x, ln2_g, ln2_b)
        x = x + jax.nn.gelu(h @ Wf1, approximate=False) @ Wf2
        return x

    def _L1_ffn_ref(x, W, Wp, bp, sim, temp, Wd0, Wu0, Wd1, Wu1, Wd2, Wu2, Wd3, Wu3):
        import jax, jax.numpy as jnp
        import numpy as np
        B, C, D, O = (4, 512, 128, 128)
        PROJ = 32
        RANKS = [1, 2, 4, 8]
        E = len(RANKS)
        CLAMP_MAX = float(np.log(1.0 / 0.01))

        def _l2norm(v, axis):
            return v / jnp.maximum(jnp.linalg.norm(v, axis=axis, keepdims=True), 1e-12)
        base = jnp.einsum('bcd,od->bco', x, W)
        xf = x.reshape(-1, x.shape[-1])
        proj = _l2norm(xf @ Wp.T + bp, axis=1)
        simn = _l2norm(sim, axis=0)
        scale = jnp.exp(jnp.minimum(temp, CLAMP_MAX))
        logits = proj @ simn * scale
        lw = jax.nn.softmax(logits, axis=1)
        top1 = jnp.argmax(lw, axis=1)
        ret = jnp.where(jnp.arange(E)[None, :] == top1[:, None], lw, 0.0)
        ret = ret.reshape(x.shape[0], x.shape[1], E)
        downs = (Wd0, Wd1, Wd2, Wd3)
        ups = (Wu0, Wu1, Wu2, Wu3)
        l = jnp.stack([jnp.einsum('bcr,or->bco', jnp.einsum('bcd,rd->bcr', x, d), u) for d, u in zip(downs, ups)], axis=2)
        res = jnp.sum(ret[..., None] * l, axis=2)
        return base + res
    x = L0_attn_x
    xn = _layernorm(x, axis=-1)
    s = _L0_attn_ref(xn, L0_attn_Wq, L0_attn_Wk, L0_attn_Wv, L0_attn_Wo, L0_attn_b_o, L0_attn_rel_k_emb, L0_attn_rel_v_emb)
    g = _silu(_L0_ffn_ref(xn, L0_ffn_ln1_g, L0_ffn_ln1_b, L0_ffn_ln2_g, L0_ffn_ln2_b, L0_ffn_Wq, L0_ffn_bq, L0_ffn_Wk, L0_ffn_bk, L0_ffn_Wv, L0_ffn_bv, L0_ffn_Wp, L0_ffn_bp, L0_ffn_gate_W, L0_ffn_gate_b, L0_ffn_exp_W1, L0_ffn_exp_b1, L0_ffn_exp_W2, L0_ffn_exp_b2))
    x = x + s * g
    xn = _layernorm(x, axis=-1)
    s = _L1_attn_ref(xn, L1_attn_ln1_g, L1_attn_ln1_b, L1_attn_Wq, L1_attn_Wk, L1_attn_Wv, L1_attn_Wo, L1_attn_ln2_g, L1_attn_ln2_b, L1_attn_Wf1, L1_attn_Wf2)
    g = _silu(_L1_ffn_ref(xn, L1_ffn_W, L1_ffn_Wp, L1_ffn_bp, L1_ffn_sim, L1_ffn_temp, L1_ffn_Wd0, L1_ffn_Wu0, L1_ffn_Wd1, L1_ffn_Wu1, L1_ffn_Wd2, L1_ffn_Wu2, L1_ffn_Wd3, L1_ffn_Wu3))
    x = x + s * g
    return x

_drawn_inputs = setup_inputs


def setup_inputs(seed=0):
    import zlib

    import numpy as np

    out = dict(_drawn_inputs(seed))
    spreads = {'L0_attn_b_o': (0.0, 0.1),
     'L0_ffn_ln1_g': (1.0, 0.6),
     'L0_ffn_ln1_b': (0.0, 0.8),
     'L0_ffn_ln2_g': (1.0, 0.6),
     'L0_ffn_ln2_b': (0.0, 0.8),
     'L0_ffn_bq': (0.0, 0.8),
     'L0_ffn_bk': (0.0, 2.0),
     'L0_ffn_bv': (0.0, 0.8),
     'L0_ffn_bp': (0.0, 0.737),
     'L0_ffn_gate_b': (0.0, 0.8),
     'L0_ffn_exp_b1': (0.0, 0.8),
     'L0_ffn_exp_b2': (0.0, 0.8),
     'L1_attn_ln1_g': (1.0, 0.6),
     'L1_attn_ln1_b': (0.0, 0.8),
     'L1_attn_ln2_g': (1.0, 0.6),
     'L1_attn_ln2_b': (0.0, 2.0),
     'L1_ffn_bp': (0.0, 0.8)}
    factors = {'L0_attn_rel_k_emb': 8.0,
     'L0_attn_rel_v_emb': 4.846,
     'L0_ffn_Wq': 8.0,
     'L0_ffn_Wk': 8.0,
     'L0_ffn_Wv': 8.0,
     'L0_ffn_Wp': 8.0,
     'L0_ffn_gate_W': 7.85,
     'L0_ffn_exp_W1': 8.0,
     'L0_ffn_exp_W2': 8.0,
     'L1_attn_Wq': 8.0,
     'L1_attn_Wk': 8.0,
     'L1_attn_Wv': 5.203,
     'L1_attn_Wo': 5.827,
     'L1_ffn_Wp': 5.1,
     'L1_ffn_sim': 4.652,
     'L1_ffn_Wd0': 6.495,
     'L1_ffn_Wu0': 5.835,
     'L1_ffn_Wd1': 8.0,
     'L1_ffn_Wu1': 8.0,
     'L1_ffn_Wd2': 8.0,
     'L1_ffn_Wu2': 8.0,
     'L1_ffn_Wd3': 8.0,
     'L1_ffn_Wu3': 8.0,
     'L1_attn_Wf1': 3.496,
     'L1_attn_Wf2': 3.578}
    for name, (base, spread) in spreads.items():
        noise = np.random.default_rng([zlib.crc32(name.encode()), seed]).standard_normal(out[name].shape)
        drawn = base * np.exp(spread * noise) if base else spread * noise
        out[name] = jnp.asarray(drawn.astype(out[name].dtype))
    for name, factor in factors.items():
        out[name] = (out[name] * factor).astype(out[name].dtype)
    return out
```

```python
from contextlib import ExitStack

import numpy as np
import concourse.bass as bass
import concourse.mybir as mybir

F32 = mybir.dt.float32
BF16 = mybir.dt.bfloat16
U32 = mybir.dt.uint32
ALU = mybir.AluOpType
ACT = mybir.ActivationFunctionType
AX = mybir.AxisListType

P = 128
B, S, D = 2, 1024, 128
T = B * S
NT = T // P
NS = S // P
H, DK = 16, 8
BH = B * H
REL = 32
NREL = 2 * REL + 1
WIN = P + 2 * REL
E, HID = 8, 512
LH, LD = 16, 64
DF = 512
PROJ, NE1 = 32, 4
RANKS = [1, 2, 4, 8]
RSUM = sum(RANKS)
BANK = 512
QUAD = BANK // P
RING = 4
EPS = 1e-5
MASKED = -1e38
PIECES = 3
QROWS = 6 * DK
SROWS = QROWS + PIECES
RPAD = 2
RHEAD = (S + 2 * RPAD) * NREL

COLS = ["ln1_g", "ln1_b", "ln2_g", "ln2_b", "bq", "bk", "rk_first", "rk_last",
        "l1_ln1_g", "l1_ln1_b", "l1_ln2_g", "l1_ln2_b"]
COL = {name: n for n, name in enumerate(COLS)}
EXP_B1 = len(COLS)
NCOLS = EXP_B1 + E * HID // P
ROWS = {}
_at = 0
for _name, _n in [("b_o", D), ("bv", D), ("bp", D), ("gate_b", E), ("rv_first", D), ("rv_last", D),
                  ("router_b", PROJ), ("temp", 1), ("slots", E)]:
    ROWS[_name] = (_at, _n)
    _at += _n
NROWS = _at
MATS = {}
_at = 0
for _name, _n in [("r_q", D), ("r_k", D), ("r_v", D), ("r_o", D), ("c_q", D), ("c_k", D), ("c_v", D),
                  ("c_p", D), ("gate", E)]:
    MATS[_name] = (_at, _n)
    _at += _n
NMATS = _at
MATS1 = {}
_at = 0
for _name, _n in [("l_q", LH * LD), ("l_k", LH * LD), ("l_v", LH * LD), ("l_o", LH * LD), ("f1", DF),
                  ("f2", DF), ("base", D), ("router", PROJ), ("down", RSUM)]:
    MATS1[_name] = (_at, _n)
    _at += _n
NMATS1 = _at
RCH = (H * NREL + P - 1) // P
RGROUPS = [(0, 6), (6, 11), (11, 16)]


def chained(eng, sem, start=0):
    done = [0]

    def link(ins):
        done[0] += 1
        ins.then_inc(sem, 1)
        eng.wait_ge(sem, start + done[0])

    link.done = done
    return link


class Named(dict):
    __getattr__ = dict.__getitem__
    __setattr__ = dict.__setitem__


def norm_stats_tensors(sb, tag):
    return Named(
        stats=sb(f"{tag}_stats", [P, NT, 6], F32), mean_var=sb(f"{tag}_mean_var", [P, NT, 2], F32),
        var=sb(f"{tag}_var", [P, NT], F32), std=sb(f"{tag}_std", [P, NT], F32),
        rstd=sb(f"{tag}_rstd", [P, NT], F32), tmp=sb(f"{tag}_tmp", [P, NT], F32))


def layer_norm(nc, dve, link, N, src, dst, var_ready, std_ready, turn, tiles=range(NT)):
    a, b = tiles[0], tiles[-1] + 1
    for t in tiles:
        last = nc.vector.bn_stats(N.stats[:, t, :], src[:, t, :])
    link(last)
    for t in tiles:
        last = nc.vector.bn_aggr(N.mean_var[:, t, :], N.stats[:, t, :])
    link(last)
    nc.vector.tensor_scalar(N.var[:, a:b], N.mean_var[:, a:b, 1], EPS, None, ALU.add).then_inc(var_ready, 1)
    dve.wait_ge(std_ready, turn)
    link(nc.vector.reciprocal(N.rstd[:, a:b], N.std[:, a:b]))
    link(nc.vector.tensor_tensor(N.tmp[:, a:b], N.rstd[:, a:b], N.rstd[:, a:b], ALU.mult))
    link(nc.vector.tensor_tensor(N.tmp[:, a:b], N.tmp[:, a:b], N.var[:, a:b], ALU.mult))
    link(nc.vector.tensor_scalar(N.tmp[:, a:b], N.tmp[:, a:b], -0.5, 1.5, ALU.mult, ALU.add))
    link(nc.vector.tensor_tensor(N.rstd[:, a:b], N.rstd[:, a:b], N.tmp[:, a:b], ALU.mult))
    for t in tiles:
        last = nc.vector.tensor_scalar(dst[:, t, :], src[:, t, :], N.mean_var[:, t, 0:1], N.rstd[:, t:t + 1],
                                       ALU.subtract, ALU.mult)
    link(last)


def layer_norm_root(nc, act, N, var_ready, std_ready, turn, tiles=range(NT)):
    a, b = tiles[0], tiles[-1] + 1
    act.wait_ge(var_ready, turn)
    nc.scalar.activation(N.std[:, a:b], N.var[:, a:b], ACT.Sqrt).then_inc(std_ready, 1)


def stage_normalize(nc, G, M, tag, gain, bias, first):
    with ExitStack() as ctx:
        def sb(name, shape, dt=F32):
            return ctx.enter_context(nc.sbuf_tensor(name, shape, dt))

        def sem(name):
            return ctx.enter_context(nc.semaphore(name))

        N = norm_stats_tensors(sb, tag)
        xnn = sb(f"{tag}_xnn", [P, NT, D])
        xn_ps = [ctx.enter_context(nc.psum_tensor(f"{tag}_xn_ps{i}", [P, BANK], F32)) for i in range(2)]
        h1_ps = [ctx.enter_context(nc.psum_tensor(f"{tag}_h1_ps{i}", [P, BANK], F32)) for i in range(2)]
        x_in = sem(f"{tag}_x_in")
        par_in = sem(f"{tag}_par_in")
        chain = sem(f"{tag}_chain")
        var_ready = sem(f"{tag}_var_ready")
        std_ready = sem(f"{tag}_std_ready")
        xn_ready = sem(f"{tag}_xn_ready")
        ident0 = sem(f"{tag}_ident0")
        ident_ready = sem(f"{tag}_ident_ready")
        xn_turned = sem(f"{tag}_xn_turned")
        h1_turned = sem(f"{tag}_h1_turned")
        xn_kept = sem(f"{tag}_xn_kept")
        h1_kept = sem(f"{tag}_h1_kept")
        block = ctx.enter_context(nc.Block())

        @block.sync
        def _(sp):
            if not first:
                return
            sp.dma_start(G.xt[:, :, :], M.x.rearrange("(t p) d -> p t d", p=P)).then_inc(x_in, 16)
            sp.dma_start(G.cols[:, :], M.cols).then_inc(par_in, 16)
            sp.dma_start(G.rows[:, :], M.rows.partition_broadcast(P)).then_inc(par_in, 16)
            sp.dma_start(G.mats[:, :], M.mats).then_inc(par_in, 16)
            sp.wait_ge(par_in, 48)

        @block.gpsimd
        def _(pool):
            if not first:
                return
            nc.gpsimd.memset(G.ident[:, :], 0.0).then_inc(ident0, 1)
            nc.gpsimd.memset(G.identb[:, :], 0.0).then_inc(ident0, 1)
            nc.gpsimd.memset(G.mask_ij[:, :], 0.0).then_inc(ident0, 1)
            nc.gpsimd.memset(G.mask_ji[:, :], 0.0).then_inc(ident0, 1)
            for m in (G.causal01, G.before_last, G.after_first):
                nc.gpsimd.memset(m[:, :], 1.0).then_inc(ident0, 1)
            pool.wait_ge(ident0, 7)
            for m in (G.ident, G.identb):
                nc.gpsimd.affine_select(out=m[:, :], in_=m[:, :], compare_op=ALU.not_equal, fill=1.0, base=0,
                                        pattern=[[-1, P]], channel_multiplier=1).then_inc(ident_ready, 1)
            nc.gpsimd.affine_select(out=G.mask_ij[:, :], in_=G.mask_ij[:, :], compare_op=ALU.is_ge, fill=MASKED,
                                    base=0, pattern=[[-1, P]], channel_multiplier=1).then_inc(ident_ready, 1)
            nc.gpsimd.affine_select(out=G.mask_ji[:, :], in_=G.mask_ji[:, :], compare_op=ALU.is_ge, fill=MASKED,
                                    base=0, pattern=[[1, P]], channel_multiplier=-1).then_inc(ident_ready, 1)
            nc.gpsimd.affine_select(out=G.causal01[:, :], in_=G.causal01[:, :], compare_op=ALU.is_ge, fill=0.0,
                                    base=0, pattern=[[1, P]], channel_multiplier=-1).then_inc(ident_ready, 1)
            nc.gpsimd.affine_select(out=G.before_last[:, :], in_=G.before_last[:, :], compare_op=ALU.is_gt,
                                    fill=0.0, base=2 * REL, pattern=[[-1, WIN]],
                                    channel_multiplier=1).then_inc(ident_ready, 1)
            nc.gpsimd.affine_select(out=G.after_first[:, :], in_=G.after_first[:, :], compare_op=ALU.is_gt,
                                    fill=0.0, base=0, pattern=[[1, P]],
                                    channel_multiplier=-1).then_inc(ident_ready, 1)

        @block.vector
        def _(dve):
            link = chained(dve, chain)
            if first:
                dve.wait_ge(x_in, 16)
            layer_norm(nc, dve, link, N, G.xt, G.xn, var_ready, std_ready, 1)
            nc.vector.memset(G.zeros[:, :], 0.0).then_inc(xn_ready, 1)
            layer_norm(nc, dve, link, N, G.xn, xnn, var_ready, std_ready, 2)
            nc.vector.memset(G.negs[:, :], 0.0).then_inc(xn_ready, 1)
            if first:
                dve.wait_ge(par_in, 48)
            for c in range(QUAD):
                dve.wait_ge(h1_turned, c + 1)
                nc.vector.tensor_scalar(G.h1T[:, c * BANK:(c + 1) * BANK], h1_ps[c % 2][:, :],
                                        G.col(gain), G.col(bias), ALU.mult, ALU.add).then_inc(h1_kept, 1)

        @block.scalar
        def _(act):
            layer_norm_root(nc, act, N, var_ready, std_ready, 1)
            layer_norm_root(nc, act, N, var_ready, std_ready, 2)
            for c in range(QUAD):
                act.wait_ge(xn_turned, c + 1)
                nc.scalar.copy(G.xnT[:, c * BANK:(c + 1) * BANK], xn_ps[c % 2][:, :]).then_inc(xn_kept, 1)

        @block.tensor
        def _(pe):
            if first:
                pe.wait_ge(ident_ready, 2)
            for src, ps, ready, turned, kept in ((G.xn, xn_ps, 1, xn_turned, xn_kept),
                                                 (xnn, h1_ps, 2, h1_turned, h1_kept)):
                pe.wait_ge(xn_ready, ready)
                for c in range(QUAD):
                    if c >= 2:
                        pe.wait_ge(kept, c - 1)
                    for k in range(QUAD):
                        last = nc.tensor.transpose(ps[c % 2][:, k * P:(k + 1) * P], src[:, c * QUAD + k, :],
                                                   G.ident[:, :])
                    last.then_inc(turned, 1)


def stage_project(nc, G, M):
    inv = 1.0 / float(np.sqrt(DK))
    with ExitStack() as ctx:
        def sb(name, shape, dt=F32):
            return ctx.enter_context(nc.sbuf_tensor(name, shape, dt))

        def sem(name):
            return ctx.enter_context(nc.semaphore(name))

        proj = sb("proj", [P, 5, T])
        rest = sb("rest", [P, T])
        pieces = sb("pieces", [P, 2, PIECES, T], BF16)
        bq_scaled = sb("bq_scaled", [P, 1])
        rel_w = sb("rel_w", [P, 2, H * NREL])
        rel_sb = sb("rel_sb", [P, 2, H, NREL])
        rv_mix = sb("rv_mix", [P, D])
        proj_ps = [ctx.enter_context(nc.psum_tensor(f"proj_ps{i}", [P, BANK], F32)) for i in range(2)]
        v_ps = [ctx.enter_context(nc.psum_tensor(f"v_ps{i}", [P, BANK], F32)) for i in range(2)]
        rel_ps = [ctx.enter_context(nc.psum_tensor(f"rel_ps{i}", [P, BANK], F32)) for i in range(3)]
        rel_w_in = sem("p_rel_w_in")
        rel_w_ready = sem("p_rel_w_ready")
        bias_ready = sem("p_bias_ready")
        projected = sem("p_projected")
        proj_kept = sem("p_proj_kept")
        chain = sem("p_chain")
        cut = sem("p_cut")
        pieces_stored = [sem(f"p_pieces_stored{i}") for i in range(2)]
        v_projected = sem("p_v_projected")
        v_kept = sem("p_v_kept")
        v_ones = sem("p_v_ones")
        mix_ready = sem("p_mix_ready")
        scored = sem("p_scored")
        rel_kept = sem("p_rel_kept")
        last_kept = sem("p_last_kept")
        rel_stored = [sem(f"p_rel_stored{i}") for i in range(2)]
        pad_stored = sem("p_pad_stored")
        block = ctx.enter_context(nc.Block())
        plan = [("r_q", G.xnT, 1), ("r_k", G.xnT, 2), ("c_q", G.h1T, 1), ("c_k", G.h1T, 1)]
        kept_after = [4, 12, 12, 16, 20]

        @block.sync
        def _(sp):
            sp.dma_start(rel_w[:, 0, :], M.rk_block).then_inc(rel_w_in, 16)
            sp.dma_start(rel_w[:, 1, :], M.rk_block_first).then_inc(rel_w_in, 16)
            for row in (0, (S + RPAD) * NREL):
                sp.dma_start(bass.AP(M.rel.tensor, row, [[RHEAD, BH], [1, RPAD * NREL]]),
                             G.zeros[0:BH, 0:RPAD * NREL]).then_inc(pad_stored, 16)
            for a in range(5):
                sp.wait_ge(cut, a + 1)
                sp.dma_start(M.split[a].rearrange("c b p s -> p c b s"),
                             pieces[:, a % 2, :, :].rearrange("p c (b s) -> p c b s", b=B)
                             ).then_inc(pieces_stored[a % 2], 16)
            for t in range(NT):
                b, tile = divmod(t, NS)
                sp.wait_ge(rel_kept, t + 1)
                sp.dma_start(bass.AP(M.rel.tensor, b * H * RHEAD + (RPAD + tile * P) * NREL,
                                     [[NREL, P], [RHEAD, H], [1, NREL]]),
                             rel_sb[:, t % 2, :, :]).then_inc(rel_stored[t % 2], 16)
            sp.wait_ge(pad_stored, 32)
            sp.wait_ge(pieces_stored[0], 48)
            sp.wait_ge(pieces_stored[1], 32)
            for i in range(2):
                sp.wait_ge(rel_stored[i], 16 * (NT // 2))

        @block.gpsimd
        def _(pool):
            pool.wait_ge(rel_w_in, 32)
            nc.gpsimd.tensor_tensor(rel_w[:, 0, :], rel_w[:, 0, :], rel_w[:, 1, :],
                                    ALU.subtract).then_inc(rel_w_ready, 1)
            nc.gpsimd.tensor_copy(rv_mix[:, :], G.row("rv_last")).then_inc(mix_ready, 1)
            pool.wait_ge(mix_ready, 1)
            nc.gpsimd.tensor_copy(rv_mix[0:REL, :], G.row("rv_first")[0:REL, :]).then_inc(mix_ready, 1)
            nc.gpsimd.memset(G.v_rel[:, :, DK:DK + 1], 1.0).then_inc(v_ones, 1)
            nc.gpsimd.memset(G.v_causal[:, :, DK:DK + 1], 1.0).then_inc(v_ones, 1)
            for t in range(NT):
                pool.wait_ge(rel_kept, t + 1)
                nc.gpsimd.tensor_copy(G.rel_last[:, t // NS, :, t % NS], rel_sb[:, t % 2, :, NREL - 1]
                                      ).then_inc(last_kept, 1)

        @block.scalar
        def _(act):
            nc.scalar.mul(bq_scaled[:, :], G.col("bq"), inv).then_inc(bias_ready, 1)
            act.wait_ge(bias_ready, 1)
            n = 0
            for i in range(4):
                for c in range(QUAD):
                    act.wait_ge(projected, n + 1)
                    ps, cols = proj_ps[n % 2], slice(c * BANK, (c + 1) * BANK)
                    n += 1
                    if i == 0:
                        nc.scalar.activation(proj[:, 0, cols], ps[:, :], ACT.Identity, scale=inv
                                             ).then_inc(proj_kept, 1)
                    elif i == 1:
                        nc.scalar.activation(proj[:, 1, cols], ps[:, :], ACT.Identity,
                                             bias=G.col("rk_first")).then_inc(proj_kept, 1)
                        nc.scalar.activation(proj[:, 2, cols], ps[:, :], ACT.Identity,
                                             bias=G.col("rk_last")).then_inc(proj_kept, 1)
                    elif i == 2:
                        nc.scalar.activation(proj[:, 3, cols], ps[:, :], ACT.Identity, bias=bq_scaled[:, :],
                                             scale=inv).then_inc(proj_kept, 1)
                    else:
                        nc.scalar.activation(proj[:, 4, cols], ps[:, :], ACT.Identity,
                                             bias=G.col("bk")).then_inc(proj_kept, 1)
            for t in range(NT):
                act.wait_ge(scored, t + 1)
                if t >= 2:
                    act.wait_ge(rel_stored[t % 2], 16 * (t // 2))
                    act.wait_ge(last_kept, t - 1)
                for g, (h0, h1) in enumerate(RGROUPS):
                    last = nc.scalar.copy(rel_sb[:, t % 2, h0:h1, :],
                                          rel_ps[g][:, 0:(h1 - h0) * NREL].rearrange("p (h r) -> p h r", r=NREL))
                last.then_inc(rel_kept, 1)

        @block.vector
        def _(dve):
            link = chained(dve, chain)
            dve.wait_ge(mix_ready, 2)
            dve.wait_ge(v_ones, 2)
            for a in range(5):
                dve.wait_ge(proj_kept, kept_after[a])
                if a >= 2:
                    dve.wait_ge(pieces_stored[a % 2], 16 * (a // 2))
                src, hi, mid, lo = proj[:, a, :], *(pieces[:, a % 2, i, :] for i in range(PIECES))
                link(nc.vector.tensor_copy(hi, src))
                link(nc.vector.tensor_tensor(rest[:, :], src, hi, ALU.subtract))
                link(nc.vector.tensor_copy(mid, rest[:, :]))
                nc.vector.tensor_tensor(lo, rest[:, :], mid, ALU.subtract).then_inc(cut, 1)
                dve.wait_ge(cut, a + 1)
            for t in range(NT):
                b, tile = divmod(t, NS)
                heads = slice(b * H, (b + 1) * H)
                dve.wait_ge(v_projected, t + 1)
                v_rel = v_ps[t % 2][:, 0:D].rearrange("p (h d) -> p h d", d=DK)
                v_causal = v_ps[t % 2][:, D:2 * D].rearrange("p (h d) -> p h d", d=DK)
                for kind, bias in enumerate((G.row("rv_first"), G.row("rv_last"), rv_mix[:, :])):
                    nc.vector.tensor_tensor(G.v_rel_at(heads, kind, tile), v_rel,
                                            bias.rearrange("p (h d) -> p h d", d=DK), ALU.add)
                nc.vector.tensor_tensor(G.v_causal_at(heads, tile), v_causal,
                                        G.row("bv").rearrange("p (h d) -> p h d", d=DK), ALU.add).then_inc(v_kept, 1)

        @block.tensor
        def _(pe):
            n = 0
            for name, src, _copies in plan:
                for c in range(QUAD):
                    if n >= 2:
                        pe.wait_ge(proj_kept, [1, 2, 3, 4, 6, 8, 10, 12, 13, 14, 15, 16, 17, 18, 19, 20][n - 2])
                    nc.tensor.matmul(proj_ps[n % 2][:, :], G.mat(name), src[:, c * BANK:(c + 1) * BANK],
                                     start=True, stop=True).then_inc(projected, 1)
                    n += 1
            for t in range(NT):
                if t >= 2:
                    pe.wait_ge(v_kept, t - 1)
                nc.tensor.matmul(v_ps[t % 2][:, 0:D], G.xnT[:, t * P:(t + 1) * P], G.mat("r_v"),
                                 start=True, stop=True)
                nc.tensor.matmul(v_ps[t % 2][:, D:2 * D], G.h1T[:, t * P:(t + 1) * P], G.mat("c_v"),
                                 start=True, stop=True).then_inc(v_projected, 1)
            pe.wait_ge(rel_w_ready, 1)
            for t in range(NT):
                if t >= 1:
                    pe.wait_ge(rel_kept, t)
                for g, (h0, h1) in enumerate(RGROUPS):
                    last = nc.tensor.matmul(rel_ps[g][:, 0:(h1 - h0) * NREL], proj[:, 0, t * P:(t + 1) * P],
                                            rel_w[:, 0, h0 * NREL:h1 * NREL], start=True, stop=True)
                last.then_inc(scored, 1)


def await_count(eng, sem, value):
    if not isinstance(value, int) or value > 0:
        eng.wait_ge(sem, value)


def clear_semaphores(nc, numbers):
    with nc.Block() as block:
        @block.sync
        def _(sp):
            sp.sem_clear(numbers)


def over_heads(eng, head):
    for u in range(RING):
        head(u, 0, u, u)
    with eng.Fori(1, BH // RING - 1) as k:
        for u in range(RING):
            head(k * RING + u, k, u, RING + u)
    last = BH // RING - 1
    for u in range(RING):
        head(last * RING + u, last, u, last * RING + u)


def stage_attention(nc, G, M, relative):
    tag = "r" if relative else "c"
    q_array, k_arrays = (0, (1, 2)) if relative else (3, (4,))
    NK = len(k_arrays)
    KINDS = 3 if relative else 1
    LOADS = 3 * (1 + NK) + (1 if relative else 0)
    VW = KINDS * NS * (DK + 1)
    halves = [(i, hf, hf * BANK, min((hf + 1) * BANK, S if relative else (i + 1) * P))
              for i in range(NS) for hf in range(2) if relative or hf * BANK < (i + 1) * P]
    NA = len(halves) + 1
    assert NA % 2 == 1
    share = [3, 3, 3, 3, 2, 2, 0, 0] if relative else [2, 2, 2, 2, 2, 2, 0, 0]
    beside = [list(range(sum(share[:j]), sum(share[:j + 1]))) for j in range(NS)]
    assert sum(share) == len(halves)

    with ExitStack() as ctx:
        def sb(name, shape, dt=F32):
            return ctx.enter_context(nc.sbuf_tensor(f"{tag}_{name}", shape, dt))

        def sem(name):
            return ctx.enter_context(nc.semaphore(f"{tag}_{name}"))

        q = sb("q", [64, RING, S], BF16)
        ks = sb("ks", [64, RING, NK, S], BF16)
        vs = sb("vs", [P, RING, VW])
        probs = sb("probs", [P, NS, S])
        half_max = sb("half_max", [P, NS, 2])
        row_max = sb("row_max", [P, NS])
        neg_rest = sb("neg_rest", [P, NS])
        neg_max = sb("neg_max", [P, PIECES, NS], BF16)
        neg_maxT = sb("neg_maxT", [PIECES * NS, 2, P], BF16)
        a_ps = [ctx.enter_context(nc.psum_tensor(f"{tag}_a_ps{i}", [P, BANK], F32)) for i in range(2)]
        b_ps = [ctx.enter_context(nc.psum_tensor(f"{tag}_b_ps{i}", [P, S], F32)) for i in range(2)]
        o_ps = ctx.enter_context(nc.psum_tensor(f"{tag}_o_ps", [P, NS, DK + 1], F32))
        if relative:
            rel = sb("rel", [P, RING, NS, WIN])
            rel_edge = sb("rel_edge", [P, RING, NS])
            win_sb = sb("win_sb", [P, 2, NS, WIN])
            far_sb = sb("far_sb", [P, NS, P])
            win_ps = ctx.enter_context(nc.psum_tensor(f"{tag}_win_ps", [P, 2, WIN], F32))
        loaded = [sem(f"loaded{i}") for i in range(RING)]
        max_in = [sem(f"max_in{i}") for i in range(RING)]
        ones_ready = sem("ones_ready")
        values_ready = sem("values_ready")
        rel_ready = sem("rel_ready")
        pool_chain = sem("pool_chain")
        chain = sem("chain")
        a_scored = sem("a_scored")
        a_used = sem("a_used")
        b_scored = sem("b_scored")
        exp_done = sem("exp_done")
        pv_done = sem("pv_done")
        o_kept = sem("o_kept")
        floor_ready = sem("floor_ready")
        win_kept = sem("win_kept")
        win_stored = [sem(f"win_stored{i}") for i in range(2)]
        far_masked = sem("far_masked")
        far_summed = sem("far_summed")
        block = ctx.enter_context(nc.Block())
        SRCROW, SRCPIECE = S, B * P * S

        def bank_of_a(u, x):
            return a_ps[(NA * u + x) % 2]

        @block.sync
        def _(sp):
            def load(n, u):
                def rows(array, piece, step, count):
                    return bass.AP(M.split.tensor, array * PIECES * SRCPIECE + piece * SRCPIECE + n * (DK * S),
                                   [[step, count], [SRCROW, DK], [1, S]])
                r1, r2 = 3 * DK, 5 * DK
                sp.dma_start(q[0:r1, u, :], rows(q_array, 0, SRCPIECE, 3)).then_inc(loaded[u], 16)
                sp.dma_start(q[r1:r2, u, :], rows(q_array, 0, SRCPIECE, 2)).then_inc(loaded[u], 16)
                sp.dma_start(q[r2:QROWS, u, :], rows(q_array, 0, 0, 1)).then_inc(loaded[u], 16)
                for i, array in enumerate(k_arrays):
                    sp.dma_start(ks[0:r1, u, i, :], rows(array, 0, 0, 3)).then_inc(loaded[u], 16)
                    sp.dma_start(ks[r1:r2, u, i, :], rows(array, 1, 0, 2)).then_inc(loaded[u], 16)
                    sp.dma_start(ks[r2:QROWS, u, i, :], rows(array, 2, 0, 1)).then_inc(loaded[u], 16)
                if relative:
                    sp.dma_start(rel[:, u, :, :],
                                 bass.AP(M.rel.tensor, n * RHEAD + RPAD * NREL,
                                         [[NREL - 1, P], [P * NREL, NS], [1, WIN]])).then_inc(loaded[u], 16)

            def maxima(n, u):
                sp.wait_ge(a_used, n * NA + NA)
                sp.dma_start(q[QROWS:SROWS, u, :], neg_maxT[:, u % 2, :]).then_inc(max_in[u], 16)

            def store_window(n, u):
                sp.wait_ge(win_kept, n * 4 + 4)
                sp.dma_start(bass.AP(M.window.tensor, n * (S * WIN), [[WIN, P], [P * WIN, NS], [1, WIN]]),
                             win_sb[:, u % 2, :, :]).then_inc(win_stored[u % 2], 16)

            def head(n, k, u, at):
                if at + 3 < BH:
                    if at >= 1:
                        sp.wait_ge(pv_done, n * NS)
                    load(n + 3, (u + 3) % RING)
                if relative and at >= 1:
                    store_window(n - 1, (u - 1) % RING)
                if at + 1 < BH:
                    maxima(n + 1, (u + 1) % RING)

            sp.wait_ge(ones_ready, 2)
            for n in range(3):
                load(n, n)
            maxima(0, 0)
            over_heads(sp, head)
            if relative:
                store_window(BH - 1, RING - 1)
                for i in range(2):
                    sp.wait_ge(win_stored[i], 16 * (BH // 2))

        @block.gpsimd
        def _(pool):
            nc.gpsimd.memset(q[32:64, :, :], 1.0).then_inc(ones_ready, 1)
            nc.gpsimd.memset(ks[32:64, :, :, :], 1.0).then_inc(ones_ready, 1)
            pool.wait_ge(ones_ready, 2)

            def prepare(n, k, u, at):
                link = chained(pool, pool_chain, n * 4)
                if at >= RING:
                    pool.wait_ge(pv_done, (n - RING + 1) * NS)
                values, width = (G.v_rel, VW) if relative else (G.v_causal, VW)
                nc.gpsimd.tensor_copy(vs[:, u, :], values[:, :, :].rearrange("p a b -> p (a b)")[
                    :, bass.ds(n * width, width)]).then_inc(values_ready, 1)
                if not relative:
                    return
                link(nc.gpsimd.tensor_copy(rel_edge[:, u, :], G.rel_last[:, :, :, :].rearrange(
                    "p b h t -> p (b h t)")[:, bass.ds(n * NS, NS)]))
                pool.wait_ge(loaded[u], 16 * LOADS * (k + 1))
                edge = rel_edge[:, u, :].unsqueeze(2)
                link(nc.gpsimd.tensor_tensor(rel[:, u, :, :], rel[:, u, :, :], edge.to_broadcast([P, NS, WIN]),
                                             ALU.subtract))
                link(nc.gpsimd.tensor_tensor(rel[:, u, :, :], rel[:, u, :, :],
                                             G.before_last[:, :].unsqueeze(1).to_broadcast([P, NS, WIN]),
                                             ALU.mult))
                link(nc.gpsimd.tensor_tensor(rel[:, u, :, 0:REL + P], rel[:, u, :, 0:REL + P],
                                             edge.to_broadcast([P, NS, REL + P]), ALU.add))
                nc.gpsimd.tensor_tensor(rel[:, u, :, 0:P], rel[:, u, :, 0:P],
                                        G.after_first[:, :].unsqueeze(1).to_broadcast([P, NS, P]),
                                        ALU.mult).then_inc(rel_ready, 1)
                assert link.done[0] == 4

            def mask_far(n, u, at):
                pool.wait_ge(win_kept, n * 4 + 4)
                if at >= 1:
                    pool.wait_ge(far_summed, n)
                nc.gpsimd.tensor_tensor(far_sb[:, :, :], win_sb[:, u % 2, :, 2 * REL:WIN],
                                        G.causal01[:, :].unsqueeze(1).to_broadcast([P, NS, P]), ALU.mult
                                        ).then_inc(far_masked, 1)

            def head(n, k, u, at):
                if at + 2 < BH:
                    prepare(n + 2, k + (u + 2) // RING, (u + 2) % RING, at + 2)
                if relative and at >= 1:
                    mask_far(n - 1, (u - 1) % RING, at - 1)

            for n in range(2):
                prepare(n, 0, n, n)
            over_heads(pool, head)
            if relative:
                mask_far(BH - 1, RING - 1, BH - 1)

        @block.scalar
        def _(act):
            def head(n, k, u, at):
                for j in range(NS):
                    act.wait_ge(b_scored, n * NS + j + 1)
                    if at >= 1:
                        act.wait_ge(pv_done, (n - 1) * NS + (min(j + 3, NS) if relative else j + 1))
                    lo = 0 if relative else j * P
                    nc.scalar.activation(probs[:, j, lo:S], b_ps[j % 2][:, lo:S], ACT.Exp).then_inc(exp_done, 1)

            over_heads(act, head)

        @block.vector
        def _(dve):
            def max_piece(n, u, x):
                i, hf, lo, hi = halves[x]
                dve.wait_ge(a_scored, n * NA + x + 1)
                nc.vector.tensor_reduce(half_max[:, i, hf:hf + 1], bank_of_a(u, x)[:, 0:hi - lo], AX.X,
                                        ALU.max).then_inc(a_used, 1)

            def negate_max(n, k, u, at):
                link = chained(dve, chain, n * 5)
                dve.wait_ge(a_used, n * NA + NA - 1)
                link(nc.vector.tensor_tensor(row_max[:, :], half_max[:, :, 0], half_max[:, :, 1], ALU.max))
                link(nc.vector.tensor_scalar(neg_max[:, 0, :], row_max[:, :], -1.0, None, ALU.mult))
                link(nc.vector.scalar_tensor_tensor(neg_rest[:, :], row_max[:, :], -1.0, neg_max[:, 0, :],
                                                    ALU.mult, ALU.subtract))
                link(nc.vector.tensor_copy(neg_max[:, 1, :], neg_rest[:, :]))
                link(nc.vector.tensor_tensor(neg_max[:, 2, :], neg_rest[:, :], neg_max[:, 1, :], ALU.subtract))
                assert link.done[0] == 5

            def keep_turned(n, k, u, at):
                dve.wait_ge(a_scored, n * NA + NA)
                if at >= 2:
                    dve.wait_ge(max_in[(u + 2) % RING], 16 * k + (16 if u >= 2 else 0))
                nc.vector.tensor_copy(neg_maxT[:, u % 2, :], bank_of_a(u, NA - 1)[0:PIECES * NS, 0:P // 2].bitcast(
                    BF16)).then_inc(a_used, 1)

            def keep_window(n, k, u, at, pair):
                dve.wait_ge(pv_done, n * NS + min(2 * pair + 3, NS))
                if pair == 0 and at >= 2:
                    dve.wait_ge(win_stored[u % 2], k * 32 + 16 * (u // 2))
                    dve.wait_ge(far_masked, n - 1)
                nc.vector.tensor_copy(win_sb[:, u % 2, 2 * pair:2 * pair + 2, :], win_ps[:, :, :]
                                      ).then_inc(win_kept, 1)

            def sum_far(n):
                dve.wait_ge(far_masked, n + 1)
                nc.vector.tensor_reduce(G.far[:, :, :].rearrange("p n t -> p (n t)")[:, bass.ds(n * NS, NS)],
                                        far_sb[:, :, :], AX.X, ALU.add).then_inc(far_summed, 1)

            def head(n, k, u, at):
                with_a = at + 1 < BH
                a = (n + 1, k + (u + 1) // RING, (u + 1) % RING, at + 1)
                for j in range(NS):
                    if with_a:
                        for x in beside[j]:
                            max_piece(a[0], a[2], x)
                        if j == 5:
                            negate_max(*a)
                        if j == 7:
                            keep_turned(*a)
                    if relative and j in (3, 5, 7):
                        keep_window(n, k, u, at, (j - 3) // 2)
                    if relative and j == 4 and at >= 1:
                        sum_far(n - 1)
                if relative:
                    keep_window(n, k, u, at, 3)
                dve.wait_ge(pv_done, (n + 1) * NS)
                att = G.att if relative else G.catt
                nc.vector.tensor_copy(att[:, :, :, :].rearrange("p n t d -> p (n t d)")[
                    :, bass.ds(n * (NS * (DK + 1)), NS * (DK + 1))],
                    o_ps[:, :, :].rearrange("p t d -> p (t d)")).then_inc(o_kept, 1)

            if not relative:
                nc.vector.memset(half_max[:, :, 1], -3e38).then_inc(floor_ready, 1)
                dve.wait_ge(floor_ready, 1)
            for x in range(len(halves)):
                max_piece(0, 0, x)
            negate_max(0, 0, 0, 0)
            keep_turned(0, 0, 0, 0)
            over_heads(dve, head)
            if relative:
                sum_far(BH - 1)

        @block.tensor
        def _(pe):
            def score_piece(n, u, x):
                i, hf, lo, hi = halves[x]
                ps = bank_of_a(u, x)
                await_count(pe, a_used, n * NA + x - 1)
                lhs = q[0:QROWS, u, i * P:(i + 1) * P]
                if relative:
                    mid = (i + 1) * P
                    parts = [(0, lo, min(hi, mid)), (1, max(lo, mid), hi)]
                else:
                    parts = [(0, lo, hi)]
                parts = [p for p in parts if p[1] < p[2]]
                for m, (kind, a, b) in enumerate(parts):
                    last = nc.tensor.matmul(ps[:, a - lo:b - lo], lhs, ks[0:QROWS, u, kind, a:b], start=(m == 0),
                                            stop=False, skip_group_check=True)
                if relative:
                    a, b = max(lo, i * P - REL), min(hi, i * P + P + REL)
                    if a < b:
                        w = a - (i * P - REL)
                        last = nc.tensor.matmul(ps[:, a - lo:b - lo], G.ident[:, :], rel[:, u, i, w:w + b - a],
                                                start=False, stop=True, skip_group_check=True)
                elif lo <= i * P < hi:
                    last = nc.tensor.matmul(ps[:, i * P - lo:(i + 1) * P - lo], G.identb[:, :], G.mask_ij[:, :],
                                            start=False, stop=True, skip_group_check=True)
                last.then_inc(a_scored, 1)

            def begin_a(n, k, u):
                pe.wait_ge(loaded[u], 16 * LOADS * (k + 1))
                if relative:
                    pe.wait_ge(rel_ready, n + 1)

            def turn_max(n, u):
                pe.wait_ge(chain, n * 5 + 5)
                await_count(pe, a_used, n * NA + NA - 2)
                nc.tensor.transpose(bank_of_a(u, NA - 1)[0:PIECES * NS, 0:P // 2].bitcast(BF16),
                                    neg_max[:, :, :].rearrange("p c t -> p (c t)"), G.identb[:, :]
                                    ).then_inc(a_scored, 1)

            def score_keys(n, k, u, at, j):
                ps = b_ps[j % 2]
                await_count(pe, exp_done, n * NS + j - 1)
                if relative:
                    parts = [(1, 0, j * P), (0, j * P, S)]
                else:
                    parts = [(0, j * P, S)]
                cuts = [(kind, max(a, c), min(b, c + BANK), c) for c in (0, BANK) for kind, a, b in parts
                        if max(a, c) < min(b, c + BANK)]
                seen = set()
                for kind, a, b, c in cuts:
                    last = nc.tensor.matmul(ps[:, a:b], ks[0:SROWS, u, kind, j * P:(j + 1) * P],
                                            q[0:SROWS, u, a:b], start=(c not in seen), stop=False,
                                            skip_group_check=True)
                    seen.add(c)
                if relative:
                    for i, w, rows in ((j, REL, slice(0, P)), (j + 1, 0, slice(P - REL, P)),
                                       (j - 1, REL + P, slice(0, REL))):
                        if 0 <= i < NS:
                            last = nc.tensor.matmul(ps[rows, i * P:(i + 1) * P],
                                                    rel[:, u, i, w:w + rows.stop - rows.start], G.ident[:, :],
                                                    start=False, stop=True, skip_group_check=True)
                else:
                    last = nc.tensor.matmul(ps[:, j * P:(j + 1) * P], G.identb[:, :], G.mask_ji[:, :],
                                            start=False, stop=True, skip_group_check=True)
                last.then_inc(b_scored, 1)

            def weigh_values(n, k, u, at, j):
                pe.wait_ge(exp_done, n * NS + j + 1)
                if j == 0:
                    pe.wait_ge(values_ready, n + 1)
                    await_count(pe, o_kept, n)
                for i in range(0 if relative else j, NS):
                    kind = 0 if not relative or j <= i else (2 if j == i + 1 else 1)
                    at_v = (kind * NS + j) * (DK + 1)
                    last = nc.tensor.matmul(o_ps[:, i, :], probs[:, j, i * P:(i + 1) * P],
                                            vs[:, u, at_v:at_v + DK + 1], start=(j == 0 and i == 0),
                                            stop=(j == NS - 1), skip_group_check=True)
                return last

            def turn_window(n, i):
                if i % 2 == 0:
                    await_count(pe, win_kept, n * 4 + i // 2)
                cols = slice(i * P, (i + 1) * P)
                left = (probs[:, i - 1, cols], G.ident[:, P - REL:P]) if i else (G.ident[:, :], G.zeros[:, 0:REL])
                right = (probs[:, i + 1, cols], G.ident[:, 0:REL]) if i + 1 < NS else (
                    G.ident[:, :], G.zeros[:, 0:REL])
                nc.tensor.matmul(win_ps[:, i % 2, 0:REL], *left, start=True, stop=True, skip_group_check=True)
                nc.tensor.transpose(win_ps[:, i % 2, REL:REL + P], probs[:, i, cols], G.ident[:, :])
                return nc.tensor.matmul(win_ps[:, i % 2, REL + P:WIN], *right, start=True, stop=True,
                                        skip_group_check=True)

            def use_keys(n, k, u, at, j):
                last = weigh_values(n, k, u, at, j)
                if relative:
                    for i in ([j - 1] if j else []) + ([j] if j == NS - 1 else []):
                        last = turn_window(n, i)
                last.then_inc(pv_done, 1)

            def head(n, k, u, at):
                with_a = at + 1 < BH
                a = (n + 1, k + (u + 1) // RING, (u + 1) % RING, at + 1)
                pe.wait_ge(max_in[u], 16 * (k + 1))
                if with_a:
                    begin_a(a[0], a[1], a[2])
                for j in range(NS):
                    score_keys(n, k, u, at, j)
                    if with_a:
                        for x in beside[j]:
                            score_piece(a[0], a[2], x)
                        if j == 7:
                            turn_max(a[0], a[2])
                    if j >= 1:
                        use_keys(n, k, u, at, j - 1)
                use_keys(n, k, u, at, NS - 1)

            pe.wait_ge(ones_ready, 2)
            begin_a(0, 0, 0)
            for x in range(len(halves)):
                score_piece(0, 0, x)
            turn_max(0, 0)
            over_heads(pe, head)


def stage_combine(nc, G, M):
    with ExitStack() as ctx:
        def sb(name, shape, dt=F32):
            return ctx.enter_context(nc.sbuf_tensor(f"o_{name}", shape, dt))

        def sem(name):
            return ctx.enter_context(nc.semaphore(f"o_{name}"))

        def ps(name, shape):
            return ctx.enter_context(nc.psum_tensor(f"o_{name}", shape, F32))

        rv_w = sb("rv_w", [P, 2, RCH, D])
        by_rel = sb("by_rel", [P, 2, H, NREL])
        by_relT = sb("by_relT", [P, 2, RCH, P])
        inv_r = sb("inv_r", [P, BH, NS])
        inv_c = sb("inv_c", [P, BH, NS])
        yc = sb("yc", [P, NT, D])
        yr = sb("yr", [P, 2, D])
        yT = sb("yT", [P, 2, 2, P])
        plus = sb("plus", [P, 2, D])
        turn_ps = [ps(f"turn_ps{i}", [P, 3, P]) for i in range(3)]
        mix_ps = ps("mix_ps", [P, D])
        yT_ps = [ps(f"yT_ps{i}", [P, 2, P]) for i in range(2)]
        out_ps = [ps(f"out_ps{i}", [P, 2, D]) for i in range(2)]
        rv_in = sem("rv_in")
        rv_ready = sem("rv_ready")
        by_rel_in = [sem(f"by_rel_in{i}") for i in range(2)]
        far_placed = sem("far_placed")
        turned = sem("turned")
        turn_kept = sem("turn_kept")
        mixed = sem("mixed")
        chain = sem("chain")
        inverted = sem("inverted")
        y_ready = sem("y_ready")
        y_turned = sem("y_turned")
        yT_kept = sem("yT_kept")
        out_done = sem("out_done")
        out_kept = sem("out_kept")
        block = ctx.enter_context(nc.Block())

        @block.sync
        def _(sp):
            sp.dma_start(rv_w[:, 0, :, :], M.rv_block.rearrange("p (c d) -> p c d", d=D)).then_inc(rv_in, 16)
            sp.dma_start(rv_w[:, 1, :, :], M.rv_block_first.rearrange("p (c d) -> p c d", d=D)).then_inc(rv_in, 16)
            for t in range(NT):
                b, tile = divmod(t, NS)
                if t >= 2:
                    sp.wait_ge(turned, t - 1)
                sp.dma_start(by_rel[:, t % 2, :, 0:NREL - 1],
                             bass.AP(M.window.tensor, b * H * S * WIN + tile * P * WIN,
                                     [[WIN + 1, P], [S * WIN, H], [1, NREL - 1]])).then_inc(by_rel_in[t % 2], 16)

        @block.gpsimd
        def _(pool):
            pool.wait_ge(rv_in, 32)
            nc.gpsimd.tensor_tensor(rv_w[:, 0, :, :], rv_w[:, 0, :, :], rv_w[:, 1, :, :],
                                    ALU.subtract).then_inc(rv_ready, 1)
            for t in range(NT):
                b, tile = divmod(t, NS)
                if t >= 2:
                    pool.wait_ge(turned, t - 1)
                nc.gpsimd.tensor_copy(by_rel[:, t % 2, :, NREL - 1], G.far[:, b * H:(b + 1) * H, tile]
                                      ).then_inc(far_placed, 1)

        @block.scalar
        def _(act):
            for t in range(NT + 2):
                if t < NT:
                    act.wait_ge(turned, t + 1)
                    if t >= 2:
                        act.wait_ge(mixed, t - 1)
                    for g in range(3):
                        rows = P if g < 2 else P
                        last = nc.scalar.copy(by_relT[0:rows, t % 2, 3 * g:3 * g + 3, :], turn_ps[g][0:rows, :, :])
                    last.then_inc(turn_kept, 1)
                if t >= 2:
                    act.wait_ge(y_turned, t - 1)
                    if t >= 4:
                        act.wait_ge(out_done, t - 3)
                    nc.scalar.copy(yT[:, t % 2, :, :], yT_ps[t % 2][:, :, :]).then_inc(yT_kept, 1)

        @block.vector
        def _(dve):
            link = chained(dve, chain)
            nc.vector.reciprocal(inv_r[:, :, :], G.att[:, :, :, DK])
            link(nc.vector.reciprocal(inv_c[:, :, :], G.catt[:, :, :, DK]))
            for b in range(B):
                heads = slice(b * H, (b + 1) * H)
                last = nc.vector.tensor_tensor(
                    yc[:, b * NS:(b + 1) * NS, :].rearrange("p t (h d) -> p h t d", d=DK), G.catt[:, heads, :, 0:DK],
                    inv_c[:, heads, :].unsqueeze(3).to_broadcast([P, H, NS, DK]), ALU.mult)
            link(last)
            for t in range(NT + 3):
                if t < NT:
                    b, tile = divmod(t, NS)
                    heads = slice(b * H, (b + 1) * H)
                    dve.wait_ge(mixed, t + 1)
                    if t >= 2:
                        dve.wait_ge(y_turned, t - 1)
                    y = yr[:, t % 2, :].rearrange("p (h d) -> p h d", d=DK)
                    link(nc.vector.tensor_tensor(y, mix_ps[:, :].rearrange("p (h d) -> p h d", d=DK),
                                                 G.att[:, heads, tile, 0:DK], ALU.add))
                    nc.vector.tensor_tensor(y, y, inv_r[:, heads, tile].unsqueeze(2).to_broadcast([P, H, DK]),
                                            ALU.mult).then_inc(y_ready, 1)
                if t >= 3:
                    s = t - 3
                    dve.wait_ge(out_done, s + 1)
                    nc.vector.tensor_tensor(G.mixer[:, s, :], out_ps[s % 2][:, 0, :], G.row("b_o"), ALU.add)
                    link(nc.vector.tensor_tensor(plus[:, s % 2, :], out_ps[s % 2][:, 1, :], G.row("bp"), ALU.add))
                    nc.vector.tensor_tensor(G.x2[:, s, :], plus[:, s % 2, :], G.xn[:, s, :], ALU.add
                                            ).then_inc(out_kept, 1)

        @block.tensor
        def _(pe):
            def turn(t):
                pe.wait_ge(by_rel_in[t % 2], 16 * (t // 2 + 1))
                pe.wait_ge(far_placed, t + 1)
                if t:
                    pe.wait_ge(turn_kept, t)
                flat = by_rel[:, t % 2, :, :].rearrange("p h r -> p (h r)")
                for c in range(RCH):
                    rows = min(P, H * NREL - c * P)
                    if rows < P:
                        nc.tensor.transpose(turn_ps[c // 3][:, c % 3, :], G.zeros[:, 0:P], G.ident[:, :])
                    last = nc.tensor.transpose(turn_ps[c // 3][0:rows, c % 3, :], flat[:, c * P:c * P + rows],
                                               G.ident[:, :])
                last.then_inc(turned, 1)

            def mix(t):
                pe.wait_ge(turn_kept, t + 1)
                if t == 0:
                    pe.wait_ge(rv_ready, 1)
                else:
                    pe.wait_ge(y_ready, t)
                for c in range(RCH):
                    last = nc.tensor.matmul(mix_ps[:, :], by_relT[:, t % 2, c, :], rv_w[:, 0, c, :],
                                            start=(c == 0), stop=(c == RCH - 1))
                last.then_inc(mixed, 1)

            def turn_y(t):
                pe.wait_ge(y_ready, t + 1)
                if t >= 2:
                    pe.wait_ge(yT_kept, t - 1)
                nc.tensor.transpose(yT_ps[t % 2][:, 0, :], yr[:, t % 2, :], G.ident[:, :])
                nc.tensor.transpose(yT_ps[t % 2][:, 1, :], yc[:, t, :], G.ident[:, :]).then_inc(y_turned, 1)

            def project(t):
                pe.wait_ge(yT_kept, t + 1)
                if t >= 2:
                    pe.wait_ge(out_kept, t - 1)
                nc.tensor.matmul(out_ps[t % 2][:, 0, :], yT[:, t % 2, 0, :], G.mat("r_o"), start=True, stop=True)
                nc.tensor.matmul(out_ps[t % 2][:, 1, :], yT[:, t % 2, 1, :], G.mat("c_p"), start=True,
                                 stop=True).then_inc(out_done, 1)

            for t in range(NT + 3):
                if t < NT:
                    turn(t)
                if 1 <= t <= NT:
                    mix(t - 1)
                if 2 <= t <= NT + 1:
                    turn_y(t - 2)
                if t >= 3:
                    project(t - 3)


def stage_experts(nc, G, M):
    UNITS = E * QUAD
    HC = HID // P
    with ExitStack() as ctx:
        def sb(name, shape, dt=F32):
            return ctx.enter_context(nc.sbuf_tensor(f"e_{name}", shape, dt))

        def sem(name):
            return ctx.enter_context(nc.semaphore(f"e_{name}"))

        def ps(name, shape):
            return ctx.enter_context(nc.psum_tensor(f"e_{name}", shape, F32))

        N = norm_stats_tensors(sb, "n")
        h2 = sb("h2", [P, NT, D])
        h2T = sb("h2T", [P, T])
        w1 = sb("w1", [P, 2, HID])
        w2 = sb("w2", [P, 2, HC, D])
        b1 = sb("b1", [P, 2, HC])
        b2 = sb("b2", [E, D])
        mid = sb("mid", [P, 2, HC, BANK])
        logits = sb("logits", [P, NT, E])
        top = sb("top", [P, NT, E])
        top_at = sb("top_at", [P, NT, E], U32)
        top_slot = sb("top_slot", [P, NT, 2])
        gap = sb("gap", [P, NT])
        ratio = sb("ratio", [P, NT])
        share = sb("share", [P, 2, NT])
        pick = sb("pick", [P, 2, NT, E])
        gates = sb("gates", [P, NT, E])
        gatesT = sb("gatesT", [E, T])
        bank = [ps(f"bank{i}", [P, BANK]) for i in range(6)]
        weights_in = [sem(f"weights_in{i}") for i in range(2)]
        b2_in = sem("b2_in")
        layer1_in = sem("layer1_in")
        chain = sem("chain")
        var_ready = sem("var_ready")
        std_ready = sem("std_ready")
        h2_ready = sem("h2_ready")
        h2_turned = sem("h2_turned")
        h2T_kept = sem("h2T_kept")
        gated = sem("gated")
        gap_ready = sem("gap_ready")
        ratio_ready = sem("ratio_ready")
        gates_ready = sem("gates_ready")
        gates_turned = sem("gates_turned")
        gatesT_kept = sem("gatesT_kept")
        biased = sem("biased")
        bias_kept = sem("bias_kept")
        hidden = sem("hidden")
        hidden_kept = sem("hidden_kept")
        expert_done = sem("expert_done")
        expert_kept = sem("expert_kept")
        silu_ready = sem("silu_ready")
        block = ctx.enter_context(nc.Block())

        def over_experts(eng, expert):
            for slot in range(2):
                expert(slot, 0, slot, slot)
            with eng.Fori(1, E // 2 - 1) as pair:
                for slot in range(2):
                    expert(pair * 2 + slot, pair, slot, 2 + slot)
            for slot in range(2):
                expert(E - 2 + slot, E // 2 - 1, slot, E - 2 + slot)

        @block.sync
        def _(sp):
            sp.dma_start(b2[:, :], M.exp_b2).then_inc(b2_in, 16)
            sp.dma_start(G.mats1[:, :], M.mats1).then_inc(layer1_in, 16)

            def expert(e, pair, slot, at):
                if at >= 2:
                    sp.wait_ge(expert_done, e * QUAD - QUAD)
                sp.dma_start(w1[:, slot, :], bass.AP(M.exp_w1.tensor, e * (P * HID), [[HID, P], [1, HID]])
                             ).then_inc(weights_in[slot], 16)
                sp.dma_start(w2[:, slot, :, :], bass.AP(M.exp_w2.tensor, e * (P * HID), [[HID, P], [1, HID]])
                             ).then_inc(weights_in[slot], 16)
                sp.dma_start(b1[:, slot, :], bass.AP(M.cols.tensor, e * HC + EXP_B1, [[NCOLS, P], [1, HC]])
                             ).then_inc(weights_in[slot], 16)

            over_experts(sp, expert)
            sp.wait_ge(layer1_in, 16)

        @block.scalar
        def _(act):
            layer_norm_root(nc, act, N, var_ready, std_ready, 1)
            act.wait_ge(gap_ready, 1)
            nc.scalar.activation(ratio[:, :], gap[:, :], ACT.Exp).then_inc(ratio_ready, 1)
            for c in range(QUAD):
                act.wait_ge(gates_turned, c + 1)
                nc.scalar.copy(gatesT[:, c * BANK:(c + 1) * BANK], bank[2 + c % 2][0:E, :]).then_inc(gatesT_kept, 1)

            def expert(e, pair, slot, at):
                act.wait_ge(weights_in[slot], 48 * (pair + 1))
                for c in range(QUAD):
                    unit = e * QUAD + c
                    if at * QUAD + c >= 2:
                        act.wait_ge(expert_done, unit - 1)
                    for k in range(HC):
                        act.wait_ge(hidden, unit * HC + k + 1)
                        nc.scalar.activation(mid[:, c % 2, k, :], bank[k][:, :], ACT.Gelu,
                                             bias=b1[:, slot, k:k + 1]).then_inc(hidden_kept, 1)

            over_experts(act, expert)
            act.wait_ge(expert_kept, UNITS)
            for t in range(0, NT, QUAD):
                nc.scalar.activation(h2[:, t:t + QUAD, :], G.x2[:, t:t + QUAD, :], ACT.Silu).then_inc(silu_ready, 1)

        @block.vector
        def _(dve):
            link = chained(dve, chain)
            layer_norm(nc, dve, link, N, G.x2, h2, var_ready, std_ready, 1)
            nc.vector.memset(gates[:, :, :], 0.0).then_inc(h2_ready, 1)
            for c in range(QUAD):
                dve.wait_ge(h2_turned, c + 1)
                nc.vector.tensor_scalar(h2T[:, c * BANK:(c + 1) * BANK], bank[c % 2][:, :], G.col("ln2_g"),
                                        G.col("ln2_b"), ALU.mult, ALU.add).then_inc(h2T_kept, 1)
            dve.wait_ge(gated, 1)
            link(nc.vector.tensor_tensor(logits[:, :, :], bank[4][:, 0:NT * E].rearrange("p (t e) -> p t e", e=E),
                                         G.row("gate_b").unsqueeze(1).to_broadcast([P, NT, E]), ALU.add))
            for t in range(NT):
                last = nc.vector.max(top[:, t, :], logits[:, t, :])
            link(last)
            for t in range(NT):
                last = nc.vector.max_index(top_at[:, t, :], top[:, t, :], logits[:, t, :])
            link(last)
            link(nc.vector.tensor_copy(top_slot[:, :, :], top_at[:, :, 0:2]))
            nc.vector.tensor_tensor(gap[:, :], top[:, :, 1], top[:, :, 0], ALU.subtract).then_inc(gap_ready, 1)
            dve.wait_ge(ratio_ready, 1)
            link(nc.vector.tensor_scalar(share[:, 1, :], ratio[:, :], 1.0, None, ALU.add))
            link(nc.vector.reciprocal(share[:, 0, :], share[:, 1, :]))
            link(nc.vector.tensor_tensor(share[:, 1, :], ratio[:, :], share[:, 0, :], ALU.mult))
            slots = G.row("slots").unsqueeze(1).to_broadcast([P, NT, E])
            for i in range(2):
                link(nc.vector.tensor_tensor(pick[:, i, :, :], slots,
                                             top_slot[:, :, i].unsqueeze(2).to_broadcast([P, NT, E]), ALU.is_equal))
                link(nc.vector.tensor_tensor(pick[:, i, :, :], pick[:, i, :, :],
                                             share[:, i, :].unsqueeze(2).to_broadcast([P, NT, E]), ALU.mult))
            nc.vector.tensor_tensor(gates[:, :, :], pick[:, 0, :, :], pick[:, 1, :, :], ALU.add
                                    ).then_inc(gates_ready, 1)
            for c in range(QUAD):
                dve.wait_ge(biased, c + 1)
                tiles = G.x2[:, c * QUAD:(c + 1) * QUAD, :]
                nc.vector.tensor_tensor(tiles, tiles, bank[5][:, :].rearrange("p (t d) -> p t d", d=D), ALU.add
                                        ).then_inc(bias_kept, 1)

            def expert(e, pair, slot, at):
                for c in range(QUAD):
                    unit = e * QUAD + c
                    dve.wait_ge(expert_done, unit + 1)
                    if at == 0:
                        dve.wait_ge(bias_kept, c + 1)
                    else:
                        dve.wait_ge(expert_kept, unit - QUAD + 1)
                    for t in range(QUAD):
                        tile = G.x2[:, c * QUAD + t, :]
                        gate = gates[:, c * QUAD + t, :]
                        last = nc.vector.scalar_tensor_tensor(tile, bank[4 + c % 2][:, t * D:(t + 1) * D],
                                                              gate[:, bass.ds(e, 1)], tile, ALU.mult, ALU.add)
                    last.then_inc(expert_kept, 1)

            over_experts(dve, expert)
            for i in range(QUAD):
                tiles = slice(i * QUAD, (i + 1) * QUAD)
                dve.wait_ge(silu_ready, i + 1)
                link(nc.vector.tensor_tensor(h2[:, tiles, :], h2[:, tiles, :], G.mixer[:, tiles, :], ALU.mult))
                last = nc.vector.tensor_tensor(G.xt[:, tiles, :], G.xt[:, tiles, :], h2[:, tiles, :], ALU.add)
            link(last)

        @block.tensor
        def _(pe):
            pe.wait_ge(h2_ready, 1)
            for c in range(QUAD):
                if c >= 2:
                    pe.wait_ge(h2T_kept, c - 1)
                for k in range(QUAD):
                    last = nc.tensor.transpose(bank[c % 2][:, k * P:(k + 1) * P], h2[:, c * QUAD + k, :],
                                               G.ident[:, :])
                last.then_inc(h2_turned, 1)
            pe.wait_ge(h2T_kept, QUAD)
            for t in range(NT):
                last = nc.tensor.matmul(bank[4][:, t * E:(t + 1) * E], h2T[:, t * P:(t + 1) * P], G.mat("gate"),
                                        start=True, stop=True)
            last.then_inc(gated, 1)

            def hidden_layer(e, pair, slot, at, c):
                unit = e * QUAD + c
                if c == 0:
                    pe.wait_ge(weights_in[slot], 48 * (pair + 1))
                for k in range(HC):
                    if at * QUAD + c >= 1:
                        pe.wait_ge(hidden_kept, unit * HC + k - 3)
                    nc.tensor.matmul(bank[k][:, :], w1[:, slot, k * P:(k + 1) * P],
                                     h2T[:, c * BANK:(c + 1) * BANK], start=True, stop=True).then_inc(hidden, 1)

            def output_layer(e, pair, slot, at, c):
                unit = e * QUAD + c
                pe.wait_ge(hidden_kept, (unit + 1) * HC)
                if at * QUAD + c >= 2:
                    pe.wait_ge(expert_kept, unit - 1)
                for t in range(QUAD):
                    for k in range(HC):
                        last = nc.tensor.matmul(bank[4 + c % 2][:, t * D:(t + 1) * D],
                                                mid[:, c % 2, k, t * P:(t + 1) * P], w2[:, slot, k, :],
                                                start=(k == 0), stop=(k == HC - 1))
                last.then_inc(expert_done, 1)

            pe.wait_ge(gates_ready, 1)
            for c in range(QUAD):
                if c >= 2:
                    pe.wait_ge(gatesT_kept, c - 1)
                for k in range(QUAD):
                    last = nc.tensor.transpose(bank[2 + c % 2][0:E, k * P:(k + 1) * P],
                                               gates[:, c * QUAD + k, :], G.ident[:, :])
                last.then_inc(gates_turned, 1)
            pe.wait_ge(b2_in, 16)
            for c in range(QUAD):
                pe.wait_ge(gatesT_kept, c + 1)
                if c >= 1:
                    pe.wait_ge(bias_kept, c)
                for k in range(QUAD):
                    t = c * QUAD + k
                    last = nc.tensor.matmul(bank[5][:, k * D:(k + 1) * D], gatesT[:, t * P:(t + 1) * P], b2[:, :],
                                            start=True, stop=True)
                last.then_inc(biased, 1)
            pe.wait_ge(bias_kept, QUAD)
            hidden_layer(0, 0, 0, 0, 0)

            def expert(e, pair, slot, at):
                for c in range(QUAD):
                    if c + 1 < QUAD:
                        hidden_layer(e, pair, slot, at, c + 1)
                    elif at + 1 < E:
                        hidden_layer(e + 1, pair + slot, 1 - slot, at + 1, 0)
                    output_layer(e, pair, slot, at, c)

            over_experts(pe, expert)


def stage_linear_attention(nc, G, M):
    EPS_DEN = 1e-6
    NB = 7
    PAIRS = LH // 2
    VA = LD + 1
    PAIR_GROUPS = [range(0, 3), range(3, 6), range(6, 8)]
    NAMES = ["q0", "q1", "k0", "k1", "v0", "v1", "turn0", "turn1", "out", "s0", "s1", "s2", "s3",
             "kt0", "kt1", "num0", "num1", "num2", "st0", "st1", "st2"]
    LATE = NAMES[6:9]
    ACT_JOBS = [n for n in NAMES if n[:-1] in ("v", "turn", "kt")]
    DVE_JOBS = [n for n in NAMES if n not in ACT_JOBS]
    NJ = len(NAMES)
    assert NJ % NB == 0

    def count(names, t, name):
        late = sum(n in names for n in LATE)
        if isinstance(t, int) and t == 0:
            return [n for n in names if n not in LATE].index(name) + 1
        return t * len(names) + (names.index(name) + 1 - late)

    def count_tail(names, name):
        late = [n for n in LATE if n in names]
        return NT * len(names) - len(late) + late.index(name) + 1

    with ExitStack() as ctx:
        def sb(name, shape, dt=F32):
            return ctx.enter_context(nc.sbuf_tensor(f"l_{name}", shape, dt))

        def sem(name):
            return ctx.enter_context(nc.semaphore(f"l_{name}"))

        h = sb("h", [P, P])
        exps = sb("exps", [P, 4, BANK])
        qk = sb("qk", [P, 2, PAIRS, P])
        k_tok = sb("k_tok", [P, PAIRS * P])
        v = sb("v", [P, LH, VA])
        scores = sb("scores", [P, LH, P])
        state = sb("state", [P, PAIRS, 2 * VA])
        den = sb("den", [P, 3, 6])
        inv_den = sb("inv_den", [P, 3, 6])
        att = sb("att", [P, LH * LD])
        attT = sb("attT", [P, PAIRS, P])
        bank = [ctx.enter_context(nc.psum_tensor(f"l_bank{i}", [P, BANK], F32)) for i in range(NB)]
        h_in = sem("h_in")
        ones_ready = sem("ones_ready")
        state_zero = sem("state_zero")
        done = sem("done")
        exp_ready = sem("exp_ready")
        act_kept = sem("act_kept")
        dve_kept = sem("dve_kept")
        chain = sem("chain")
        block = ctx.enter_context(nc.Block())

        def over_tiles(eng, tile):
            for b in range(B):
                peeled = 2 if b == 0 else 1
                for t in range(b * NS, b * NS + peeled):
                    tile(t, t)
                with eng.Fori(b * NS + peeled, (b + 1) * NS) as t:
                    tile(t, b * NS + peeled)

        def bank_of(name):
            return bank[NAMES.index(name) % NB]

        @block.gpsimd
        def _(pool):
            nc.gpsimd.memset(v[:, :, LD:VA], 1.0).then_inc(ones_ready, 1)

            def tile(t, at):
                if at >= 1:
                    pool.wait_ge(done, count(NAMES, t - 1, "v1"))
                nc.gpsimd.tensor_copy(h[:, :], G.h1T[:, bass.ds(t * P, P)]).then_inc(h_in, 1)

            over_tiles(pool, tile)

        @block.scalar
        def _(act):
            def turned(wait_for, g):
                act.wait_ge(done, wait_for)
                nc.scalar.copy(attT[:, 4 * g:4 * g + 4, :], bank_of(f"turn{g}")[:, :].rearrange(
                    "p (c t) -> p c t", t=P)).then_inc(act_kept, 1)

            def tile(t, at):
                for i, name in enumerate(("q0", "q1", "k0", "k1")):
                    act.wait_ge(done, count(NAMES, t, name))
                    if at >= 1:
                        act.wait_ge(dve_kept, count(DVE_JOBS, t - 1, name))
                    nc.scalar.activation(exps[:, i, :], bank_of(name)[:, :], ACT.Exp).then_inc(exp_ready, 1)
                if at == 0:
                    act.wait_ge(ones_ready, 1)
                for g in range(2):
                    act.wait_ge(done, count(NAMES, t, f"v{g}"))
                    nc.scalar.copy(v[:, 8 * g:8 * g + 8, 0:LD], bank_of(f"v{g}")[:, :].rearrange(
                        "p (h d) -> p h d", d=LD)).then_inc(act_kept, 1)
                if at >= 1:
                    for g in range(2):
                        turned(count(NAMES, t, f"turn{g}"), g)
                for g in range(2):
                    act.wait_ge(done, count(NAMES, t, f"kt{g}"))
                    nc.scalar.copy(k_tok[:, g * BANK:(g + 1) * BANK], bank_of(f"kt{g}")[:, :]).then_inc(act_kept, 1)

            over_tiles(act, tile)
            for g in range(2):
                turned(count_tail(NAMES, f"turn{g}"), g)

        @block.vector
        def _(dve):
            def residual(wait_for, t):
                dve.wait_ge(done, wait_for)
                nc.vector.tensor_tensor(G.x2[:, :, :].rearrange("p t d -> p (t d)")[:, bass.ds(t * P, P)],
                                        bank_of("out")[:, 0:D],
                                        G.xn[:, :, :].rearrange("p t d -> p (t d)")[:, bass.ds(t * P, P)],
                                        ALU.add).then_inc(dve_kept, 1)

            def tile(t, at):
                link = chained(dve, chain, t * 10)
                if at in (0, NS):
                    if at:
                        dve.wait_ge(dve_kept, count(DVE_JOBS, t - 1, "st2"))
                    nc.vector.memset(state[:, :, :], 0.0).then_inc(state_zero, 1)
                    dve.wait_ge(state_zero, at // NS + 1)
                for i, name in enumerate(("q0", "q1", "k0", "k1")):
                    dve.wait_ge(exp_ready, t * 4 + i + 1)
                    link(nc.vector.tensor_scalar(exps[:, i, :], exps[:, i, :], 1.0, None, ALU.min))
                    nc.vector.scalar_tensor_tensor(
                        qk[:, i // 2, 4 * (i % 2):4 * (i % 2) + 4, :].rearrange("p c t -> p (c t)"),
                        bank_of(name)[:, :], 1.0, exps[:, i, :], ALU.add, ALU.max).then_inc(dve_kept, 1)
                if at >= 1:
                    residual(count(NAMES, t, "out"), t - 1)
                for i in range(4):
                    dve.wait_ge(done, count(NAMES, t, f"s{i}"))
                    first = 8 * (i // 2) + i % 2
                    nc.vector.tensor_tensor(scores[:, first:first + 7:2, :], bank_of(f"s{i}")[:, :].rearrange(
                        "p (h t) -> p h t", t=P), G.causal01[:, :].unsqueeze(1).to_broadcast([P, 4, P]),
                        ALU.mult).then_inc(dve_kept, 1)
                for g, pairs in enumerate(PAIR_GROUPS):
                    n = 2 * len(pairs)
                    dve.wait_ge(done, count(NAMES, t, f"num{g}"))
                    sums = bank_of(f"num{g}")[:, 0:n * VA].rearrange("p (h d) -> p h d", d=VA)
                    link(nc.vector.tensor_scalar(den[:, g, 0:n], sums[:, :, LD], EPS_DEN, None, ALU.max))
                    link(nc.vector.reciprocal(inv_den[:, g, 0:n], den[:, g, 0:n]))
                    first = 2 * pairs[0] * LD
                    nc.vector.tensor_tensor(att[:, first:first + n * LD].rearrange("p (h d) -> p h d", d=LD),
                                            sums[:, :, 0:LD], inv_den[:, g, 0:n].unsqueeze(2).to_broadcast(
                                                [P, n, LD]), ALU.mult).then_inc(dve_kept, 1)
                for g, pairs in enumerate(PAIR_GROUPS):
                    dve.wait_ge(done, count(NAMES, t, f"st{g}"))
                    some = slice(pairs[0], pairs[-1] + 1)
                    part = bank_of(f"st{g}")[:, 0:len(pairs) * 2 * VA].rearrange("p (c d) -> p c d", d=2 * VA)
                    for rows, cols in ((slice(0, LD), slice(0, VA)), (slice(LD, P), slice(VA, 2 * VA))):
                        last = nc.vector.tensor_tensor(state[rows, some, cols], part[rows, :, cols],
                                                       state[rows, some, cols], ALU.add)
                    last.then_inc(dve_kept, 1)
                assert link.done[0] == 10

            over_tiles(dve, tile)
            residual(count_tail(NAMES, "out"), NT - 1)

        @block.tensor
        def _(pe):
            def free(t, at, name):
                p = NAMES.index(name) - NB
                if at == 0:
                    while p >= 0 and NAMES[p] in LATE:
                        p -= NB
                    if p < 0:
                        return
                if at == NT and p >= 0:
                    p -= NB
                before = t if p >= 0 else t - 1
                owner = NAMES[p % NJ]
                if at == 1 and p < 0 and owner in LATE:
                    owner = NAMES[p % NJ - NB]
                if owner in ACT_JOBS:
                    pe.wait_ge(act_kept, count(ACT_JOBS, before, owner))
                else:
                    pe.wait_ge(dve_kept, count(DVE_JOBS, before, owner))

            def turn_att(g):
                for c in range(4):
                    last = nc.tensor.transpose(bank_of(f"turn{g}")[:, c * P:(c + 1) * P],
                                               att[:, (4 * g + c) * P:(4 * g + c + 1) * P], G.ident[:, :])
                last.then_inc(done, 1)

            def project():
                w = G.mat1("l_o")
                for c in range(PAIRS):
                    last = nc.tensor.matmul(bank_of("out")[:, 0:D], attT[:, c, :], w[:, c * D:(c + 1) * D],
                                            start=(c == 0), stop=(c == PAIRS - 1))
                last.then_inc(done, 1)

            def tile(t, at):
                pe.wait_ge(h_in, t + 1)
                for i, name in enumerate(("q0", "q1", "k0", "k1")):
                    free(t, at, name)
                    w = G.mat1("l_q" if i < 2 else "l_k")
                    for c in range(4):
                        f = (4 * (i % 2) + c) * P
                        last = nc.tensor.matmul(bank_of(name)[:, c * P:(c + 1) * P], w[:, f:f + P], h[:, :],
                                                start=True, stop=True)
                    last.then_inc(done, 1)
                for g in range(2):
                    free(t, at, f"v{g}")
                    nc.tensor.matmul(bank_of(f"v{g}")[:, :], h[:, :], G.mat1("l_v")[:, g * BANK:(g + 1) * BANK],
                                     start=True, stop=True).then_inc(done, 1)
                if at >= 1:
                    pe.wait_ge(dve_kept, count(DVE_JOBS, t - 1, "num2"))
                    for g in range(2):
                        free(t, at, f"turn{g}")
                        turn_att(g)
                    free(t, at, "out")
                    pe.wait_ge(act_kept, count(ACT_JOBS, t, "turn1"))
                    project()
                pe.wait_ge(dve_kept, count(DVE_JOBS, t, "k1"))
                for i in range(4):
                    free(t, at, f"s{i}")
                    rows = slice(0, LD) if i % 2 == 0 else slice(LD, P)
                    for c in range(4):
                        pair = 4 * (i // 2) + c
                        last = nc.tensor.matmul(bank_of(f"s{i}")[:, c * P:(c + 1) * P], qk[rows, 1, pair, :],
                                                qk[rows, 0, pair, :], start=True, stop=True)
                    last.then_inc(done, 1)
                for g in range(2):
                    free(t, at, f"kt{g}")
                    for c in range(4):
                        last = nc.tensor.transpose(bank_of(f"kt{g}")[:, c * P:(c + 1) * P],
                                                   qk[:, 1, 4 * g + c, :], G.ident[:, :])
                    last.then_inc(done, 1)
                pe.wait_ge(act_kept, count(ACT_JOBS, t, "v1"))
                for g, pairs in enumerate(PAIR_GROUPS):
                    free(t, at, f"num{g}")
                    pe.wait_ge(dve_kept, count(DVE_JOBS, t, "s1" if pairs[-1] < 4 else "s3"))
                    for m, c in enumerate(pairs):
                        out = bank_of(f"num{g}")[:, m * 2 * VA:(m + 1) * 2 * VA]
                        nc.tensor.matmul(out, qk[:, 0, c, :], state[:, c, :], start=(m == 0), stop=False,
                                         skip_group_check=True)
                        for i in range(2):
                            last = nc.tensor.matmul(out[:, i * VA:(i + 1) * VA], scores[:, 2 * c + i, :],
                                                    v[:, 2 * c + i, :], start=False, stop=True,
                                                    skip_group_check=True)
                    last.then_inc(done, 1)
                for g, pairs in enumerate(PAIR_GROUPS):
                    free(t, at, f"st{g}")
                    pe.wait_ge(act_kept, count(ACT_JOBS, t, "kt0" if pairs[-1] < 4 else "kt1"))
                    for m, c in enumerate(pairs):
                        last = nc.tensor.matmul(bank_of(f"st{g}")[:, m * 2 * VA:(m + 1) * 2 * VA],
                                                k_tok[:, c * P:(c + 1) * P],
                                                v[:, 2 * c:2 * c + 2, :].rearrange("p h d -> p (h d)"),
                                                start=True, stop=True)
                    last.then_inc(done, 1)

            over_tiles(pe, tile)
            pe.wait_ge(dve_kept, count(DVE_JOBS, NT - 1, "num2"))
            for g in range(2):
                free(NT, NT, f"turn{g}")
                turn_att(g)
            free(NT, NT, "out")
            pe.wait_ge(act_kept, count_tail(ACT_JOBS, "turn1"))
            project()


def stage_adapters(nc, G, M):
    CLAMP_MAX = float(np.log(1.0 / 0.01))
    EPS_NORM = 1e-12
    ZW = D + PROJ + RSUM
    FC = DF // P
    with ExitStack() as ctx:
        def sb(name, shape, dt=F32):
            return ctx.enter_context(nc.sbuf_tensor(f"a_{name}", shape, dt))

        used = []

        def sem(name):
            s = ctx.enter_context(nc.semaphore(f"a_{name}"))
            used.append(s.num)
            return s

        N = norm_stats_tensors(sb, "n")
        h = sb("h", [P, NT, D])
        hT = sb("hT", [P, T])
        mid = sb("mid", [P, 2, FC, BANK])
        z = sb("z", [P, NT, ZW])
        sim = sb("sim", [PROJ, 4, NE1])
        ones = sb("ones", [PROJ, PROJ])
        up = sb("up", [RSUM, D])
        proj = sb("proj", [P, NT, PROJ])
        proj_sq = sb("proj_sq", [P, NT, PROJ])
        norms = sb("norms", [P, 4, NT])
        temp = sb("temp", [P, 2])
        projT = sb("projT", [PROJ, T])
        logits = sb("logits", [P, NT, 8])
        top = sb("top", [P, NT, 8])
        top_at = sb("top_at", [P, NT, 8], U32)
        top_slot = sb("top_slot", [P, NT])
        exps = sb("exps", [P, NT, NE1])
        total = sb("total", [P, 2, NT])
        pick = sb("pick", [P, NT, NE1])
        low = sb("low", [P, NT, RSUM])
        lowT = sb("lowT", [RSUM, T])
        gate = sb("gate", [P, NT, D])
        result = sb("result", [P, NT, D])
        bank = [ctx.enter_context(nc.psum_tensor(f"a_bank{i}", [P, BANK], F32)) for i in range(8)]
        small_in = sem("small_in")
        chain = sem("chain")
        pool_ready = sem("pool_ready")
        var_ready = sem("var_ready")
        std_ready = sem("std_ready")
        z_done = sem("z_done")
        z_kept = sem("z_kept")
        h_ready = sem("h_ready")
        h_turned = sem("h_turned")
        hT_kept = sem("hT_kept")
        hidden = sem("hidden")
        hidden_kept = sem("hidden_kept")
        ffn_done = sem("ffn_done")
        ffn_kept = sem("ffn_kept")
        sim_summed = sem("sim_summed")
        squares_ready = sem("squares_ready")
        roots_ready = sem("roots_ready")
        temp_ready = sem("temp_ready")
        temp_exp = sem("temp_exp")
        sim_ready = sem("sim_ready")
        proj_ready = sem("proj_ready")
        proj_turned = sem("proj_turned")
        projT_kept = sem("projT_kept")
        logits_done = sem("logits_done")
        margin_ready = sem("margin_ready")
        exps_ready = sem("exps_ready")
        low_ready = sem("low_ready")
        low_turned = sem("low_turned")
        lowT_kept = sem("lowT_kept")
        gate_done = sem("gate_done")
        gate_kept = sem("gate_kept")
        silu_ready = sem("silu_ready")
        result_ready = sem("result_ready")
        stored = sem("stored")
        clear_semaphores(nc, range(min(used), max(used) + 1))
        block = ctx.enter_context(nc.Block())

        @block.sync
        def _(sp):
            sp.dma_start(sim[:, 0, :], M.sim).then_inc(small_in, 16)
            sp.dma_start(up[:, :], M.up).then_inc(small_in, 16)
            out = M.out.rearrange("b (t p) d -> p (b t) d", p=P)
            for c in range(QUAD):
                sp.wait_ge(result_ready, c + 1)
                sp.dma_start(out[:, c * QUAD:(c + 1) * QUAD, :], result[:, c * QUAD:(c + 1) * QUAD, :]
                             ).then_inc(stored, 16)
            sp.wait_ge(stored, 16 * QUAD)

        @block.gpsimd
        def _(pool):
            nc.gpsimd.memset(ones[:, :], 1.0).then_inc(pool_ready, 1)
            pool.wait_ge(pool_ready, 1)
            nc.gpsimd.memset(logits[:, :, :], -3e38).then_inc(pool_ready, 1)

        @block.scalar
        def _(act):
            for i in range(NT // 2):
                act.wait_ge(z_done, i + 1)
                nc.scalar.copy(z[:, 2 * i:2 * i + 2, :], bank[6 + i % 2][:, 0:2 * ZW].rearrange(
                    "p (t w) -> p t w", w=ZW)).then_inc(z_kept, 1)
            layer_norm_root(nc, act, N, var_ready, std_ready, 1)
            act.wait_ge(sim_summed, 1)
            nc.scalar.activation(sim[:, 2, :], bank[5][0:PROJ, 0:NE1], ACT.Sqrt).then_inc(roots_ready, 1)
            act.wait_ge(squares_ready, 1)
            nc.scalar.activation(norms[:, 1, :], norms[:, 0, :], ACT.Sqrt).then_inc(roots_ready, 1)
            act.wait_ge(temp_ready, 1)
            nc.scalar.activation(temp[:, 1:2], temp[:, 0:1], ACT.Exp).then_inc(temp_exp, 1)
            for c in range(QUAD):
                act.wait_ge(proj_turned, c + 1)
                nc.scalar.copy(projT[:, c * BANK:(c + 1) * BANK], bank[6 + c % 2][0:PROJ, :]).then_inc(projT_kept, 1)
            act.wait_ge(margin_ready, 1)
            nc.scalar.activation(exps[:, :, :], exps[:, :, :], ACT.Exp).then_inc(exps_ready, 1)
            for c in range(QUAD):
                act.wait_ge(low_turned, c + 1)
                nc.scalar.copy(lowT[:, c * BANK:(c + 1) * BANK], bank[6 + c % 2][0:RSUM, :]).then_inc(lowT_kept, 1)
            for c in range(QUAD):
                if c >= 2:
                    act.wait_ge(ffn_done, c - 1)
                for k in range(FC):
                    act.wait_ge(hidden, c * FC + k + 1)
                    nc.scalar.activation(mid[:, c % 2, k, :], bank[k][:, :], ACT.Gelu).then_inc(hidden_kept, 1)
            for c in range(QUAD):
                act.wait_ge(gate_kept, c + 1)
                tiles = slice(c * QUAD, (c + 1) * QUAD)
                nc.scalar.activation(result[:, tiles, :], gate[:, tiles, :], ACT.Silu).then_inc(silu_ready, 1)

        @block.vector
        def _(dve):
            link = chained(dve, chain)
            layer_norm(nc, dve, link, N, G.x2, h, var_ready, std_ready, 1)
            dve.wait_ge(small_in, 32)
            nc.vector.tensor_tensor(sim[:, 1, :], sim[:, 0, :], sim[:, 0, :], ALU.mult).then_inc(h_ready, 1)
            nc.vector.tensor_scalar(temp[:, 0:1], G.row("temp"), CLAMP_MAX, None, ALU.min).then_inc(temp_ready, 1)
            dve.wait_ge(z_kept, NT // 2)
            nc.vector.tensor_tensor(proj[:, :, :], z[:, :, D:D + PROJ], G.row("router_b").unsqueeze(1).to_broadcast(
                [P, NT, PROJ]), ALU.add).then_inc(proj_ready, 1)
            for c in range(QUAD):
                dve.wait_ge(h_turned, c + 1)
                nc.vector.tensor_scalar(hT[:, c * BANK:(c + 1) * BANK], bank[c][:, :], G.col("l1_ln2_g"),
                                        G.col("l1_ln2_b"), ALU.mult, ALU.add).then_inc(hT_kept, 1)
            dve.wait_ge(proj_ready, 1)
            link(nc.vector.tensor_tensor(proj_sq[:, :, :], proj[:, :, :], proj[:, :, :], ALU.mult))
            nc.vector.tensor_reduce(norms[:, 0, :], proj_sq[:, :, :], AX.X, ALU.add).then_inc(squares_ready, 1)
            dve.wait_ge(roots_ready, 2)
            link(nc.vector.tensor_scalar(sim[:, 2, :], sim[:, 2, :], EPS_NORM, None, ALU.max))
            link(nc.vector.reciprocal(sim[:, 1, :], sim[:, 2, :]))
            nc.vector.tensor_tensor(sim[:, 3, :], sim[:, 0, :], sim[:, 1, :], ALU.mult).then_inc(sim_ready, 1)
            link(nc.vector.tensor_scalar(norms[:, 2, :], norms[:, 1, :], EPS_NORM, None, ALU.max))
            link(nc.vector.reciprocal(norms[:, 3, :], norms[:, 2, :]))
            dve.wait_ge(temp_exp, 1)
            link(nc.vector.tensor_scalar(norms[:, 3, :], norms[:, 3, :], temp[:, 1:2], None, ALU.mult))
            dve.wait_ge(pool_ready, 2)
            dve.wait_ge(logits_done, 1)
            link(nc.vector.tensor_tensor(logits[:, :, 0:NE1], bank[4][:, 0:NT * NE1].rearrange(
                "p (t e) -> p t e", e=NE1), norms[:, 3, :].unsqueeze(2).to_broadcast([P, NT, NE1]), ALU.mult))
            for t in range(NT):
                last = nc.vector.max(top[:, t, :], logits[:, t, :])
            link(last)
            nc.vector.tensor_tensor(exps[:, :, :], logits[:, :, 0:NE1], top[:, :, 0].unsqueeze(2).to_broadcast(
                [P, NT, NE1]), ALU.subtract).then_inc(margin_ready, 1)
            for t in range(NT):
                last = nc.vector.max_index(top_at[:, t, :], top[:, t, :], logits[:, t, :])
            link(last)
            link(nc.vector.tensor_copy(top_slot[:, :], top_at[:, :, 0]))
            link(nc.vector.tensor_tensor(pick[:, :, :], G.row("slots")[:, 0:NE1].unsqueeze(1).to_broadcast(
                [P, NT, NE1]), top_slot[:, :].unsqueeze(2).to_broadcast([P, NT, NE1]), ALU.is_equal))
            dve.wait_ge(exps_ready, 1)
            link(nc.vector.tensor_reduce(total[:, 0, :], exps[:, :, :], AX.X, ALU.add))
            link(nc.vector.reciprocal(total[:, 1, :], total[:, 0, :]))
            link(nc.vector.tensor_tensor(pick[:, :, :], pick[:, :, :], total[:, 1, :].unsqueeze(2).to_broadcast(
                [P, NT, NE1]), ALU.mult))
            at = 0
            for e, rank in enumerate(RANKS):
                last = nc.vector.tensor_tensor(low[:, :, at:at + rank], z[:, :, D + PROJ + at:D + PROJ + at + rank],
                                               pick[:, :, e].unsqueeze(2).to_broadcast([P, NT, rank]), ALU.mult)
                at += rank
            last.then_inc(low_ready, 1)
            for c in range(QUAD):
                tiles = slice(c * QUAD, (c + 1) * QUAD)
                dve.wait_ge(gate_done, c + 1)
                nc.vector.tensor_tensor(gate[:, tiles, :], bank[4 + c % 2][:, :].rearrange("p (t d) -> p t d", d=D),
                                        z[:, tiles, 0:D], ALU.add).then_inc(gate_kept, 1)
            for c in range(QUAD):
                tiles = slice(c * QUAD, (c + 1) * QUAD)
                dve.wait_ge(ffn_done, c + 1)
                nc.vector.tensor_tensor(G.mixer[:, tiles, :], bank[6 + c % 2][:, :].rearrange(
                    "p (t d) -> p t d", d=D), G.x2[:, tiles, :], ALU.add).then_inc(ffn_kept, 1)
            dve.wait_ge(ffn_kept, QUAD)
            for c in range(QUAD):
                tiles = slice(c * QUAD, (c + 1) * QUAD)
                dve.wait_ge(silu_ready, c + 1)
                link(nc.vector.tensor_tensor(result[:, tiles, :], result[:, tiles, :], G.mixer[:, tiles, :],
                                             ALU.mult))
                nc.vector.tensor_tensor(result[:, tiles, :], result[:, tiles, :], G.xt[:, tiles, :], ALU.add
                                        ).then_inc(result_ready, 1)

        @block.tensor
        def _(pe):
            w = G.mats1[:, MATS1["base"][0]:MATS1["base"][0] + ZW]
            for i in range(NT // 2):
                if i >= 2:
                    pe.wait_ge(z_kept, i - 1)
                for k in range(2):
                    t = 2 * i + k
                    last = nc.tensor.matmul(bank[6 + i % 2][:, k * ZW:(k + 1) * ZW], G.xnT[:, t * P:(t + 1) * P], w,
                                            start=True, stop=True)
                last.then_inc(z_done, 1)
            pe.wait_ge(h_ready, 1)
            for c in range(QUAD):
                for k in range(QUAD):
                    last = nc.tensor.transpose(bank[c][:, k * P:(k + 1) * P], h[:, c * QUAD + k, :], G.ident[:, :])
                last.then_inc(h_turned, 1)
            pe.wait_ge(pool_ready, 1)
            nc.tensor.matmul(bank[5][0:PROJ, 0:NE1], ones[:, :], sim[:, 1, :], start=True, stop=True
                             ).then_inc(sim_summed, 1)
            pe.wait_ge(proj_ready, 1)
            pe.wait_ge(z_kept, NT // 2)
            for c in range(QUAD):
                if c >= 2:
                    pe.wait_ge(projT_kept, c - 1)
                for k in range(QUAD):
                    last = nc.tensor.transpose(bank[6 + c % 2][0:PROJ, k * P:(k + 1) * P],
                                               proj[:, c * QUAD + k, :], G.ident[:, :])
                last.then_inc(proj_turned, 1)

            def hidden_layer(c):
                pe.wait_ge(hT_kept, QUAD)
                for k in range(FC):
                    if c >= 1:
                        pe.wait_ge(hidden_kept, (c - 1) * FC + k + 1)
                    nc.tensor.matmul(bank[k][:, :], G.mat1("f1")[:, k * P:(k + 1) * P],
                                     hT[:, c * BANK:(c + 1) * BANK], start=True, stop=True).then_inc(hidden, 1)

            pe.wait_ge(projT_kept, QUAD)
            pe.wait_ge(sim_ready, 1)
            for t in range(NT):
                last = nc.tensor.matmul(bank[4][:, t * NE1:(t + 1) * NE1], projT[:, t * P:(t + 1) * P],
                                        sim[:, 3, :], start=True, stop=True)
            last.then_inc(logits_done, 1)
            hidden_layer(0)
            pe.wait_ge(low_ready, 1)
            for c in range(QUAD):
                if c >= 2:
                    pe.wait_ge(lowT_kept, c - 1)
                for k in range(QUAD):
                    last = nc.tensor.transpose(bank[6 + c % 2][0:RSUM, k * P:(k + 1) * P], low[:, c * QUAD + k, :],
                                               G.ident[:, :])
                last.then_inc(low_turned, 1)
            for c in range(QUAD):
                pe.wait_ge(lowT_kept, c + 1)
                if c >= 2:
                    pe.wait_ge(gate_kept, c - 1)
                for k in range(QUAD):
                    t = c * QUAD + k
                    last = nc.tensor.matmul(bank[4 + c % 2][:, k * D:(k + 1) * D], lowT[:, t * P:(t + 1) * P],
                                            up[:, :], start=True, stop=True)
                last.then_inc(gate_done, 1)
            pe.wait_ge(lowT_kept, QUAD)
            for c in range(QUAD):
                if c + 1 < QUAD:
                    hidden_layer(c + 1)
                pe.wait_ge(hidden_kept, (c + 1) * FC)
                if c >= 2:
                    pe.wait_ge(ffn_kept, c - 1)
                for k in range(QUAD):
                    for m in range(FC):
                        last = nc.tensor.matmul(bank[6 + c % 2][:, k * D:(k + 1) * D],
                                                mid[:, c % 2, m, k * P:(k + 1) * P],
                                                G.mat1("f2")[:, m * D:(m + 1) * D], start=(m == 0),
                                                stop=(m == FC - 1))
                last.then_inc(ffn_done, 1)


def recurrent_block_kernel(nc, out, **ins):
    def scratch(name, shape, dt=F32):
        return nc.dram_tensor(name, shape, dt).ap()

    M = Named(**ins)
    M.out = out
    M.split = scratch("split", [5, PIECES, B, P, S], BF16)
    M.rel = scratch("rel", [BH, S + 2 * RPAD, NREL])
    M.window = scratch("window", [BH, S, WIN])
    with ExitStack() as ctx:
        def sb(name, shape, dt=F32):
            return ctx.enter_context(nc.sbuf_tensor(name, shape, dt))

        G = Named()
        G.xt = sb("xt", [P, NT, D])
        G.xn = sb("xn", [P, NT, D])
        G.cols = sb("cols", [P, NCOLS])
        G.rows = sb("rows", [P, NROWS])
        G.mats = sb("mats", [P, NMATS])
        G.ident = sb("ident", [P, P])
        G.identb = sb("identb", [P, P], BF16)
        G.mask_ij = sb("mask_ij", [P, P], BF16)
        G.mask_ji = sb("mask_ji", [P, P], BF16)
        G.causal01 = sb("causal01", [P, P])
        G.before_last = sb("before_last", [P, WIN])
        G.after_first = sb("after_first", [P, P])
        G.zeros = sb("zeros", [P, RPAD * NREL])
        G.negs = sb("negs", [P, 1])
        G.col = lambda name: G.cols[:, COL[name]:COL[name] + 1]
        G.row = lambda name: G.rows[:, ROWS[name][0]:ROWS[name][0] + ROWS[name][1]]
        G.mat = lambda name: G.mats[:, MATS[name][0]:MATS[name][0] + MATS[name][1]]
        G.mixer = sb("mixer", [P, NT, D])
        G.x2 = sb("x2", [P, NT, D])
        with ExitStack() as layer0:
            def sb0(name, shape, dt=F32):
                return layer0.enter_context(nc.sbuf_tensor(name, shape, dt))

            G.att = sb0("att", [P, BH, NS, DK + 1])
            G.catt = sb0("catt", [P, BH, NS, DK + 1])
            G.far = sb0("far", [P, BH, NS])
            G.v_rel = sb0("v_rel", [P, BH * 3 * NS, DK + 1])
            G.v_causal = sb0("v_causal", [P, BH * NS, DK + 1])
            G.v_rel_at = lambda heads, kind, tile: G.v_rel[:, :, 0:DK].rearrange(
                "p (n k j) d -> p n k j d", k=3, j=NS)[:, heads, kind, tile, :]
            G.v_causal_at = lambda heads, tile: G.v_causal[:, :, 0:DK].rearrange(
                "p (n j) d -> p n j d", j=NS)[:, heads, tile, :]
            G.rel_last = sb0("rel_last", [P, B, H, NS])
            with ExitStack() as turned:
                G.xnT = turned.enter_context(nc.sbuf_tensor("xnT", [P, T], F32))
                G.h1T = turned.enter_context(nc.sbuf_tensor("h1T", [P, T], F32))
                stage_normalize(nc, G, M, "n0", "ln1_g", "ln1_b", True)
                stage_project(nc, G, M)
            stage_attention(nc, G, M, True)
            stage_attention(nc, G, M, False)
            stage_combine(nc, G, M)
        with ExitStack() as layer1:
            G.mats1 = layer1.enter_context(nc.sbuf_tensor("mats1", [P, NMATS1], F32))
            G.mat1 = lambda name: G.mats1[:, MATS1[name][0]:MATS1[name][0] + MATS1[name][1]]
            stage_experts(nc, G, M)
            G.xnT = layer1.enter_context(nc.sbuf_tensor("xnT1", [P, T], F32))
            with ExitStack() as turned:
                G.h1T = turned.enter_context(nc.sbuf_tensor("h1T1", [P, T], F32))
                stage_normalize(nc, G, M, "n1", "l1_ln1_g", "l1_ln1_b", False)
                stage_linear_attention(nc, G, M)
            stage_adapters(nc, G, M)


def layout(inputs):
    f = lambda name: np.asarray(inputs[name])
    chunks = lambda w: w.reshape(-1, P, w.shape[-1]).transpose(1, 0, 2).reshape(P, -1)
    rk, rv = f("L0_attn_rel_k_emb"), f("L0_attn_rel_v_emb")
    cols = [f("L0_ffn_ln1_g"), f("L0_ffn_ln1_b"), f("L0_ffn_ln2_g"), f("L0_ffn_ln2_b"), f("L0_ffn_bq"),
            f("L0_ffn_bk"), np.tile(rk[0], H), np.tile(rk[-1], H), f("L1_attn_ln1_g"), f("L1_attn_ln1_b"),
            f("L1_attn_ln2_g"), f("L1_attn_ln2_b"), *f("L0_ffn_exp_b1").reshape(-1, P)]
    rows = [f("L0_attn_b_o"), f("L0_ffn_bv"), f("L0_ffn_bp"), f("L0_ffn_gate_b"), np.tile(rv[0], H),
            np.tile(rv[-1], H), f("L1_ffn_bp"), f("L1_ffn_temp"), np.arange(E, dtype=np.float32)]
    mats = [f("L0_attn_Wq").T, f("L0_attn_Wk").T, f("L0_attn_Wv").T, f("L0_attn_Wo").T, f("L0_ffn_Wq"),
            f("L0_ffn_Wk"), f("L0_ffn_Wv"), f("L0_ffn_Wp"), f("L0_ffn_gate_W")]
    mats1 = [f("L1_attn_Wq"), f("L1_attn_Wk"), f("L1_attn_Wv"), chunks(f("L1_attn_Wo")), f("L1_attn_Wf1"),
             chunks(f("L1_attn_Wf2")), f("L1_ffn_W").T, f("L1_ffn_Wp").T,
             np.concatenate([f(f"L1_ffn_Wd{i}") for i in range(NE1)], 0).T]
    rk_block = np.zeros((H, DK, H, NREL), np.float32)
    rk_block_first = np.zeros((H, DK, H, NREL), np.float32)
    rv_block = np.zeros((H, NREL, H, DK), np.float32)
    rv_block_first = np.zeros((H, NREL, H, DK), np.float32)
    for h in range(H):
        rk_block[h, :, h, :] = rk.T
        rk_block_first[h, :, h, :] = np.broadcast_to(rk[0][:, None], (DK, NREL))
        rv_block[h, :, h, :] = rv
        rv_block_first[h, :, h, :] = np.broadcast_to(rv[0], (NREL, DK))
    fill = lambda w: np.concatenate([w.reshape(H * NREL, D), np.zeros((RCH * P - H * NREL, D), np.float32)], 0)
    return {
        "x": f("L0_attn_x").reshape(T, D),
        "cols": np.stack(cols, 1), "rows": np.concatenate(rows), "mats": np.concatenate(mats, 1),
        "mats1": np.concatenate(mats1, 1),
        "rk_block": rk_block.reshape(D, H * NREL), "rk_block_first": rk_block_first.reshape(D, H * NREL),
        "rv_block": chunks(fill(rv_block)), "rv_block_first": chunks(fill(rv_block_first)),
        "exp_w1": f("L0_ffn_exp_W1"), "exp_w2": f("L0_ffn_exp_W2").reshape(E, HID // P, P, D).transpose(0, 2, 1, 3),
        "exp_b2": f("L0_ffn_exp_b2"), "sim": f("L1_ffn_sim"),
        "up": np.concatenate([f(f"L1_ffn_Wu{i}").T for i in range(NE1)], 0),
    }


def kernel(**inputs):
    import concourse.bacc as bacc
    from concourse.bass_utils import run_bass_kernel_spmd

    nc = bacc.Bacc("TRN2", target_bir_lowering=False, num_devices=1)
    arrays, args = {}, {}
    for name, a in layout(inputs).items():
        arrays[f"in_{name}"] = a = np.ascontiguousarray(a)
        args[name] = nc.dram_tensor(f"in_{name}", a.shape, mybir.dt.from_np(a.dtype), kind="ExternalInput").ap()
    out = nc.dram_tensor("out", (B, S, D), F32, kind="ExternalOutput").ap()
    recurrent_block_kernel(nc, out, **args)
    result = run_bass_kernel_spmd(nc, [arrays], core_ids=[0])
    return result.results[0]["out"]
```

```python
from contextlib import ExitStack

import numpy as np
import concourse.bass as bass
import concourse.mybir as mybir

F32 = mybir.dt.float32
BF16 = mybir.dt.bfloat16
U32 = mybir.dt.uint32
ALU = mybir.AluOpType
ACT = mybir.ActivationFunctionType
AX = mybir.AxisListType

P = 128
B, S, D = 2, 1024, 128
T = B * S
NT = T // P
NS = S // P
H, DK = 16, 8
BH = B * H
REL = 32
NREL = 2 * REL + 1
WIN = P + 2 * REL
E, HID = 8, 512
LH, LD = 16, 64
DF = 512
PROJ, NE1 = 32, 4
RANKS = [1, 2, 4, 8]
RSUM = sum(RANKS)
WARM = 3
BANK = 512
QUAD = BANK // P
RING = 4
EPS = 1e-5
MASKED = -1e38
PIECES = 3
QROWS = 6 * DK
AROWS = 96
SROWS = AROWS + PIECES
VCOLS = DK + 1 + NS
RPAD = 2
RHEAD = (S + 2 * RPAD) * NREL

COLS = ["ln1_g", "ln1_b", "ln2_g", "ln2_b", "bq", "bk", "rk_first", "rk_last",
        "l1_ln1_g", "l1_ln1_b", "l1_ln2_g", "l1_ln2_b"]
COL = {name: n for n, name in enumerate(COLS)}
EXP_B1 = len(COLS)
NCOLS = EXP_B1 + E * HID // P
ROWS = {}
_at = 0
for _name, _n in [("b_o", D), ("bv", D), ("bp", D), ("gate_b", E), ("rv_first", D), ("rv_last", D),
                  ("router_b", PROJ), ("temp", 1), ("slots", E)]:
    ROWS[_name] = (_at, _n)
    _at += _n
NROWS = _at
MATS = {}
_at = 0
for _name, _n in [("r_q", D), ("r_k", D), ("r_v", D), ("r_o", D), ("c_q", D), ("c_k", D), ("c_v", D),
                  ("c_p", D), ("gate", E)]:
    MATS[_name] = (_at, _n)
    _at += _n
NMATS = _at
MATS1 = {}
_at = 0
for _name, _n in [("l_q", LH * LD), ("l_k", LH * LD), ("l_v", LH * LD), ("l_o", LH * LD), ("f1", DF),
                  ("f2", DF), ("base", D), ("router", PROJ), ("down", RSUM)]:
    MATS1[_name] = (_at, _n)
    _at += _n
NMATS1 = _at
RCH = (H * NREL + P - 1) // P
RGROUPS = [(0, 6), (6, 11), (11, 16)]


def chained(eng, sem, start=0):
    done = [0]

    def link(ins):
        done[0] += 1
        ins.then_inc(sem, 1)
        eng.wait_ge(sem, start + done[0])

    link.done = done
    return link


class Named(dict):
    __getattr__ = dict.__getitem__
    __setattr__ = dict.__setitem__


def norm_stats_tensors(sb, tag):
    return Named(
        stats=sb(f"{tag}_stats", [P, NT, 6], F32), mean_var=sb(f"{tag}_mean_var", [P, NT, 2], F32),
        var=sb(f"{tag}_var", [P, NT], F32), std=sb(f"{tag}_std", [P, NT], F32),
        rstd=sb(f"{tag}_rstd", [P, NT], F32), tmp=sb(f"{tag}_tmp", [P, NT], F32))


def layer_norm(nc, dve, link, N, src, dst, var_ready, std_ready, turn, tiles=range(NT)):
    a, b = tiles[0], tiles[-1] + 1
    for t in tiles:
        last = nc.vector.bn_stats(N.stats[:, t, :], src[:, t, :])
    link(last)
    for t in tiles:
        last = nc.vector.bn_aggr(N.mean_var[:, t, :], N.stats[:, t, :])
    link(last)
    nc.vector.tensor_scalar(N.var[:, a:b], N.mean_var[:, a:b, 1], EPS, None, ALU.add).then_inc(var_ready, 1)
    dve.wait_ge(std_ready, turn)
    link(nc.vector.reciprocal(N.rstd[:, a:b], N.std[:, a:b]))
    link(nc.vector.tensor_tensor(N.tmp[:, a:b], N.rstd[:, a:b], N.rstd[:, a:b], ALU.mult))
    link(nc.vector.tensor_tensor(N.tmp[:, a:b], N.tmp[:, a:b], N.var[:, a:b], ALU.mult))
    link(nc.vector.tensor_scalar(N.tmp[:, a:b], N.tmp[:, a:b], -0.5, 1.5, ALU.mult, ALU.add))
    link(nc.vector.tensor_tensor(N.rstd[:, a:b], N.rstd[:, a:b], N.tmp[:, a:b], ALU.mult))
    for t in tiles:
        last = nc.vector.tensor_scalar(dst[:, t, :], src[:, t, :], N.mean_var[:, t, 0:1], N.rstd[:, t:t + 1],
                                       ALU.subtract, ALU.mult)
    link(last)


def layer_norm_root(nc, act, N, var_ready, std_ready, turn, tiles=range(NT)):
    a, b = tiles[0], tiles[-1] + 1
    act.wait_ge(var_ready, turn)
    nc.scalar.activation(N.std[:, a:b], N.var[:, a:b], ACT.Sqrt).then_inc(std_ready, 1)


def stage_normalize(nc, G, M, tag, gain, bias, first):
    with ExitStack() as ctx:
        def sb(name, shape, dt=F32):
            return ctx.enter_context(nc.sbuf_tensor(name, shape, dt))

        def sem(name):
            return ctx.enter_context(nc.semaphore(name))

        N = norm_stats_tensors(sb, tag)
        xnn = sb(f"{tag}_xnn", [P, NT, D])
        xn_ps = [ctx.enter_context(nc.psum_tensor(f"{tag}_xn_ps{i}", [P, BANK], F32)) for i in range(2)]
        h1_ps = [ctx.enter_context(nc.psum_tensor(f"{tag}_h1_ps{i}", [P, BANK], F32)) for i in range(2)]
        x_in = sem(f"{tag}_x_in")
        par_in = sem(f"{tag}_par_in")
        chain = sem(f"{tag}_chain")
        var_ready = sem(f"{tag}_var_ready")
        std_ready = sem(f"{tag}_std_ready")
        xn_ready = sem(f"{tag}_xn_ready")
        ident0 = sem(f"{tag}_ident0")
        ident_ready = sem(f"{tag}_ident_ready")
        xn_turned = sem(f"{tag}_xn_turned")
        h1_turned = sem(f"{tag}_h1_turned")
        xn_kept = sem(f"{tag}_xn_kept")
        h1_kept = sem(f"{tag}_h1_kept")
        block = ctx.enter_context(nc.Block())

        @block.sync
        def _(sp):
            if not first:
                return
            sp.dma_start(G.xt[:, :, :], M.x.rearrange("(t p) d -> p t d", p=P)).then_inc(x_in, 16)
            sp.dma_start(G.cols[:, :], M.cols).then_inc(par_in, 16)
            sp.dma_start(G.rows[:, :], M.rows.partition_broadcast(P)).then_inc(par_in, 16)
            sp.dma_start(G.mats[:, :], M.mats).then_inc(par_in, 16)
            sp.wait_ge(par_in, 48)

        @block.gpsimd
        def _(pool):
            if not first:
                return
            nc.gpsimd.memset(G.ident[:, :], 0.0).then_inc(ident0, 1)
            nc.gpsimd.memset(G.identb[:, :], 0.0).then_inc(ident0, 1)
            nc.gpsimd.memset(G.mask_ij[:, :], 0.0).then_inc(ident0, 1)
            nc.gpsimd.memset(G.mask_ji[:, :], 0.0).then_inc(ident0, 1)
            for m in (G.causal01[:, :], G.far_sign[:, 0:P - REL], G.before_last[:, :], G.after_first[:, :]):
                nc.gpsimd.memset(m, 1.0).then_inc(ident0, 1)
            nc.gpsimd.memset(G.far_sign[:, P - REL:P], 0.0).then_inc(ident0, 1)
            pool.wait_ge(ident0, 9)
            for m in (G.ident, G.identb):
                nc.gpsimd.affine_select(out=m[:, :], in_=m[:, :], compare_op=ALU.not_equal, fill=1.0, base=0,
                                        pattern=[[-1, P]], channel_multiplier=1).then_inc(ident_ready, 1)
            nc.gpsimd.affine_select(out=G.mask_ij[:, :], in_=G.mask_ij[:, :], compare_op=ALU.is_ge, fill=MASKED,
                                    base=0, pattern=[[-1, P]], channel_multiplier=1).then_inc(ident_ready, 1)
            nc.gpsimd.affine_select(out=G.mask_ji[:, :], in_=G.mask_ji[:, :], compare_op=ALU.is_ge, fill=MASKED,
                                    base=0, pattern=[[1, P]], channel_multiplier=-1).then_inc(ident_ready, 1)
            nc.gpsimd.affine_select(out=G.causal01[:, :], in_=G.causal01[:, :], compare_op=ALU.is_ge, fill=0.0,
                                    base=0, pattern=[[1, P]], channel_multiplier=-1).then_inc(ident_ready, 1)
            for cols, fill in ((slice(0, P - REL), 0.0), (slice(P - REL, P), -1.0)):
                nc.gpsimd.affine_select(out=G.far_sign[:, cols], in_=G.far_sign[:, cols], compare_op=ALU.is_ge,
                                        fill=fill, base=cols.start, pattern=[[1, cols.stop - cols.start]],
                                        channel_multiplier=-1).then_inc(ident_ready, 1)
            nc.gpsimd.affine_select(out=G.before_last[:, :], in_=G.before_last[:, :], compare_op=ALU.is_gt,
                                    fill=0.0, base=0, pattern=[[-1, P]],
                                    channel_multiplier=1).then_inc(ident_ready, 1)
            nc.gpsimd.affine_select(out=G.after_first[:, :], in_=G.after_first[:, :], compare_op=ALU.is_gt,
                                    fill=0.0, base=0, pattern=[[1, P]],
                                    channel_multiplier=-1).then_inc(ident_ready, 1)

        @block.vector
        def _(dve):
            link = chained(dve, chain)
            if first:
                dve.wait_ge(x_in, 16)
            layer_norm(nc, dve, link, N, G.xt, G.xn, var_ready, std_ready, 1)
            nc.vector.memset(G.zeros[:, :], 0.0).then_inc(xn_ready, 1)
            layer_norm(nc, dve, link, N, G.xn, xnn, var_ready, std_ready, 2)
            nc.vector.memset(G.negs[:, :], 0.0).then_inc(xn_ready, 1)
            if first:
                dve.wait_ge(par_in, 48)
            for c in range(QUAD):
                dve.wait_ge(h1_turned, c + 1)
                nc.vector.tensor_scalar(G.h1T[:, c * BANK:(c + 1) * BANK], h1_ps[c % 2][:, :],
                                        G.col(gain), G.col(bias), ALU.mult, ALU.add).then_inc(h1_kept, 1)

        @block.scalar
        def _(act):
            layer_norm_root(nc, act, N, var_ready, std_ready, 1)
            layer_norm_root(nc, act, N, var_ready, std_ready, 2)
            for c in range(QUAD):
                act.wait_ge(xn_turned, c + 1)
                nc.scalar.copy(G.xnT[:, c * BANK:(c + 1) * BANK], xn_ps[c % 2][:, :]).then_inc(xn_kept, 1)

        @block.tensor
        def _(pe):
            if first:
                pe.wait_ge(ident_ready, 2)
            for src, ps, ready, turned, kept in ((G.xn, xn_ps, 1, xn_turned, xn_kept),
                                                 (xnn, h1_ps, 2, h1_turned, h1_kept)):
                pe.wait_ge(xn_ready, ready)
                for c in range(QUAD):
                    if c >= 2:
                        pe.wait_ge(kept, c - 1)
                    for k in range(QUAD):
                        last = nc.tensor.transpose(ps[c % 2][:, k * P:(k + 1) * P], src[:, c * QUAD + k, :],
                                                   G.ident[:, :])
                    last.then_inc(turned, 1)


def stage_project(nc, G, M):
    inv = 1.0 / float(np.sqrt(DK))
    with ExitStack() as ctx:
        def sb(name, shape, dt=F32):
            return ctx.enter_context(nc.sbuf_tensor(name, shape, dt))

        def sem(name):
            return ctx.enter_context(nc.semaphore(name))

        proj = sb("proj", [P, 5, T])
        rest = sb("rest", [P, T])
        pieces = sb("pieces", [P, 2, PIECES, T], BF16)
        bq_scaled = sb("bq_scaled", [P, 1])
        rel_w = sb("rel_w", [P, 2, H * NREL])
        rel_sb = sb("rel_sb", [P, 2, H, NREL])
        proj_ps = [ctx.enter_context(nc.psum_tensor(f"proj_ps{i}", [P, BANK], F32)) for i in range(2)]
        v_ps = [ctx.enter_context(nc.psum_tensor(f"v_ps{i}", [P, BANK], F32)) for i in range(2)]
        rel_ps = [ctx.enter_context(nc.psum_tensor(f"rel_ps{i}", [P, BANK], F32)) for i in range(3)]
        rel_w_in = sem("p_rel_w_in")
        rel_w_ready = sem("p_rel_w_ready")
        bias_ready = sem("p_bias_ready")
        projected = sem("p_projected")
        proj_kept = sem("p_proj_kept")
        chain = sem("p_chain")
        cut = sem("p_cut")
        pieces_stored = [sem(f"p_pieces_stored{i}") for i in range(2)]
        v_projected = sem("p_v_projected")
        v_kept = sem("p_v_kept")
        scored = sem("p_scored")
        rel_kept = sem("p_rel_kept")
        last_kept = sem("p_last_kept")
        rel_stored = [sem(f"p_rel_stored{i}") for i in range(2)]
        pad_stored = sem("p_pad_stored")
        block = ctx.enter_context(nc.Block())
        plan = [("r_q", G.xnT, 1), ("r_k", G.xnT, 2), ("c_q", G.h1T, 1), ("c_k", G.h1T, 1)]
        kept_after = [4, 12, 12, 16, 20]

        @block.sync
        def _(sp):
            sp.dma_start(rel_w[:, 0, :], M.rk_block).then_inc(rel_w_in, 16)
            sp.dma_start(rel_w[:, 1, :], M.rk_block_first).then_inc(rel_w_in, 16)
            for row in (0, (S + RPAD) * NREL):
                sp.dma_start(bass.AP(M.rel.tensor, row, [[RHEAD, BH], [1, RPAD * NREL]]),
                             G.zeros[0:BH, 0:RPAD * NREL]).then_inc(pad_stored, 16)
            def store_pieces(a):
                sp.wait_ge(cut, a + 1)
                sp.dma_start(M.split[a].rearrange("c b p s -> p c b s"),
                             pieces[:, a % 2, :, :].rearrange("p c (b s) -> p c b s", b=B)
                             ).then_inc(pieces_stored[a % 2], 16)

            store_pieces(0)
            store_pieces(1)
            for t in range(NT):
                b, tile = divmod(t, NS)
                sp.wait_ge(rel_kept, (t + 1) * len(RGROUPS))
                sp.dma_start(bass.AP(M.rel.tensor, b * H * RHEAD + (RPAD + tile * P) * NREL,
                                     [[NREL, P], [RHEAD, H], [1, NREL]]),
                             rel_sb[:, t % 2, :, :]).then_inc(rel_stored[t % 2], 16)
                if t in (1, 3, 5):
                    store_pieces(2 + t // 2)
            sp.wait_ge(pad_stored, 32)
            sp.wait_ge(pieces_stored[0], 48)
            sp.wait_ge(pieces_stored[1], 32)
            for i in range(2):
                sp.wait_ge(rel_stored[i], 16 * (NT // 2))

        @block.gpsimd
        def _(pool):
            pool.wait_ge(rel_w_in, 32)
            nc.gpsimd.tensor_tensor(rel_w[:, 0, :], rel_w[:, 0, :], rel_w[:, 1, :],
                                    ALU.subtract).then_inc(rel_w_ready, 1)
            for t in range(NT):
                pool.wait_ge(rel_kept, (t + 1) * len(RGROUPS))
                nc.gpsimd.tensor_copy(G.rel_last[:, t // NS, :, t % NS], rel_sb[:, t % 2, :, NREL - 1]
                                      ).then_inc(last_kept, 1)

        @block.scalar
        def _(act):
            nc.scalar.mul(bq_scaled[:, :], G.col("bq"), inv).then_inc(bias_ready, 1)
            act.wait_ge(bias_ready, 1)
            n = 0
            for i in range(4):
                for c in range(QUAD):
                    act.wait_ge(projected, n + 1)
                    ps, cols = proj_ps[n % 2], slice(c * BANK, (c + 1) * BANK)
                    n += 1
                    if i == 0:
                        nc.scalar.activation(proj[:, 0, cols], ps[:, :], ACT.Identity, scale=inv
                                             ).then_inc(proj_kept, 1)
                    elif i == 1:
                        nc.scalar.activation(proj[:, 1, cols], ps[:, :], ACT.Identity,
                                             bias=G.col("rk_first")).then_inc(proj_kept, 1)
                        nc.scalar.activation(proj[:, 2, cols], ps[:, :], ACT.Identity,
                                             bias=G.col("rk_last")).then_inc(proj_kept, 1)
                    elif i == 2:
                        nc.scalar.activation(proj[:, 3, cols], ps[:, :], ACT.Identity, bias=bq_scaled[:, :],
                                             scale=inv).then_inc(proj_kept, 1)
                    else:
                        nc.scalar.activation(proj[:, 4, cols], ps[:, :], ACT.Identity,
                                             bias=G.col("bk")).then_inc(proj_kept, 1)
            for t in range(NT):
                if t >= 2:
                    act.wait_ge(rel_stored[t % 2], 16 * (t // 2))
                    act.wait_ge(last_kept, t - 1)
                for g, (h0, h1) in enumerate(RGROUPS):
                    act.wait_ge(scored, t * len(RGROUPS) + g + 1)
                    nc.scalar.copy(rel_sb[:, t % 2, h0:h1, :],
                                   rel_ps[g][:, 0:(h1 - h0) * NREL].rearrange("p (h r) -> p h r", r=NREL)
                                   ).then_inc(rel_kept, 1)

        @block.vector
        def _(dve):
            link = chained(dve, chain)
            for a in range(5):
                dve.wait_ge(proj_kept, kept_after[a])
                if a >= 2:
                    dve.wait_ge(pieces_stored[a % 2], 16 * (a // 2))
                src, hi, mid, lo = proj[:, a, :], *(pieces[:, a % 2, i, :] for i in range(PIECES))
                link(nc.vector.tensor_copy(hi, src))
                link(nc.vector.tensor_tensor(rest[:, :], src, hi, ALU.subtract))
                link(nc.vector.tensor_copy(mid, rest[:, :]))
                nc.vector.tensor_tensor(lo, rest[:, :], mid, ALU.subtract).then_inc(cut, 1)
                dve.wait_ge(cut, a + 1)
            for t in range(NT):
                b, tile = divmod(t, NS)
                heads = slice(b * H, (b + 1) * H)
                dve.wait_ge(v_projected, t + 1)
                v_rel = v_ps[t % 2][:, 0:D].rearrange("p (h d) -> p h d", d=DK)
                v_causal = v_ps[t % 2][:, D:2 * D].rearrange("p (h d) -> p h d", d=DK)
                nc.vector.tensor_tensor(G.v_rel[:, heads, tile, :], v_rel,
                                        G.row("rv_first").rearrange("p (h d) -> p h d", d=DK), ALU.add)
                nc.vector.tensor_tensor(G.v_causal[:, heads, tile, :], v_causal,
                                        G.row("bv").rearrange("p (h d) -> p h d", d=DK), ALU.add).then_inc(v_kept, 1)

        @block.tensor
        def _(pe):
            n = 0
            for name, src, _copies in plan:
                for c in range(QUAD):
                    if n >= 2:
                        pe.wait_ge(proj_kept, [1, 2, 3, 4, 6, 8, 10, 12, 13, 14, 15, 16, 17, 18, 19, 20][n - 2])
                    nc.tensor.matmul(proj_ps[n % 2][:, :], G.mat(name), src[:, c * BANK:(c + 1) * BANK],
                                     start=True, stop=True).then_inc(projected, 1)
                    n += 1
            def values(t):
                if t >= 2:
                    pe.wait_ge(v_kept, t - 1)
                nc.tensor.matmul(v_ps[t % 2][:, 0:D], G.xnT[:, t * P:(t + 1) * P], G.mat("r_v"),
                                 start=True, stop=True)
                nc.tensor.matmul(v_ps[t % 2][:, D:2 * D], G.h1T[:, t * P:(t + 1) * P], G.mat("c_v"),
                                 start=True, stop=True).then_inc(v_projected, 1)

            pe.wait_ge(rel_w_ready, 1)
            for t in range(NT):
                for g, (h0, h1) in enumerate(RGROUPS):
                    if t >= 1:
                        pe.wait_ge(rel_kept, (t - 1) * len(RGROUPS) + g + 1)
                    nc.tensor.matmul(rel_ps[g][:, 0:(h1 - h0) * NREL], proj[:, 0, t * P:(t + 1) * P],
                                     rel_w[:, 0, h0 * NREL:h1 * NREL], start=True, stop=True).then_inc(scored, 1)
                if t >= NT // 2:
                    values(2 * t - NT)
                    values(2 * t - NT + 1)


def await_count(eng, sem, value):
    if not isinstance(value, int) or value > 0:
        eng.wait_ge(sem, value)


def clear_semaphores(nc, numbers):
    with nc.Block() as block:
        @block.sync
        def _(sp):
            sp.sem_clear(numbers)


def over_heads(eng, head):
    for u in range(RING):
        head(u, 0, u, u)
    with eng.Fori(1, BH // RING - 1) as k:
        for u in range(RING):
            head(k * RING + u, k, u, RING + u)
    last = BH // RING - 1
    for u in range(RING):
        head(last * RING + u, last, u, last * RING + u)


def stage_attention(nc, G, M, relative):
    tag = "r" if relative else "c"
    q_array, k_arrays = (0, (1, 2)) if relative else (3, (4,))
    NK = len(k_arrays)
    LOADS = 3 * (1 + NK)
    VUSED = VCOLS if relative else DK + 1
    halves = [(i, hf, hf * BANK, min((hf + 1) * BANK, S if relative else (i + 1) * P))
              for i in range(NS) for hf in range(2) if relative or hf * BANK < (i + 1) * P]
    NA = len(halves)
    share = [2, 2, 2, 2, 2, 2, 2, 2] if relative else [2, 2, 2, 1, 1, 1, 2, 1]
    SPLIT = 4 if relative else 1
    EARLY = sum(share[SPLIT:])
    beside = [list(range(EARLY + sum(share[:j]), EARLY + sum(share[:j + 1]))) for j in range(SPLIT)]
    beside += [list(range(sum(share[SPLIT:j]), sum(share[SPLIT:j + 1]))) for j in range(SPLIT, NS)]
    assert sum(share) == NA
    A_BANKS = 2 if relative else 3
    MAX_AT = 6 if relative else 3
    STEPS_AFTER = ((1,), (2,), (3,), (4,)) if relative else ((1, 2), (3, 4))
    FIRST_TURNS = NA + EARLY + 1
    PER_HEAD = NA + 2

    def items(at):
        for j in range(NS):
            ahead = 1 if j < SPLIT else 2
            row = [("piece", x, ahead) for x in beside[j] if at + ahead < BH]
            row += [("sums", 0, -1)] if j == 2 and at >= 1 else []
            row += [("max", 0, 1)] if j == MAX_AT and at + 1 < BH else []
            yield row

    def turns(n, at):
        first = FIRST_TURNS - (1 if at >= 1 else 0) - (EARLY if at == BH - 1 else 0)
        before = sum(len(row) for row in items(at - 1)) if at else FIRST_TURNS
        out, i = [], 0
        for row in items(at):
            out.append([])
            for item in row:
                back = A_BANKS if i >= A_BANKS else i + 1 + (before - 1 - i) % A_BANKS
                out[-1].append((*item, n * PER_HEAD + first + i, i % A_BANKS,
                                n * PER_HEAD + first + i - back + 1))
                i += 1
        return out

    LAST_TURN = turns(BH - 1, BH - 1)[2][-1][3] + 1

    with ExitStack() as ctx:
        def sb(name, shape, dt=F32):
            return ctx.enter_context(nc.sbuf_tensor(f"{tag}_{name}", shape, dt))

        def sem(name):
            return ctx.enter_context(nc.semaphore(f"{tag}_{name}"))

        q = sb("q", [SROWS, RING, S], BF16)
        ks = sb("ks", [SROWS, RING, NK, S], BF16)
        vs = sb("vs", [P, RING, NS, 32])
        probs = sb("probs", [P, NS, S])
        half_max = sb("half_max", [P, 2, NS, 2])
        row_max = sb("row_max", [P, NS])
        neg_rest = sb("neg_rest", [P, NS])
        neg_max = sb("neg_max", [P, PIECES, NS], BF16)
        neg_maxT = sb("neg_maxT", [PIECES * NS, 2, P], BF16)
        a_ps = [ctx.enter_context(nc.psum_tensor(f"{tag}_a_ps{i}", [P, BANK], F32))
                for i in range(A_BANKS)]
        b_ps = [ctx.enter_context(nc.psum_tensor(f"{tag}_b_ps{i}", [P, S], F32)) for i in range(2)]
        sumT = sb("sumT", [P, 2, P])
        o_ps = ctx.enter_context(nc.psum_tensor(f"{tag}_o_ps", [P, 2, P], F32))
        if relative:
            rel = sb("rel", [P, RING, NS, WIN])
            win_ps = ctx.enter_context(nc.psum_tensor(f"{tag}_win_ps", [P, 2, WIN], F32))
            rel_edge = sb("rel_edge", [P, RING, NS])
            win_sb = sb("win_sb", [P, 2, NS, WIN])
            far_sb = sb("far_sb", [P, NS, P])
        loaded = [sem(f"loaded{i}") for i in range(RING)]
        max_in = [sem(f"max_in{i}") for i in range(RING)]
        rows_ready = sem("rows_ready")
        late_rows_ready = sem("late_rows_ready")
        columns_ready = sem("columns_ready")
        values_ready = sem("values_ready")
        rel_loaded = [sem(f"rel_loaded{i}") for i in range(RING)] if relative else []
        rel_ready = sem("rel_ready")
        pool_chain = sem("pool_chain")
        chain = sem("chain")
        a_scored = sem("a_scored")
        a_used = sem("a_used")
        b_scored = sem("b_scored")
        exp_done = sem("exp_done")
        pv_done = sem("pv_done")
        sum_kept = sem("sum_kept")
        floor_ready = sem("floor_ready")
        win_kept = sem("win_kept")
        win_stored = [sem(f"win_stored{i}") for i in range(2)]
        far_masked = sem("far_masked")
        far_summed = sem("far_summed")
        block = ctx.enter_context(nc.Block())
        SRCROW, SRCPIECE = S, B * P * S

        @block.sync
        def _(sp):
            def load(n, u):
                def rows(array, piece, step, count):
                    return bass.AP(M.split.tensor, array * PIECES * SRCPIECE + piece * SRCPIECE + n * (DK * S),
                                   [[step, count], [SRCROW, DK], [1, S]])
                if relative:
                    sp.dma_start(rel[:, u, :, :],
                                 bass.AP(M.rel.tensor, n * RHEAD + RPAD * NREL,
                                         [[NREL - 1, P], [P * NREL, NS], [1, WIN]])).then_inc(rel_loaded[u], 16)
                for piece, r, reps in ((0, 0, 3), (1, 3 * DK, 2), (2, 5 * DK, 1)):
                    sp.dma_start(q[r:r + reps * DK, u, :], rows(q_array, 0, SRCPIECE, reps)).then_inc(loaded[u], 16)
                    for i, array in enumerate(k_arrays):
                        sp.dma_start(ks[r:r + reps * DK, u, i, :], rows(array, piece, 0, reps)
                                     ).then_inc(loaded[u], 16)

            def maxima(n, u, turn):
                sp.wait_ge(a_used, turn + 1)
                sp.dma_start(q[AROWS:SROWS, u, :], neg_maxT[:, u % 2, :]).then_inc(max_in[u], 16)

            def store_window(n, u):
                sp.wait_ge(win_kept, n * 4 + 4)
                sp.dma_start(bass.AP(M.window.tensor, n * (S * WIN), [[WIN, P], [P * WIN, NS], [1, WIN]]),
                             win_sb[:, u % 2, :, :]).then_inc(win_stored[u % 2], 16)

            def head(n, k, u, at):
                if at + 3 < BH:
                    if at >= 1:
                        sp.wait_ge(pv_done, n * NS)
                    load(n + 3, (u + 3) % RING)
                if relative and at >= 1:
                    store_window(n - 1, (u - 1) % RING)
                if at + 1 < BH:
                    turn = [item[3] for row in turns(n, at) for item in row if item[0] == "max"][0]
                    maxima(n + 1, (u + 1) % RING, turn)

            for n in range(3):
                sp.wait_ge(rows_ready, 2 * n + 2 if n < 2 else RING + 2)
                if n == 2:
                    sp.wait_ge(late_rows_ready, 2)
                load(n, n)
            maxima(0, 0, FIRST_TURNS - 1)
            over_heads(sp, head)
            if relative:
                store_window(BH - 1, RING - 1)
                for i in range(2):
                    sp.wait_ge(win_stored[i], 16 * (BH // 2))

        @block.gpsimd
        def _(pool):
            for u in range(2, RING):
                nc.gpsimd.memset(ks[:, u, :, :], 1.0).then_inc(late_rows_ready, 1)
            pool.wait_ge(late_rows_ready, 2)
            nc.gpsimd.memset(vs[:, :, :, :], 0.0).then_inc(columns_ready, 1)
            pool.wait_ge(columns_ready, 1)
            nc.gpsimd.memset(vs[:, :, :, DK:VUSED], 1.0).then_inc(columns_ready, 1)
            pool.wait_ge(columns_ready, 2)
            if relative:
                for u in range(RING):
                    nc.gpsimd.affine_select(out=vs[:, u, :, DK + 1:VCOLS], in_=vs[:, u, :, DK + 1:VCOLS],
                                            compare_op=ALU.is_ge, fill=0.0, base=-P,
                                            pattern=[[P, NS], [-P, NS]], channel_multiplier=1
                                            ).then_inc(columns_ready, 1)
                pool.wait_ge(columns_ready, 2 + RING)

            def prepare(n, k, u, at):
                link = chained(pool, pool_chain, n * 4)
                if at >= RING:
                    pool.wait_ge(pv_done, (n - RING + 1) * NS)
                values = G.v_rel if relative else G.v_causal
                nc.gpsimd.tensor_copy(vs[:, u, :, 0:DK], values[:, :, :, :].rearrange("p n j d -> p (n j d)")[
                    :, bass.ds(n * (NS * DK), NS * DK)].rearrange("p (j d) -> p j d", d=DK)
                                      ).then_inc(values_ready, 1)
                if not relative:
                    return
                link(nc.gpsimd.tensor_copy(rel_edge[:, u, :], G.rel_last[:, :, :, :].rearrange(
                    "p b h t -> p (b h t)")[:, bass.ds(n * NS, NS)]))
                pool.wait_ge(rel_loaded[u], 16 * (k + 1))
                edge = rel_edge[:, u, :].unsqueeze(2)
                link(nc.gpsimd.tensor_tensor(rel[:, u, :, 2 * REL:WIN], rel[:, u, :, 2 * REL:WIN],
                                             edge.to_broadcast([P, NS, P]), ALU.subtract))
                link(nc.gpsimd.tensor_tensor(rel[:, u, :, 2 * REL:WIN], rel[:, u, :, 2 * REL:WIN],
                                             G.before_last[:, :].unsqueeze(1).to_broadcast([P, NS, P]),
                                             ALU.mult))
                link(nc.gpsimd.tensor_tensor(rel[:, u, :, 2 * REL:REL + P], rel[:, u, :, 2 * REL:REL + P],
                                             edge.to_broadcast([P, NS, P - REL]), ALU.add))
                nc.gpsimd.tensor_tensor(rel[:, u, :, 0:P], rel[:, u, :, 0:P],
                                        G.after_first[:, :].unsqueeze(1).to_broadcast([P, NS, P]),
                                        ALU.mult).then_inc(rel_ready, 1)
                assert link.done[0] == 4

            def mask_far(n, u, at):
                pool.wait_ge(win_kept, n * 4 + 4)
                if at >= 1:
                    pool.wait_ge(far_summed, n)
                nc.gpsimd.tensor_tensor(far_sb[:, :, :], win_sb[:, u % 2, :, 2 * REL:WIN],
                                        G.far_sign[:, :].unsqueeze(1).to_broadcast([P, NS, P]), ALU.mult
                                        ).then_inc(far_masked, 1)

            def head(n, k, u, at):
                if relative and at >= 1:
                    mask_far(n - 1, (u - 1) % RING, at - 1)
                if at + 3 < BH:
                    prepare(n + 3, k + (u + 3) // RING, (u + 3) % RING, at + 3)

            for n in range(3):
                prepare(n, 0, n, n)
            over_heads(pool, head)
            if relative:
                mask_far(BH - 1, RING - 1, BH - 1)

        @block.scalar
        def _(act):
            def keep_window(n, k, u, at, pair):
                act.wait_ge(pv_done, n * NS + min(2 * pair + 3, NS))
                if pair == 0 and at >= 2:
                    act.wait_ge(win_stored[u % 2], k * 32 + 16 * (u // 2))
                    act.wait_ge(far_masked, n - 1)
                nc.scalar.copy(win_sb[:, u % 2, 2 * pair:2 * pair + 2, :],
                               win_ps[:, :, :]).then_inc(win_kept, 1)

            def keep_sums(n):
                act.wait_ge(pv_done, n * NS + NS)
                nc.scalar.copy(sumT[:, :, :], o_ps[:, :, :]).then_inc(sum_kept, 1)

            def last_head(n, k, u, at):
                if relative:
                    keep_window(n, k, u, at, 3)
                keep_sums(n)

            def head(n, k, u, at):
                for j in range(NS):
                    act.wait_ge(b_scored, n * NS + j + 1)
                    if at >= 1:
                        act.wait_ge(pv_done, (n - 1) * NS + (min(j + 3, NS) if relative else j + 1))
                    lo = 0 if relative else j * P
                    nc.scalar.activation(probs[:, j, lo:S], b_ps[j % 2][:, lo:S], ACT.Exp).then_inc(exp_done, 1)
                    if relative and j in (3, 5, 7):
                        keep_window(n, k, u, at, (j - 3) // 2)
                    if j == 0 and at >= 1:
                        last_head(n - 1, k - 1 if u == 0 else k, (u - 1) % RING, at - 1)

            over_heads(act, head)
            last_head(BH - 1, BH // RING - 1, RING - 1, BH - 1)

        @block.vector
        def _(dve):
            def max_piece(u, x, turn, bank):
                i, hf, lo, hi = halves[x]
                dve.wait_ge(a_scored, turn + 1)
                nc.vector.tensor_reduce(half_max[:, u % 2, i, hf:hf + 1], a_ps[bank][:, 0:hi - lo], AX.X,
                                        ALU.max).then_inc(a_used, 1)

            def negate_max(n, u, step):
                if step:
                    dve.wait_ge(chain, n * 5 + step)
                if step == 0:
                    out = nc.vector.tensor_tensor(row_max[:, :], half_max[:, u % 2, :, 0], half_max[:, u % 2, :, 1], ALU.max)
                elif step == 1:
                    out = nc.vector.tensor_scalar(neg_max[:, 0, :], row_max[:, :], -1.0, None, ALU.mult)
                elif step == 2:
                    out = nc.vector.scalar_tensor_tensor(neg_rest[:, :], row_max[:, :], -1.0, neg_max[:, 0, :],
                                                         ALU.mult, ALU.subtract)
                elif step == 3:
                    out = nc.vector.tensor_copy(neg_max[:, 1, :], neg_rest[:, :])
                else:
                    out = nc.vector.tensor_tensor(neg_max[:, 2, :], neg_rest[:, :], neg_max[:, 1, :],
                                                  ALU.subtract)
                out.then_inc(chain, 1)

            def negate_after_piece(n, u, x):
                for step in STEPS_AFTER[x] if x < len(STEPS_AFTER) else ():
                    negate_max(n, u, step)

            def keep_turned(k, u, at, turn, bank):
                dve.wait_ge(a_scored, turn + 1)
                if at >= 2:
                    dve.wait_ge(max_in[(u + 2) % RING], 16 * k + (16 if u >= 2 else 0))
                nc.vector.tensor_copy(neg_maxT[:, u % 2, :], a_ps[bank][0:PIECES * NS, 0:P // 2].bitcast(
                    BF16)).then_inc(a_used, 1)

            def keep_out(n, turn, bank):
                dve.wait_ge(a_scored, turn + 1)
                att, w = (G.att, VCOLS) if relative else (G.catt, DK + 1)
                nc.vector.tensor_copy(
                    att[:, :, :, :].rearrange("p n t d -> p (n t d)")[:, bass.ds(n * (NS * w), NS * w)].rearrange(
                        "p (c h d) -> p c h d", c=NS // 2, h=2),
                    a_ps[bank][:, 0:2 * P].rearrange("p (h c d) -> p c h d", h=2, d=32)[:, :, :, 0:w]
                    ).then_inc(a_used, 1)

            def sum_far(n):
                dve.wait_ge(far_masked, n + 1)
                nc.vector.tensor_reduce(G.far[:, :, :].rearrange("p n t -> p (n t)")[:, bass.ds(n * NS, NS)],
                                        far_sb[:, :, :], AX.X, ALU.add).then_inc(far_summed, 1)

            def head(n, k, u, at):
                for j, row in enumerate(turns(n, at)):
                    for kind, x, ahead, turn, bank, free in row:
                        if kind == "piece":
                            max_piece(u + ahead, x, turn, bank)
                            if ahead == 2:
                                negate_after_piece(n + 1, u + 1, x)
                        elif kind == "sums":
                            keep_out(n - 1, turn, bank)
                        else:
                            keep_turned(k + (u + 1) // RING, (u + 1) % RING, at + 1, turn, bank)
                    if j == SPLIT - 1 and at + 1 < BH:
                        dve.wait_ge(a_used, row[-1][3] + 1)
                        negate_max(n + 1, u + 1, 0)
                        if at + 2 == BH:
                            for step in range(1, 5):
                                negate_max(n + 1, u + 1, step)
                    if relative and j == 4 and at >= 1:
                        sum_far(n - 1)

            for u in range(RING):
                nc.vector.memset(q[:, u, :], 0.0).then_inc(rows_ready, 1)
                if u < 2:
                    nc.vector.memset(ks[:, u, :, :], 1.0).then_inc(rows_ready, 1)
            if not relative:
                nc.vector.memset(half_max[:, :, :, 1], -3e38).then_inc(floor_ready, 1)
                dve.wait_ge(floor_ready, 1)
            for x in range(NA):
                max_piece(0, x, x, x % A_BANKS)
            dve.wait_ge(a_used, NA)
            negate_max(0, 0, 0)
            for x in range(EARLY):
                max_piece(1, x, NA + x, (NA + x) % A_BANKS)
                negate_after_piece(0, 0, x)
            keep_turned(0, 0, 0, FIRST_TURNS - 1, (FIRST_TURNS - 1) % A_BANKS)
            over_heads(dve, head)
            keep_out(BH - 1, LAST_TURN, 0)
            if relative:
                sum_far(BH - 1)

        @block.tensor
        def _(pe):
            def score_piece(u, x, bank, free):
                i, hf, lo, hi = halves[x]
                ps = a_ps[bank]
                await_count(pe, a_used, free)
                lhs = q[0:AROWS, u, i * P:(i + 1) * P]
                if relative:
                    mid = (i + 1) * P
                    parts = [(0, lo, min(hi, mid)), (1, max(lo, mid), hi)]
                else:
                    parts = [(0, lo, hi)]
                parts = [p for p in parts if p[1] < p[2]]
                for m, (kind, a, b) in enumerate(parts):
                    last = nc.tensor.matmul(ps[:, a - lo:b - lo], lhs, ks[0:AROWS, u, kind, a:b], start=(m == 0),
                                            stop=False, skip_group_check=True)
                if relative:
                    a, b = max(lo, i * P - REL), min(hi, i * P + P + REL)
                    if a < b:
                        w = a - (i * P - REL)
                        last = nc.tensor.matmul(ps[:, a - lo:b - lo], G.ident[:, :], rel[:, u, i, w:w + b - a],
                                                start=False, stop=True, skip_group_check=True)
                elif lo <= i * P < hi:
                    last = nc.tensor.matmul(ps[:, i * P - lo:(i + 1) * P - lo], G.identb[:, :], G.mask_ij[:, :],
                                            start=False, stop=True, skip_group_check=True)
                last.then_inc(a_scored, 1)

            def begin_a(n, k, u):
                pe.wait_ge(loaded[u], 16 * LOADS * (k + 1))
                if relative:
                    pe.wait_ge(rel_ready, n + 1)

            def turn_max(n, bank, free):
                pe.wait_ge(chain, n * 5 + 5)
                pe.wait_ge(a_used, free)
                nc.tensor.transpose(a_ps[bank][0:PIECES * NS, 0:P // 2].bitcast(BF16),
                                    neg_max[:, :, :].rearrange("p c t -> p (c t)"), G.identb[:, :]
                                    ).then_inc(a_scored, 1)

            def score_keys(n, k, u, at, j):
                ps = b_ps[j % 2]
                await_count(pe, exp_done, n * NS + j - 1)
                if relative:
                    parts = [(1, 0, j * P), (0, j * P, S)]
                else:
                    parts = [(0, j * P, S)]
                cuts = [(kind, max(a, c), min(b, c + BANK), c) for c in (0, BANK) for kind, a, b in parts
                        if max(a, c) < min(b, c + BANK)]
                seen = set()
                for kind, a, b, c in cuts:
                    last = nc.tensor.matmul(ps[:, a:b], ks[0:SROWS, u, kind, j * P:(j + 1) * P],
                                            q[0:SROWS, u, a:b], start=(c not in seen), stop=False,
                                            skip_group_check=True)
                    seen.add(c)
                if relative:
                    for i, w, rows, a, b in ((j, REL, slice(0, P), 0, P), (j + 1, 0, slice(P - REL, P), 0, REL),
                                             (j - 1, REL + P, slice(0, REL), P - REL, P)):
                        if 0 <= i < NS:
                            last = nc.tensor.matmul(ps[rows, i * P + a:i * P + b],
                                                    rel[:, u, i, w:w + rows.stop - rows.start], G.ident[:, a:b],
                                                    start=False, stop=True, skip_group_check=True)
                else:
                    last = nc.tensor.matmul(ps[:, j * P:(j + 1) * P], G.identb[:, :], G.mask_ji[:, :],
                                            start=False, stop=True, skip_group_check=True)
                last.then_inc(b_scored, 1)

            def weigh_values(n, u, j):
                pe.wait_ge(exp_done, n * NS + j + 1)
                if j == 0:
                    pe.wait_ge(values_ready, n + 1)
                    await_count(pe, sum_kept, n)
                for c in range(0 if relative else j // 2, NS // 2):
                    a, b = max(2 * c * P, 0 if relative else j * P), 2 * (c + 1) * P
                    last = nc.tensor.matmul(o_ps[32 * c:32 * (c + 1), :, :].rearrange("p h q -> p (h q)")[
                        :, a - 2 * c * P:2 * P], vs[:, u, j, :], probs[:, j, a:b], start=(j == 0),
                                            stop=(j == (NS - 1 if relative else 2 * c + 1)), skip_group_check=True)
                return last

            def turn_sums(n, bank, free):
                pe.wait_ge(sum_kept, n + 1)
                pe.wait_ge(a_used, free)
                for h in range(2):
                    last = nc.tensor.transpose(a_ps[bank][:, h * P:(h + 1) * P], sumT[:, h, :], G.ident[:, :])
                last.then_inc(a_scored, 1)

            def turn_window(n, i):
                if i % 2 == 0:
                    await_count(pe, win_kept, n * 4 + i // 2)
                last = nc.tensor.transpose(win_ps[:, i % 2, REL:REL + P], probs[:, i, i * P:(i + 1) * P],
                                           G.ident[:, :])
                for side, a, b, w, keys in ((i - 1, 0, REL, 0, slice(P - REL, P)),
                                            (i + 1, P - REL, P, REL + P, slice(0, REL))):
                    if 0 <= side < NS:
                        data, pick = probs[:, side, i * P + a:i * P + b], G.ident[:, keys]
                    else:
                        data, pick = G.ident[:, a:b], G.zeros[:, 0:REL]
                    last = nc.tensor.matmul(win_ps[a:b, i % 2, w:w + REL], data, pick, start=True, stop=True,
                                            skip_group_check=True)
                return last

            def use_keys(n, u, j):
                last = weigh_values(n, u, j)
                if relative:
                    for i in ([j - 1] if j else []) + ([j] if j == NS - 1 else []):
                        last = turn_window(n, i)
                last.then_inc(pv_done, 1)

            def last_keys(n, u, at, j):
                if j >= 1:
                    use_keys(n, u, j - 1)
                elif at >= 1:
                    use_keys(n - 1, (u - 1) % RING, NS - 1)

            def head(n, k, u, at):
                pe.wait_ge(max_in[u], 16 * (k + 1))
                for j, row in enumerate(turns(n, at)):
                    score_keys(n, k, u, at, j)
                    if j == SPLIT and at + 2 < BH:
                        begin_a(n + 2, k + (u + 2) // RING, (u + 2) % RING)
                    for m, (kind, x, ahead, turn, bank, free) in enumerate(row):
                        if relative and m == 1:
                            last_keys(n, u, at, j)
                        if kind == "piece":
                            score_piece((u + ahead) % RING, x, bank, free)
                        elif kind == "sums":
                            turn_sums(n - 1, bank, free)
                        else:
                            turn_max(n + 1, bank, free)
                    if not relative or len(row) < 2:
                        last_keys(n, u, at, j)

            pe.wait_ge(rows_ready, RING + 2)
            pe.wait_ge(late_rows_ready, 2)
            pe.wait_ge(columns_ready, 2 + (RING if relative else 0))
            if relative:
                nc.tensor.matmul(win_ps[:, :, :].rearrange("p i w -> p (i w)"), G.ident[:, :], G.zeros[
                    :, 0:1].to_broadcast([P, 2 * WIN]), start=True, stop=True)
            begin_a(0, 0, 0)
            for x in range(NA):
                score_piece(0, x, x % A_BANKS, x - A_BANKS + 1)
            begin_a(1, 0, 1)
            for x in range(EARLY):
                score_piece(1, x, (NA + x) % A_BANKS, NA + x - A_BANKS + 1)
            turn_max(0, (FIRST_TURNS - 1) % A_BANKS, FIRST_TURNS - A_BANKS)
            for _ in range(WARM):
                nc.tensor.matmul(b_ps[0][:, 0:BANK], G.ident[:, :], (G.v_rel if relative else G.v_causal)[
                    :, 0:BANK // (NS * DK), :, :].rearrange("p n j d -> p (n j d)"), start=True, stop=True)
            over_heads(pe, head)
            use_keys(BH - 1, RING - 1, NS - 1)
            turn_sums(BH - 1, 0, LAST_TURN)


def stage_combine(nc, G, M):
    with ExitStack() as ctx:
        def sb(name, shape, dt=F32):
            return ctx.enter_context(nc.sbuf_tensor(f"o_{name}", shape, dt))

        def sem(name):
            return ctx.enter_context(nc.semaphore(f"o_{name}"))

        def ps(name, shape):
            return ctx.enter_context(nc.psum_tensor(f"o_{name}", shape, F32))

        rv_w = sb("rv_w", [P, 2, RCH, D])
        by_rel = sb("by_rel", [P, 2, H, NREL])
        by_relT = sb("by_relT", [P, 2, RCH, P])
        inv_r = sb("inv_r", [P, BH, NS])
        inv_c = sb("inv_c", [P, BH, NS])
        yc = sb("yc", [P, NT, D])
        yr = sb("yr", [P, 2, D])
        yT = sb("yT", [P, 2, 2, P])
        plus = sb("plus", [P, 2, D])
        turn_ps = [ps(f"turn_ps{i}", [P, 3, P]) for i in range(3)]
        mix_ps = ps("mix_ps", [P, D])
        yT_ps = [ps(f"yT_ps{i}", [P, 2, P]) for i in range(2)]
        out_ps = [ps(f"out_ps{i}", [P, 2, D]) for i in range(2)]
        rv_in = sem("rv_in")
        rv_ready = sem("rv_ready")
        by_rel_in = [sem(f"by_rel_in{i}") for i in range(2)]
        far_placed = sem("far_placed")
        turned = sem("turned")
        turn_kept = sem("turn_kept")
        mixed = sem("mixed")
        chain = sem("chain")
        inverted = sem("inverted")
        y_ready = sem("y_ready")
        y_turned = sem("y_turned")
        yT_kept = sem("yT_kept")
        out_done = sem("out_done")
        out_kept = sem("out_kept")
        block = ctx.enter_context(nc.Block())

        @block.sync
        def _(sp):
            sp.dma_start(rv_w[:, 0, :, :], M.rv_block.rearrange("p (c d) -> p c d", d=D)).then_inc(rv_in, 16)
            sp.dma_start(rv_w[:, 1, :, :], M.rv_block_first.rearrange("p (c d) -> p c d", d=D)).then_inc(rv_in, 16)
            for t in range(NT):
                b, tile = divmod(t, NS)
                if t >= 2:
                    sp.wait_ge(turned, t - 1)
                sp.dma_start(by_rel[:, t % 2, :, 0:NREL - 1],
                             bass.AP(M.window.tensor, b * H * S * WIN + tile * P * WIN,
                                     [[WIN + 1, P], [S * WIN, H], [1, NREL - 1]])).then_inc(by_rel_in[t % 2], 16)

        @block.gpsimd
        def _(pool):
            pool.wait_ge(rv_in, 32)
            nc.gpsimd.tensor_tensor(rv_w[:, 0, :, :], rv_w[:, 0, :, :], rv_w[:, 1, :, :],
                                    ALU.subtract).then_inc(rv_ready, 1)
            for t in range(NT):
                b, tile = divmod(t, NS)
                if t >= 2:
                    pool.wait_ge(turned, t - 1)
                heads = slice(b * H, (b + 1) * H)
                nc.gpsimd.tensor_tensor(by_rel[:, t % 2, :, NREL - 1], G.far[:, heads, tile],
                                        G.att[:, heads, tile, DK + 1 + tile], ALU.add).then_inc(far_placed, 1)

        @block.scalar
        def _(act):
            for t in range(NT + 2):
                if t < NT:
                    act.wait_ge(turned, t + 1)
                    if t >= 2:
                        act.wait_ge(mixed, t - 1)
                    for g in range(3):
                        rows = P if g < 2 else P
                        last = nc.scalar.copy(by_relT[0:rows, t % 2, 3 * g:3 * g + 3, :], turn_ps[g][0:rows, :, :])
                    last.then_inc(turn_kept, 1)
                if t >= 2:
                    act.wait_ge(y_turned, t - 1)
                    if t >= 4:
                        act.wait_ge(out_done, t - 3)
                    nc.scalar.copy(yT[:, t % 2, :, :], yT_ps[t % 2][:, :, :]).then_inc(yT_kept, 1)

        @block.vector
        def _(dve):
            link = chained(dve, chain)
            nc.vector.reciprocal(inv_r[:, :, :], G.att[:, :, :, DK])
            link(nc.vector.reciprocal(inv_c[:, :, :], G.catt[:, :, :, DK]))
            for b in range(B):
                heads = slice(b * H, (b + 1) * H)
                last = nc.vector.tensor_tensor(
                    yc[:, b * NS:(b + 1) * NS, :].rearrange("p t (h d) -> p h t d", d=DK), G.catt[:, heads, :, 0:DK],
                    inv_c[:, heads, :].unsqueeze(3).to_broadcast([P, H, NS, DK]), ALU.mult)
            link(last)
            for t in range(NT + 3):
                if t < NT:
                    b, tile = divmod(t, NS)
                    heads = slice(b * H, (b + 1) * H)
                    dve.wait_ge(mixed, t + 1)
                    if t >= 2:
                        dve.wait_ge(y_turned, t - 1)
                    y = yr[:, t % 2, :].rearrange("p (h d) -> p h d", d=DK)
                    link(nc.vector.tensor_tensor(y, mix_ps[:, :].rearrange("p (h d) -> p h d", d=DK),
                                                 G.att[:, heads, tile, 0:DK], ALU.add))
                    nc.vector.tensor_tensor(y, y, inv_r[:, heads, tile].unsqueeze(2).to_broadcast([P, H, DK]),
                                            ALU.mult).then_inc(y_ready, 1)
                if t >= 3:
                    s = t - 3
                    dve.wait_ge(out_done, s + 1)
                    nc.vector.tensor_tensor(G.mixer[:, s, :], out_ps[s % 2][:, 0, :], G.row("b_o"), ALU.add)
                    link(nc.vector.tensor_tensor(plus[:, s % 2, :], out_ps[s % 2][:, 1, :], G.row("bp"), ALU.add))
                    nc.vector.tensor_tensor(G.x2[:, s, :], plus[:, s % 2, :], G.xn[:, s, :], ALU.add
                                            ).then_inc(out_kept, 1)

        @block.tensor
        def _(pe):
            def turn(t):
                pe.wait_ge(by_rel_in[t % 2], 16 * (t // 2 + 1))
                pe.wait_ge(far_placed, t + 1)
                if t:
                    pe.wait_ge(turn_kept, t)
                flat = by_rel[:, t % 2, :, :].rearrange("p h r -> p (h r)")
                for c in range(RCH):
                    rows = min(P, H * NREL - c * P)
                    if rows < P:
                        nc.tensor.transpose(turn_ps[c // 3][:, c % 3, :], G.zeros[:, 0:P], G.ident[:, :])
                    last = nc.tensor.transpose(turn_ps[c // 3][0:rows, c % 3, :], flat[:, c * P:c * P + rows],
                                               G.ident[:, :])
                last.then_inc(turned, 1)

            def mix(t):
                pe.wait_ge(turn_kept, t + 1)
                if t == 0:
                    pe.wait_ge(rv_ready, 1)
                else:
                    pe.wait_ge(y_ready, t)
                for c in range(RCH):
                    last = nc.tensor.matmul(mix_ps[:, :], by_relT[:, t % 2, c, :], rv_w[:, 0, c, :],
                                            start=(c == 0), stop=(c == RCH - 1))
                last.then_inc(mixed, 1)

            def turn_y(t):
                pe.wait_ge(y_ready, t + 1)
                if t >= 2:
                    pe.wait_ge(yT_kept, t - 1)
                nc.tensor.transpose(yT_ps[t % 2][:, 0, :], yr[:, t % 2, :], G.ident[:, :])
                nc.tensor.transpose(yT_ps[t % 2][:, 1, :], yc[:, t, :], G.ident[:, :]).then_inc(y_turned, 1)

            def project(t):
                pe.wait_ge(yT_kept, t + 1)
                if t >= 2:
                    pe.wait_ge(out_kept, t - 1)
                nc.tensor.matmul(out_ps[t % 2][:, 0, :], yT[:, t % 2, 0, :], G.mat("r_o"), start=True, stop=True)
                nc.tensor.matmul(out_ps[t % 2][:, 1, :], yT[:, t % 2, 1, :], G.mat("c_p"), start=True,
                                 stop=True).then_inc(out_done, 1)

            for t in range(NT + 3):
                if t < NT:
                    turn(t)
                if 1 <= t <= NT:
                    mix(t - 1)
                if 2 <= t <= NT + 1:
                    turn_y(t - 2)
                if t >= 3:
                    project(t - 3)


def stage_experts(nc, G, M):
    UNITS = E * QUAD
    HC = HID // P
    with ExitStack() as ctx:
        def sb(name, shape, dt=F32):
            return ctx.enter_context(nc.sbuf_tensor(f"e_{name}", shape, dt))

        def sem(name):
            return ctx.enter_context(nc.semaphore(f"e_{name}"))

        def ps(name, shape):
            return ctx.enter_context(nc.psum_tensor(f"e_{name}", shape, F32))

        N = norm_stats_tensors(sb, "n")
        h2 = sb("h2", [P, NT, D])
        h2T = sb("h2T", [P, T])
        w1 = sb("w1", [P, 2, HID])
        w2 = sb("w2", [P, 2, HC, D])
        b1 = sb("b1", [P, 2, HC])
        b2 = sb("b2", [E, D])
        mid = sb("mid", [P, 2, HC, BANK])
        logits = sb("logits", [P, NT, E])
        top = sb("top", [P, NT, E])
        top_at = sb("top_at", [P, NT, E], U32)
        top_slot = sb("top_slot", [P, NT, 2])
        gap = sb("gap", [P, NT])
        ratio = sb("ratio", [P, NT])
        share = sb("share", [P, 2, NT])
        pick = sb("pick", [P, 2, NT, E])
        gates = sb("gates", [P, NT, E])
        gatesT = sb("gatesT", [E, T])
        bank = [ps(f"bank{i}", [P, BANK]) for i in range(6)]
        weights_in = [sem(f"weights_in{i}") for i in range(2)]
        b2_in = sem("b2_in")
        layer1_in = sem("layer1_in")
        chain = sem("chain")
        var_ready = sem("var_ready")
        std_ready = sem("std_ready")
        h2_ready = sem("h2_ready")
        h2_turned = sem("h2_turned")
        h2T_kept = sem("h2T_kept")
        gated = sem("gated")
        gap_ready = sem("gap_ready")
        ratio_ready = sem("ratio_ready")
        gates_ready = sem("gates_ready")
        gates_turned = sem("gates_turned")
        gatesT_kept = sem("gatesT_kept")
        biased = sem("biased")
        bias_kept = sem("bias_kept")
        hidden = sem("hidden")
        hidden_kept = sem("hidden_kept")
        expert_done = sem("expert_done")
        expert_kept = sem("expert_kept")
        silu_ready = sem("silu_ready")
        block = ctx.enter_context(nc.Block())

        def over_experts(eng, expert):
            for slot in range(2):
                expert(slot, 0, slot, slot)
            with eng.Fori(1, E // 2 - 1) as pair:
                for slot in range(2):
                    expert(pair * 2 + slot, pair, slot, 2 + slot)
            for slot in range(2):
                expert(E - 2 + slot, E // 2 - 1, slot, E - 2 + slot)

        @block.sync
        def _(sp):
            sp.dma_start(b2[:, :], M.exp_b2).then_inc(b2_in, 16)
            sp.dma_start(G.mats1[:, :], M.mats1).then_inc(layer1_in, 16)

            def expert(e, pair, slot, at):
                if at >= 2:
                    sp.wait_ge(expert_done, e * QUAD - QUAD)
                sp.dma_start(w1[:, slot, :], bass.AP(M.exp_w1.tensor, e * (P * HID), [[HID, P], [1, HID]])
                             ).then_inc(weights_in[slot], 16)
                sp.dma_start(w2[:, slot, :, :], bass.AP(M.exp_w2.tensor, e * (P * HID), [[HID, P], [1, HID]])
                             ).then_inc(weights_in[slot], 16)
                sp.dma_start(b1[:, slot, :], bass.AP(M.cols.tensor, e * HC + EXP_B1, [[NCOLS, P], [1, HC]])
                             ).then_inc(weights_in[slot], 16)

            over_experts(sp, expert)
            sp.wait_ge(layer1_in, 16)

        @block.scalar
        def _(act):
            layer_norm_root(nc, act, N, var_ready, std_ready, 1)
            act.wait_ge(gap_ready, 1)
            nc.scalar.activation(ratio[:, :], gap[:, :], ACT.Exp).then_inc(ratio_ready, 1)
            for c in range(QUAD):
                act.wait_ge(gates_turned, c + 1)
                nc.scalar.copy(gatesT[:, c * BANK:(c + 1) * BANK], bank[2 + c % 2][0:E, :]).then_inc(gatesT_kept, 1)

            def expert(e, pair, slot, at):
                act.wait_ge(weights_in[slot], 48 * (pair + 1))
                for c in range(QUAD):
                    unit = e * QUAD + c
                    if at * QUAD + c >= 2:
                        act.wait_ge(expert_done, unit - 1)
                    for k in range(HC):
                        act.wait_ge(hidden, unit * HC + k + 1)
                        nc.scalar.activation(mid[:, c % 2, k, :], bank[k][:, :], ACT.Gelu,
                                             bias=b1[:, slot, k:k + 1]).then_inc(hidden_kept, 1)

            over_experts(act, expert)
            act.wait_ge(expert_kept, UNITS)
            for t in range(0, NT, QUAD):
                nc.scalar.activation(h2[:, t:t + QUAD, :], G.x2[:, t:t + QUAD, :], ACT.Silu).then_inc(silu_ready, 1)

        @block.vector
        def _(dve):
            link = chained(dve, chain)
            layer_norm(nc, dve, link, N, G.x2, h2, var_ready, std_ready, 1)
            nc.vector.memset(gates[:, :, :], 0.0).then_inc(h2_ready, 1)
            for c in range(QUAD):
                dve.wait_ge(h2_turned, c + 1)
                nc.vector.tensor_scalar(h2T[:, c * BANK:(c + 1) * BANK], bank[c % 2][:, :], G.col("ln2_g"),
                                        G.col("ln2_b"), ALU.mult, ALU.add).then_inc(h2T_kept, 1)
            dve.wait_ge(gated, 1)
            link(nc.vector.tensor_tensor(logits[:, :, :], bank[4][:, 0:NT * E].rearrange("p (t e) -> p t e", e=E),
                                         G.row("gate_b").unsqueeze(1).to_broadcast([P, NT, E]), ALU.add))
            for t in range(NT):
                last = nc.vector.max(top[:, t, :], logits[:, t, :])
            link(last)
            for t in range(NT):
                last = nc.vector.max_index(top_at[:, t, :], top[:, t, :], logits[:, t, :])
            link(last)
            link(nc.vector.tensor_copy(top_slot[:, :, :], top_at[:, :, 0:2]))
            nc.vector.tensor_tensor(gap[:, :], top[:, :, 1], top[:, :, 0], ALU.subtract).then_inc(gap_ready, 1)
            dve.wait_ge(ratio_ready, 1)
            link(nc.vector.tensor_scalar(share[:, 1, :], ratio[:, :], 1.0, None, ALU.add))
            link(nc.vector.reciprocal(share[:, 0, :], share[:, 1, :]))
            link(nc.vector.tensor_tensor(share[:, 1, :], ratio[:, :], share[:, 0, :], ALU.mult))
            slots = G.row("slots").unsqueeze(1).to_broadcast([P, NT, E])
            for i in range(2):
                link(nc.vector.tensor_tensor(pick[:, i, :, :], slots,
                                             top_slot[:, :, i].unsqueeze(2).to_broadcast([P, NT, E]), ALU.is_equal))
                link(nc.vector.tensor_tensor(pick[:, i, :, :], pick[:, i, :, :],
                                             share[:, i, :].unsqueeze(2).to_broadcast([P, NT, E]), ALU.mult))
            nc.vector.tensor_tensor(gates[:, :, :], pick[:, 0, :, :], pick[:, 1, :, :], ALU.add
                                    ).then_inc(gates_ready, 1)
            for c in range(QUAD):
                dve.wait_ge(biased, c + 1)
                tiles = G.x2[:, c * QUAD:(c + 1) * QUAD, :]
                nc.vector.tensor_tensor(tiles, tiles, bank[5][:, :].rearrange("p (t d) -> p t d", d=D), ALU.add
                                        ).then_inc(bias_kept, 1)

            def expert(e, pair, slot, at):
                for c in range(QUAD):
                    unit = e * QUAD + c
                    dve.wait_ge(expert_done, unit + 1)
                    if at == 0:
                        dve.wait_ge(bias_kept, c + 1)
                    else:
                        dve.wait_ge(expert_kept, unit - QUAD + 1)
                    for t in range(QUAD):
                        tile = G.x2[:, c * QUAD + t, :]
                        gate = gates[:, c * QUAD + t, :]
                        last = nc.vector.scalar_tensor_tensor(tile, bank[4 + c % 2][:, t * D:(t + 1) * D],
                                                              gate[:, bass.ds(e, 1)], tile, ALU.mult, ALU.add)
                    last.then_inc(expert_kept, 1)

            over_experts(dve, expert)
            for i in range(QUAD):
                tiles = slice(i * QUAD, (i + 1) * QUAD)
                dve.wait_ge(silu_ready, i + 1)
                link(nc.vector.tensor_tensor(h2[:, tiles, :], h2[:, tiles, :], G.mixer[:, tiles, :], ALU.mult))
                last = nc.vector.tensor_tensor(G.xt[:, tiles, :], G.xt[:, tiles, :], h2[:, tiles, :], ALU.add)
            link(last)

        @block.tensor
        def _(pe):
            pe.wait_ge(h2_ready, 1)
            for c in range(QUAD):
                if c >= 2:
                    pe.wait_ge(h2T_kept, c - 1)
                for k in range(QUAD):
                    last = nc.tensor.transpose(bank[c % 2][:, k * P:(k + 1) * P], h2[:, c * QUAD + k, :],
                                               G.ident[:, :])
                last.then_inc(h2_turned, 1)
            pe.wait_ge(h2T_kept, QUAD)
            for t in range(NT):
                last = nc.tensor.matmul(bank[4][:, t * E:(t + 1) * E], h2T[:, t * P:(t + 1) * P], G.mat("gate"),
                                        start=True, stop=True)
            last.then_inc(gated, 1)

            def hidden_layer(e, pair, slot, at, c):
                unit = e * QUAD + c
                if c == 0:
                    pe.wait_ge(weights_in[slot], 48 * (pair + 1))
                for k in range(HC):
                    if at * QUAD + c >= 1:
                        pe.wait_ge(hidden_kept, unit * HC + k - 3)
                    nc.tensor.matmul(bank[k][:, :], w1[:, slot, k * P:(k + 1) * P],
                                     h2T[:, c * BANK:(c + 1) * BANK], start=True, stop=True).then_inc(hidden, 1)

            def output_layer(e, pair, slot, at, c):
                unit = e * QUAD + c
                pe.wait_ge(hidden_kept, (unit + 1) * HC)
                if at * QUAD + c >= 2:
                    pe.wait_ge(expert_kept, unit - 1)
                for t in range(QUAD):
                    for k in range(HC):
                        last = nc.tensor.matmul(bank[4 + c % 2][:, t * D:(t + 1) * D],
                                                mid[:, c % 2, k, t * P:(t + 1) * P], w2[:, slot, k, :],
                                                start=(k == 0), stop=(k == HC - 1))
                last.then_inc(expert_done, 1)

            pe.wait_ge(gates_ready, 1)
            for c in range(QUAD):
                if c >= 2:
                    pe.wait_ge(gatesT_kept, c - 1)
                for k in range(QUAD):
                    last = nc.tensor.transpose(bank[2 + c % 2][0:E, k * P:(k + 1) * P],
                                               gates[:, c * QUAD + k, :], G.ident[:, :])
                last.then_inc(gates_turned, 1)
            pe.wait_ge(b2_in, 16)
            for c in range(QUAD):
                pe.wait_ge(gatesT_kept, c + 1)
                if c >= 1:
                    pe.wait_ge(bias_kept, c)
                for k in range(QUAD):
                    t = c * QUAD + k
                    last = nc.tensor.matmul(bank[5][:, k * D:(k + 1) * D], gatesT[:, t * P:(t + 1) * P], b2[:, :],
                                            start=True, stop=True)
                last.then_inc(biased, 1)
            pe.wait_ge(bias_kept, QUAD)
            hidden_layer(0, 0, 0, 0, 0)

            def expert(e, pair, slot, at):
                for c in range(QUAD):
                    if c + 1 < QUAD:
                        hidden_layer(e, pair, slot, at, c + 1)
                    elif at + 1 < E:
                        hidden_layer(e + 1, pair + slot, 1 - slot, at + 1, 0)
                    output_layer(e, pair, slot, at, c)

            over_experts(pe, expert)


def stage_linear_attention(nc, G, M):
    EPS_DEN = 1e-6
    NB = 7
    PAIRS = LH // 2
    VA = LD + 1
    PAIR_GROUPS = [range(0, 3), range(3, 6), range(6, 8)]
    NAMES = ["q0", "q1", "k0", "k1", "v0", "v1", "turn0", "turn1", "out", "s0", "s1", "s2", "s3",
             "kt0", "kt1", "num0", "num1", "num2", "st0", "st1", "st2"]
    LATE = NAMES[6:9]
    ACT_JOBS = [n for n in NAMES if n[:-1] in ("v", "turn", "kt")]
    DVE_JOBS = [n for n in NAMES if n not in ACT_JOBS]
    NJ = len(NAMES)
    assert NJ % NB == 0

    def count(names, t, name):
        late = sum(n in names for n in LATE)
        if isinstance(t, int) and t == 0:
            return [n for n in names if n not in LATE].index(name) + 1
        return t * len(names) + (names.index(name) + 1 - late)

    def count_tail(names, name):
        late = [n for n in LATE if n in names]
        return NT * len(names) - len(late) + late.index(name) + 1

    with ExitStack() as ctx:
        def sb(name, shape, dt=F32):
            return ctx.enter_context(nc.sbuf_tensor(f"l_{name}", shape, dt))

        def sem(name):
            return ctx.enter_context(nc.semaphore(f"l_{name}"))

        h = sb("h", [P, P])
        exps = sb("exps", [P, 4, BANK])
        qk = sb("qk", [P, 2, PAIRS, P])
        k_tok = sb("k_tok", [P, PAIRS * P])
        v = sb("v", [P, LH, VA])
        scores = sb("scores", [P, LH, P])
        state = sb("state", [P, PAIRS, 2 * VA])
        den = sb("den", [P, 3, 6])
        inv_den = sb("inv_den", [P, 3, 6])
        att = sb("att", [P, LH * LD])
        attT = sb("attT", [P, PAIRS, P])
        bank = [ctx.enter_context(nc.psum_tensor(f"l_bank{i}", [P, BANK], F32)) for i in range(NB)]
        h_in = sem("h_in")
        ones_ready = sem("ones_ready")
        state_zero = sem("state_zero")
        done = sem("done")
        exp_ready = sem("exp_ready")
        act_kept = sem("act_kept")
        dve_kept = sem("dve_kept")
        chain = sem("chain")
        block = ctx.enter_context(nc.Block())

        def over_tiles(eng, tile):
            for b in range(B):
                peeled = 2 if b == 0 else 1
                for t in range(b * NS, b * NS + peeled):
                    tile(t, t)
                with eng.Fori(b * NS + peeled, (b + 1) * NS) as t:
                    tile(t, b * NS + peeled)

        def bank_of(name):
            return bank[NAMES.index(name) % NB]

        @block.gpsimd
        def _(pool):
            nc.gpsimd.memset(v[:, :, LD:VA], 1.0).then_inc(ones_ready, 1)

            def tile(t, at):
                if at >= 1:
                    pool.wait_ge(done, count(NAMES, t - 1, "v1"))
                nc.gpsimd.tensor_copy(h[:, :], G.h1T[:, bass.ds(t * P, P)]).then_inc(h_in, 1)

            over_tiles(pool, tile)

        @block.scalar
        def _(act):
            def turned(wait_for, g):
                act.wait_ge(done, wait_for)
                nc.scalar.copy(attT[:, 4 * g:4 * g + 4, :], bank_of(f"turn{g}")[:, :].rearrange(
                    "p (c t) -> p c t", t=P)).then_inc(act_kept, 1)

            def tile(t, at):
                for i, name in enumerate(("q0", "q1", "k0", "k1")):
                    act.wait_ge(done, count(NAMES, t, name))
                    if at >= 1:
                        act.wait_ge(dve_kept, count(DVE_JOBS, t - 1, name))
                    nc.scalar.activation(exps[:, i, :], bank_of(name)[:, :], ACT.Exp).then_inc(exp_ready, 1)
                if at == 0:
                    act.wait_ge(ones_ready, 1)
                for g in range(2):
                    act.wait_ge(done, count(NAMES, t, f"v{g}"))
                    nc.scalar.copy(v[:, 8 * g:8 * g + 8, 0:LD], bank_of(f"v{g}")[:, :].rearrange(
                        "p (h d) -> p h d", d=LD)).then_inc(act_kept, 1)
                if at >= 1:
                    for g in range(2):
                        turned(count(NAMES, t, f"turn{g}"), g)
                for g in range(2):
                    act.wait_ge(done, count(NAMES, t, f"kt{g}"))
                    nc.scalar.copy(k_tok[:, g * BANK:(g + 1) * BANK], bank_of(f"kt{g}")[:, :]).then_inc(act_kept, 1)

            over_tiles(act, tile)
            for g in range(2):
                turned(count_tail(NAMES, f"turn{g}"), g)

        @block.vector
        def _(dve):
            def residual(wait_for, t):
                dve.wait_ge(done, wait_for)
                nc.vector.tensor_tensor(G.x2[:, :, :].rearrange("p t d -> p (t d)")[:, bass.ds(t * P, P)],
                                        bank_of("out")[:, 0:D],
                                        G.xn[:, :, :].rearrange("p t d -> p (t d)")[:, bass.ds(t * P, P)],
                                        ALU.add).then_inc(dve_kept, 1)

            def tile(t, at):
                link = chained(dve, chain, t * 10)
                if at in (0, NS):
                    if at:
                        dve.wait_ge(dve_kept, count(DVE_JOBS, t - 1, "st2"))
                    nc.vector.memset(state[:, :, :], 0.0).then_inc(state_zero, 1)
                    dve.wait_ge(state_zero, at // NS + 1)
                for i, name in enumerate(("q0", "q1", "k0", "k1")):
                    dve.wait_ge(exp_ready, t * 4 + i + 1)
                    link(nc.vector.tensor_scalar(exps[:, i, :], exps[:, i, :], 1.0, None, ALU.min))
                    nc.vector.scalar_tensor_tensor(
                        qk[:, i // 2, 4 * (i % 2):4 * (i % 2) + 4, :].rearrange("p c t -> p (c t)"),
                        bank_of(name)[:, :], 1.0, exps[:, i, :], ALU.add, ALU.max).then_inc(dve_kept, 1)
                if at >= 1:
                    residual(count(NAMES, t, "out"), t - 1)
                for i in range(4):
                    dve.wait_ge(done, count(NAMES, t, f"s{i}"))
                    first = 8 * (i // 2) + i % 2
                    nc.vector.tensor_tensor(scores[:, first:first + 7:2, :], bank_of(f"s{i}")[:, :].rearrange(
                        "p (h t) -> p h t", t=P), G.causal01[:, :].unsqueeze(1).to_broadcast([P, 4, P]),
                        ALU.mult).then_inc(dve_kept, 1)
                for g, pairs in enumerate(PAIR_GROUPS):
                    n = 2 * len(pairs)
                    dve.wait_ge(done, count(NAMES, t, f"num{g}"))
                    sums = bank_of(f"num{g}")[:, 0:n * VA].rearrange("p (h d) -> p h d", d=VA)
                    link(nc.vector.tensor_scalar(den[:, g, 0:n], sums[:, :, LD], EPS_DEN, None, ALU.max))
                    link(nc.vector.reciprocal(inv_den[:, g, 0:n], den[:, g, 0:n]))
                    first = 2 * pairs[0] * LD
                    nc.vector.tensor_tensor(att[:, first:first + n * LD].rearrange("p (h d) -> p h d", d=LD),
                                            sums[:, :, 0:LD], inv_den[:, g, 0:n].unsqueeze(2).to_broadcast(
                                                [P, n, LD]), ALU.mult).then_inc(dve_kept, 1)
                for g, pairs in enumerate(PAIR_GROUPS):
                    dve.wait_ge(done, count(NAMES, t, f"st{g}"))
                    some = slice(pairs[0], pairs[-1] + 1)
                    part = bank_of(f"st{g}")[:, 0:len(pairs) * 2 * VA].rearrange("p (c d) -> p c d", d=2 * VA)
                    for rows, cols in ((slice(0, LD), slice(0, VA)), (slice(LD, P), slice(VA, 2 * VA))):
                        last = nc.vector.tensor_tensor(state[rows, some, cols], part[rows, :, cols],
                                                       state[rows, some, cols], ALU.add)
                    last.then_inc(dve_kept, 1)
                assert link.done[0] == 10

            over_tiles(dve, tile)
            residual(count_tail(NAMES, "out"), NT - 1)

        @block.tensor
        def _(pe):
            def free(t, at, name):
                p = NAMES.index(name) - NB
                if at == 0:
                    while p >= 0 and NAMES[p] in LATE:
                        p -= NB
                    if p < 0:
                        return
                if at == NT and p >= 0:
                    p -= NB
                before = t if p >= 0 else t - 1
                owner = NAMES[p % NJ]
                if at == 1 and p < 0 and owner in LATE:
                    owner = NAMES[p % NJ - NB]
                if owner in ACT_JOBS:
                    pe.wait_ge(act_kept, count(ACT_JOBS, before, owner))
                else:
                    pe.wait_ge(dve_kept, count(DVE_JOBS, before, owner))

            def turn_att(g):
                for c in range(4):
                    last = nc.tensor.transpose(bank_of(f"turn{g}")[:, c * P:(c + 1) * P],
                                               att[:, (4 * g + c) * P:(4 * g + c + 1) * P], G.ident[:, :])
                last.then_inc(done, 1)

            def project():
                w = G.mat1("l_o")
                for c in range(PAIRS):
                    last = nc.tensor.matmul(bank_of("out")[:, 0:D], attT[:, c, :], w[:, c * D:(c + 1) * D],
                                            start=(c == 0), stop=(c == PAIRS - 1))
                last.then_inc(done, 1)

            def tile(t, at):
                pe.wait_ge(h_in, t + 1)
                for i, name in enumerate(("q0", "q1", "k0", "k1")):
                    free(t, at, name)
                    w = G.mat1("l_q" if i < 2 else "l_k")
                    for c in range(4):
                        f = (4 * (i % 2) + c) * P
                        last = nc.tensor.matmul(bank_of(name)[:, c * P:(c + 1) * P], w[:, f:f + P], h[:, :],
                                                start=True, stop=True)
                    last.then_inc(done, 1)
                for g in range(2):
                    free(t, at, f"v{g}")
                    nc.tensor.matmul(bank_of(f"v{g}")[:, :], h[:, :], G.mat1("l_v")[:, g * BANK:(g + 1) * BANK],
                                     start=True, stop=True).then_inc(done, 1)
                if at >= 1:
                    pe.wait_ge(dve_kept, count(DVE_JOBS, t - 1, "num2"))
                    for g in range(2):
                        free(t, at, f"turn{g}")
                        turn_att(g)
                    free(t, at, "out")
                    pe.wait_ge(act_kept, count(ACT_JOBS, t, "turn1"))
                    project()
                pe.wait_ge(dve_kept, count(DVE_JOBS, t, "k1"))
                for i in range(4):
                    free(t, at, f"s{i}")
                    rows = slice(0, LD) if i % 2 == 0 else slice(LD, P)
                    for c in range(4):
                        pair = 4 * (i // 2) + c
                        last = nc.tensor.matmul(bank_of(f"s{i}")[:, c * P:(c + 1) * P], qk[rows, 1, pair, :],
                                                qk[rows, 0, pair, :], start=True, stop=True)
                    last.then_inc(done, 1)
                for g in range(2):
                    free(t, at, f"kt{g}")
                    for c in range(4):
                        last = nc.tensor.transpose(bank_of(f"kt{g}")[:, c * P:(c + 1) * P],
                                                   qk[:, 1, 4 * g + c, :], G.ident[:, :])
                    last.then_inc(done, 1)
                pe.wait_ge(act_kept, count(ACT_JOBS, t, "v1"))
                for g, pairs in enumerate(PAIR_GROUPS):
                    free(t, at, f"num{g}")
                    pe.wait_ge(dve_kept, count(DVE_JOBS, t, "s1" if pairs[-1] < 4 else "s3"))
                    for m, c in enumerate(pairs):
                        out = bank_of(f"num{g}")[:, m * 2 * VA:(m + 1) * 2 * VA]
                        nc.tensor.matmul(out, qk[:, 0, c, :], state[:, c, :], start=(m == 0), stop=False,
                                         skip_group_check=True)
                        for i in range(2):
                            last = nc.tensor.matmul(out[:, i * VA:(i + 1) * VA], scores[:, 2 * c + i, :],
                                                    v[:, 2 * c + i, :], start=False, stop=True,
                                                    skip_group_check=True)
                    last.then_inc(done, 1)
                for g, pairs in enumerate(PAIR_GROUPS):
                    free(t, at, f"st{g}")
                    pe.wait_ge(act_kept, count(ACT_JOBS, t, "kt0" if pairs[-1] < 4 else "kt1"))
                    for m, c in enumerate(pairs):
                        last = nc.tensor.matmul(bank_of(f"st{g}")[:, m * 2 * VA:(m + 1) * 2 * VA],
                                                k_tok[:, c * P:(c + 1) * P],
                                                v[:, 2 * c:2 * c + 2, :].rearrange("p h d -> p (h d)"),
                                                start=True, stop=True)
                    last.then_inc(done, 1)

            over_tiles(pe, tile)
            pe.wait_ge(dve_kept, count(DVE_JOBS, NT - 1, "num2"))
            for g in range(2):
                free(NT, NT, f"turn{g}")
                turn_att(g)
            free(NT, NT, "out")
            pe.wait_ge(act_kept, count_tail(ACT_JOBS, "turn1"))
            project()


def stage_adapters(nc, G, M):
    CLAMP_MAX = float(np.log(1.0 / 0.01))
    EPS_NORM = 1e-12
    ZW = D + PROJ + RSUM
    FC = DF // P
    with ExitStack() as ctx:
        def sb(name, shape, dt=F32):
            return ctx.enter_context(nc.sbuf_tensor(f"a_{name}", shape, dt))

        used = []

        def sem(name):
            s = ctx.enter_context(nc.semaphore(f"a_{name}"))
            used.append(s.num)
            return s

        N = norm_stats_tensors(sb, "n")
        h = sb("h", [P, NT, D])
        hT = sb("hT", [P, T])
        mid = sb("mid", [P, 2, FC, BANK])
        z = sb("z", [P, NT, ZW])
        sim = sb("sim", [PROJ, 4, NE1])
        ones = sb("ones", [PROJ, PROJ])
        up = sb("up", [RSUM, D])
        proj = sb("proj", [P, NT, PROJ])
        proj_sq = sb("proj_sq", [P, NT, PROJ])
        norms = sb("norms", [P, 4, NT])
        temp = sb("temp", [P, 2])
        projT = sb("projT", [PROJ, T])
        logits = sb("logits", [P, NT, 8])
        top = sb("top", [P, NT, 8])
        top_at = sb("top_at", [P, NT, 8], U32)
        top_slot = sb("top_slot", [P, NT])
        exps = sb("exps", [P, NT, NE1])
        total = sb("total", [P, 2, NT])
        pick = sb("pick", [P, NT, NE1])
        low = sb("low", [P, NT, RSUM])
        lowT = sb("lowT", [RSUM, T])
        gate = sb("gate", [P, NT, D])
        result = sb("result", [P, NT, D])
        bank = [ctx.enter_context(nc.psum_tensor(f"a_bank{i}", [P, BANK], F32)) for i in range(8)]
        small_in = sem("small_in")
        chain = sem("chain")
        pool_ready = sem("pool_ready")
        var_ready = sem("var_ready")
        std_ready = sem("std_ready")
        z_done = sem("z_done")
        z_kept = sem("z_kept")
        h_ready = sem("h_ready")
        h_turned = sem("h_turned")
        hT_kept = sem("hT_kept")
        hidden = sem("hidden")
        hidden_kept = sem("hidden_kept")
        ffn_done = sem("ffn_done")
        ffn_kept = sem("ffn_kept")
        sim_summed = sem("sim_summed")
        squares_ready = sem("squares_ready")
        roots_ready = sem("roots_ready")
        temp_ready = sem("temp_ready")
        temp_exp = sem("temp_exp")
        sim_ready = sem("sim_ready")
        proj_ready = sem("proj_ready")
        proj_turned = sem("proj_turned")
        projT_kept = sem("projT_kept")
        logits_done = sem("logits_done")
        margin_ready = sem("margin_ready")
        exps_ready = sem("exps_ready")
        low_ready = sem("low_ready")
        low_turned = sem("low_turned")
        lowT_kept = sem("lowT_kept")
        gate_done = sem("gate_done")
        gate_kept = sem("gate_kept")
        silu_ready = sem("silu_ready")
        result_ready = sem("result_ready")
        stored = sem("stored")
        clear_semaphores(nc, range(min(used), max(used) + 1))
        block = ctx.enter_context(nc.Block())

        @block.sync
        def _(sp):
            sp.dma_start(sim[:, 0, :], M.sim).then_inc(small_in, 16)
            sp.dma_start(up[:, :], M.up).then_inc(small_in, 16)
            out = M.out.rearrange("b (t p) d -> p (b t) d", p=P)
            for c in range(QUAD):
                sp.wait_ge(result_ready, c + 1)
                sp.dma_start(out[:, c * QUAD:(c + 1) * QUAD, :], result[:, c * QUAD:(c + 1) * QUAD, :]
                             ).then_inc(stored, 16)
            sp.wait_ge(stored, 16 * QUAD)

        @block.gpsimd
        def _(pool):
            nc.gpsimd.memset(ones[:, :], 1.0).then_inc(pool_ready, 1)
            pool.wait_ge(pool_ready, 1)
            nc.gpsimd.memset(logits[:, :, :], -3e38).then_inc(pool_ready, 1)

        @block.scalar
        def _(act):
            for i in range(NT // 2):
                act.wait_ge(z_done, i + 1)
                nc.scalar.copy(z[:, 2 * i:2 * i + 2, :], bank[6 + i % 2][:, 0:2 * ZW].rearrange(
                    "p (t w) -> p t w", w=ZW)).then_inc(z_kept, 1)
            layer_norm_root(nc, act, N, var_ready, std_ready, 1)
            act.wait_ge(sim_summed, 1)
            nc.scalar.activation(sim[:, 2, :], bank[5][0:PROJ, 0:NE1], ACT.Sqrt).then_inc(roots_ready, 1)
            act.wait_ge(squares_ready, 1)
            nc.scalar.activation(norms[:, 1, :], norms[:, 0, :], ACT.Sqrt).then_inc(roots_ready, 1)
            act.wait_ge(temp_ready, 1)
            nc.scalar.activation(temp[:, 1:2], temp[:, 0:1], ACT.Exp).then_inc(temp_exp, 1)
            for c in range(QUAD):
                act.wait_ge(proj_turned, c + 1)
                nc.scalar.copy(projT[:, c * BANK:(c + 1) * BANK], bank[6 + c % 2][0:PROJ, :]).then_inc(projT_kept, 1)
            act.wait_ge(margin_ready, 1)
            nc.scalar.activation(exps[:, :, :], exps[:, :, :], ACT.Exp).then_inc(exps_ready, 1)
            for c in range(QUAD):
                act.wait_ge(low_turned, c + 1)
                nc.scalar.copy(lowT[:, c * BANK:(c + 1) * BANK], bank[6 + c % 2][0:RSUM, :]).then_inc(lowT_kept, 1)
            for c in range(QUAD):
                if c >= 2:
                    act.wait_ge(ffn_done, c - 1)
                for k in range(FC):
                    act.wait_ge(hidden, c * FC + k + 1)
                    nc.scalar.activation(mid[:, c % 2, k, :], bank[k][:, :], ACT.Gelu).then_inc(hidden_kept, 1)
            for c in range(QUAD):
                act.wait_ge(gate_kept, c + 1)
                tiles = slice(c * QUAD, (c + 1) * QUAD)
                nc.scalar.activation(result[:, tiles, :], gate[:, tiles, :], ACT.Silu).then_inc(silu_ready, 1)

        @block.vector
        def _(dve):
            link = chained(dve, chain)
            layer_norm(nc, dve, link, N, G.x2, h, var_ready, std_ready, 1)
            dve.wait_ge(small_in, 32)
            nc.vector.tensor_tensor(sim[:, 1, :], sim[:, 0, :], sim[:, 0, :], ALU.mult).then_inc(h_ready, 1)
            nc.vector.tensor_scalar(temp[:, 0:1], G.row("temp"), CLAMP_MAX, None, ALU.min).then_inc(temp_ready, 1)
            dve.wait_ge(z_kept, NT // 2)
            nc.vector.tensor_tensor(proj[:, :, :], z[:, :, D:D + PROJ], G.row("router_b").unsqueeze(1).to_broadcast(
                [P, NT, PROJ]), ALU.add).then_inc(proj_ready, 1)
            for c in range(QUAD):
                dve.wait_ge(h_turned, c + 1)
                nc.vector.tensor_scalar(hT[:, c * BANK:(c + 1) * BANK], bank[c][:, :], G.col("l1_ln2_g"),
                                        G.col("l1_ln2_b"), ALU.mult, ALU.add).then_inc(hT_kept, 1)
            dve.wait_ge(proj_ready, 1)
            link(nc.vector.tensor_tensor(proj_sq[:, :, :], proj[:, :, :], proj[:, :, :], ALU.mult))
            nc.vector.tensor_reduce(norms[:, 0, :], proj_sq[:, :, :], AX.X, ALU.add).then_inc(squares_ready, 1)
            dve.wait_ge(roots_ready, 2)
            link(nc.vector.tensor_scalar(sim[:, 2, :], sim[:, 2, :], EPS_NORM, None, ALU.max))
            link(nc.vector.reciprocal(sim[:, 1, :], sim[:, 2, :]))
            nc.vector.tensor_tensor(sim[:, 3, :], sim[:, 0, :], sim[:, 1, :], ALU.mult).then_inc(sim_ready, 1)
            link(nc.vector.tensor_scalar(norms[:, 2, :], norms[:, 1, :], EPS_NORM, None, ALU.max))
            link(nc.vector.reciprocal(norms[:, 3, :], norms[:, 2, :]))
            dve.wait_ge(temp_exp, 1)
            link(nc.vector.tensor_scalar(norms[:, 3, :], norms[:, 3, :], temp[:, 1:2], None, ALU.mult))
            dve.wait_ge(pool_ready, 2)
            dve.wait_ge(logits_done, 1)
            link(nc.vector.tensor_tensor(logits[:, :, 0:NE1], bank[4][:, 0:NT * NE1].rearrange(
                "p (t e) -> p t e", e=NE1), norms[:, 3, :].unsqueeze(2).to_broadcast([P, NT, NE1]), ALU.mult))
            for t in range(NT):
                last = nc.vector.max(top[:, t, :], logits[:, t, :])
            link(last)
            nc.vector.tensor_tensor(exps[:, :, :], logits[:, :, 0:NE1], top[:, :, 0].unsqueeze(2).to_broadcast(
                [P, NT, NE1]), ALU.subtract).then_inc(margin_ready, 1)
            for t in range(NT):
                last = nc.vector.max_index(top_at[:, t, :], top[:, t, :], logits[:, t, :])
            link(last)
            link(nc.vector.tensor_copy(top_slot[:, :], top_at[:, :, 0]))
            link(nc.vector.tensor_tensor(pick[:, :, :], G.row("slots")[:, 0:NE1].unsqueeze(1).to_broadcast(
                [P, NT, NE1]), top_slot[:, :].unsqueeze(2).to_broadcast([P, NT, NE1]), ALU.is_equal))
            dve.wait_ge(exps_ready, 1)
            link(nc.vector.tensor_reduce(total[:, 0, :], exps[:, :, :], AX.X, ALU.add))
            link(nc.vector.reciprocal(total[:, 1, :], total[:, 0, :]))
            link(nc.vector.tensor_tensor(pick[:, :, :], pick[:, :, :], total[:, 1, :].unsqueeze(2).to_broadcast(
                [P, NT, NE1]), ALU.mult))
            at = 0
            for e, rank in enumerate(RANKS):
                last = nc.vector.tensor_tensor(low[:, :, at:at + rank], z[:, :, D + PROJ + at:D + PROJ + at + rank],
                                               pick[:, :, e].unsqueeze(2).to_broadcast([P, NT, rank]), ALU.mult)
                at += rank
            last.then_inc(low_ready, 1)
            for c in range(QUAD):
                tiles = slice(c * QUAD, (c + 1) * QUAD)
                dve.wait_ge(gate_done, c + 1)
                nc.vector.tensor_tensor(gate[:, tiles, :], bank[4 + c % 2][:, :].rearrange("p (t d) -> p t d", d=D),
                                        z[:, tiles, 0:D], ALU.add).then_inc(gate_kept, 1)
            for c in range(QUAD):
                tiles = slice(c * QUAD, (c + 1) * QUAD)
                dve.wait_ge(ffn_done, c + 1)
                nc.vector.tensor_tensor(G.mixer[:, tiles, :], bank[6 + c % 2][:, :].rearrange(
                    "p (t d) -> p t d", d=D), G.x2[:, tiles, :], ALU.add).then_inc(ffn_kept, 1)
            dve.wait_ge(ffn_kept, QUAD)
            for c in range(QUAD):
                tiles = slice(c * QUAD, (c + 1) * QUAD)
                dve.wait_ge(silu_ready, c + 1)
                link(nc.vector.tensor_tensor(result[:, tiles, :], result[:, tiles, :], G.mixer[:, tiles, :],
                                             ALU.mult))
                nc.vector.tensor_tensor(result[:, tiles, :], result[:, tiles, :], G.xt[:, tiles, :], ALU.add
                                        ).then_inc(result_ready, 1)

        @block.tensor
        def _(pe):
            w = G.mats1[:, MATS1["base"][0]:MATS1["base"][0] + ZW]
            for i in range(NT // 2):
                if i >= 2:
                    pe.wait_ge(z_kept, i - 1)
                for k in range(2):
                    t = 2 * i + k
                    last = nc.tensor.matmul(bank[6 + i % 2][:, k * ZW:(k + 1) * ZW], G.xnT[:, t * P:(t + 1) * P], w,
                                            start=True, stop=True)
                last.then_inc(z_done, 1)
            pe.wait_ge(h_ready, 1)
            for c in range(QUAD):
                for k in range(QUAD):
                    last = nc.tensor.transpose(bank[c][:, k * P:(k + 1) * P], h[:, c * QUAD + k, :], G.ident[:, :])
                last.then_inc(h_turned, 1)
            pe.wait_ge(pool_ready, 1)
            nc.tensor.matmul(bank[5][0:PROJ, 0:NE1], ones[:, :], sim[:, 1, :], start=True, stop=True
                             ).then_inc(sim_summed, 1)
            pe.wait_ge(proj_ready, 1)
            pe.wait_ge(z_kept, NT // 2)
            for c in range(QUAD):
                if c >= 2:
                    pe.wait_ge(projT_kept, c - 1)
                for k in range(QUAD):
                    last = nc.tensor.transpose(bank[6 + c % 2][0:PROJ, k * P:(k + 1) * P],
                                               proj[:, c * QUAD + k, :], G.ident[:, :])
                last.then_inc(proj_turned, 1)

            def hidden_layer(c):
                pe.wait_ge(hT_kept, QUAD)
                for k in range(FC):
                    if c >= 1:
                        pe.wait_ge(hidden_kept, (c - 1) * FC + k + 1)
                    nc.tensor.matmul(bank[k][:, :], G.mat1("f1")[:, k * P:(k + 1) * P],
                                     hT[:, c * BANK:(c + 1) * BANK], start=True, stop=True).then_inc(hidden, 1)

            pe.wait_ge(projT_kept, QUAD)
            pe.wait_ge(sim_ready, 1)
            for t in range(NT):
                last = nc.tensor.matmul(bank[4][:, t * NE1:(t + 1) * NE1], projT[:, t * P:(t + 1) * P],
                                        sim[:, 3, :], start=True, stop=True)
            last.then_inc(logits_done, 1)
            hidden_layer(0)
            pe.wait_ge(low_ready, 1)
            for c in range(QUAD):
                if c >= 2:
                    pe.wait_ge(lowT_kept, c - 1)
                for k in range(QUAD):
                    last = nc.tensor.transpose(bank[6 + c % 2][0:RSUM, k * P:(k + 1) * P], low[:, c * QUAD + k, :],
                                               G.ident[:, :])
                last.then_inc(low_turned, 1)
            for c in range(QUAD):
                pe.wait_ge(lowT_kept, c + 1)
                if c >= 2:
                    pe.wait_ge(gate_kept, c - 1)
                for k in range(QUAD):
                    t = c * QUAD + k
                    last = nc.tensor.matmul(bank[4 + c % 2][:, k * D:(k + 1) * D], lowT[:, t * P:(t + 1) * P],
                                            up[:, :], start=True, stop=True)
                last.then_inc(gate_done, 1)
            pe.wait_ge(lowT_kept, QUAD)
            for c in range(QUAD):
                if c + 1 < QUAD:
                    hidden_layer(c + 1)
                pe.wait_ge(hidden_kept, (c + 1) * FC)
                if c >= 2:
                    pe.wait_ge(ffn_kept, c - 1)
                for k in range(QUAD):
                    for m in range(FC):
                        last = nc.tensor.matmul(bank[6 + c % 2][:, k * D:(k + 1) * D],
                                                mid[:, c % 2, m, k * P:(k + 1) * P],
                                                G.mat1("f2")[:, m * D:(m + 1) * D], start=(m == 0),
                                                stop=(m == FC - 1))
                last.then_inc(ffn_done, 1)


def recurrent_block_kernel(nc, out, **ins):
    def scratch(name, shape, dt=F32):
        return nc.dram_tensor(name, shape, dt).ap()

    M = Named(**ins)
    M.out = out
    M.split = scratch("split", [5, PIECES, B, P, S], BF16)
    M.rel = scratch("rel", [BH, S + 2 * RPAD, NREL])
    M.window = scratch("window", [BH, S, WIN])
    with ExitStack() as ctx:
        def sb(name, shape, dt=F32):
            return ctx.enter_context(nc.sbuf_tensor(name, shape, dt))

        G = Named()
        G.xt = sb("xt", [P, NT, D])
        G.xn = sb("xn", [P, NT, D])
        G.cols = sb("cols", [P, NCOLS])
        G.rows = sb("rows", [P, NROWS])
        G.mats = sb("mats", [P, NMATS])
        G.ident = sb("ident", [P, P])
        G.identb = sb("identb", [P, P], BF16)
        G.mask_ij = sb("mask_ij", [P, P], BF16)
        G.mask_ji = sb("mask_ji", [P, P], BF16)
        G.causal01 = sb("causal01", [P, P])
        G.far_sign = sb("far_sign", [P, P])
        G.before_last = sb("before_last", [P, P])
        G.after_first = sb("after_first", [P, P])
        G.zeros = sb("zeros", [P, RPAD * NREL])
        G.negs = sb("negs", [P, 1])
        G.col = lambda name: G.cols[:, COL[name]:COL[name] + 1]
        G.row = lambda name: G.rows[:, ROWS[name][0]:ROWS[name][0] + ROWS[name][1]]
        G.mat = lambda name: G.mats[:, MATS[name][0]:MATS[name][0] + MATS[name][1]]
        G.mixer = sb("mixer", [P, NT, D])
        G.x2 = sb("x2", [P, NT, D])
        with ExitStack() as layer0:
            def sb0(name, shape, dt=F32):
                return layer0.enter_context(nc.sbuf_tensor(name, shape, dt))

            G.att = sb0("att", [P, BH, NS, VCOLS])
            G.catt = sb0("catt", [P, BH, NS, DK + 1])
            G.far = sb0("far", [P, BH, NS])
            G.v_rel = sb0("v_rel", [P, BH, NS, DK])
            G.v_causal = sb0("v_causal", [P, BH, NS, DK])
            G.rel_last = sb0("rel_last", [P, B, H, NS])
            with ExitStack() as turned:
                G.xnT = turned.enter_context(nc.sbuf_tensor("xnT", [P, T], F32))
                G.h1T = turned.enter_context(nc.sbuf_tensor("h1T", [P, T], F32))
                stage_normalize(nc, G, M, "n0", "ln1_g", "ln1_b", True)
                stage_project(nc, G, M)
            stage_attention(nc, G, M, True)
            stage_attention(nc, G, M, False)
            stage_combine(nc, G, M)
        with ExitStack() as layer1:
            G.mats1 = layer1.enter_context(nc.sbuf_tensor("mats1", [P, NMATS1], F32))
            G.mat1 = lambda name: G.mats1[:, MATS1[name][0]:MATS1[name][0] + MATS1[name][1]]
            stage_experts(nc, G, M)
            G.xnT = layer1.enter_context(nc.sbuf_tensor("xnT1", [P, T], F32))
            with ExitStack() as turned:
                G.h1T = turned.enter_context(nc.sbuf_tensor("h1T1", [P, T], F32))
                stage_normalize(nc, G, M, "n1", "l1_ln1_g", "l1_ln1_b", False)
                stage_linear_attention(nc, G, M)
            stage_adapters(nc, G, M)


def layout(inputs):
    f = lambda name: np.asarray(inputs[name])
    chunks = lambda w: w.reshape(-1, P, w.shape[-1]).transpose(1, 0, 2).reshape(P, -1)
    rk, rv = f("L0_attn_rel_k_emb"), f("L0_attn_rel_v_emb")
    cols = [f("L0_ffn_ln1_g"), f("L0_ffn_ln1_b"), f("L0_ffn_ln2_g"), f("L0_ffn_ln2_b"), f("L0_ffn_bq"),
            f("L0_ffn_bk"), np.tile(rk[0], H), np.tile(rk[-1], H), f("L1_attn_ln1_g"), f("L1_attn_ln1_b"),
            f("L1_attn_ln2_g"), f("L1_attn_ln2_b"), *f("L0_ffn_exp_b1").reshape(-1, P)]
    rows = [f("L0_attn_b_o"), f("L0_ffn_bv"), f("L0_ffn_bp"), f("L0_ffn_gate_b"), np.tile(rv[0], H),
            np.tile(rv[-1], H), f("L1_ffn_bp"), f("L1_ffn_temp"), np.arange(E, dtype=np.float32)]
    mats = [f("L0_attn_Wq").T, f("L0_attn_Wk").T, f("L0_attn_Wv").T, f("L0_attn_Wo").T, f("L0_ffn_Wq"),
            f("L0_ffn_Wk"), f("L0_ffn_Wv"), f("L0_ffn_Wp"), f("L0_ffn_gate_W")]
    mats1 = [f("L1_attn_Wq"), f("L1_attn_Wk"), f("L1_attn_Wv"), chunks(f("L1_attn_Wo")), f("L1_attn_Wf1"),
             chunks(f("L1_attn_Wf2")), f("L1_ffn_W").T, f("L1_ffn_Wp").T,
             np.concatenate([f(f"L1_ffn_Wd{i}") for i in range(NE1)], 0).T]
    rk_block = np.zeros((H, DK, H, NREL), np.float32)
    rk_block_first = np.zeros((H, DK, H, NREL), np.float32)
    rv_block = np.zeros((H, NREL, H, DK), np.float32)
    rv_block_first = np.zeros((H, NREL, H, DK), np.float32)
    for h in range(H):
        rk_block[h, :, h, :] = rk.T
        rk_block_first[h, :, h, :] = np.broadcast_to(rk[0][:, None], (DK, NREL))
        rv_block[h, :, h, :] = rv
        rv_block_first[h, :, h, :] = np.broadcast_to(rv[0], (NREL, DK))
    fill = lambda w: np.concatenate([w.reshape(H * NREL, D), np.zeros((RCH * P - H * NREL, D), np.float32)], 0)
    return {
        "x": f("L0_attn_x").reshape(T, D),
        "cols": np.stack(cols, 1), "rows": np.concatenate(rows), "mats": np.concatenate(mats, 1),
        "mats1": np.concatenate(mats1, 1),
        "rk_block": rk_block.reshape(D, H * NREL), "rk_block_first": rk_block_first.reshape(D, H * NREL),
        "rv_block": chunks(fill(rv_block)), "rv_block_first": chunks(fill(rv_block_first)),
        "exp_w1": f("L0_ffn_exp_W1"), "exp_w2": f("L0_ffn_exp_W2").reshape(E, HID // P, P, D).transpose(0, 2, 1, 3),
        "exp_b2": f("L0_ffn_exp_b2"), "sim": f("L1_ffn_sim"),
        "up": np.concatenate([f(f"L1_ffn_Wu{i}").T for i in range(NE1)], 0),
    }


def kernel(**inputs):
    import concourse.bacc as bacc
    from concourse.bass_utils import run_bass_kernel_spmd

    nc = bacc.Bacc("TRN2", target_bir_lowering=False, num_devices=1)
    arrays, args = {}, {}
    for name, a in layout(inputs).items():
        arrays[f"in_{name}"] = a = np.ascontiguousarray(a)
        args[name] = nc.dram_tensor(f"in_{name}", a.shape, mybir.dt.from_np(a.dtype), kind="ExternalInput").ap()
    out = nc.dram_tensor("out", (B, S, D), F32, kind="ExternalOutput").ap()
    recurrent_block_kernel(nc, out, **args)
    result = run_bass_kernel_spmd(nc, [arrays], core_ids=[0])
    return result.results[0]["out"]
```

```python
from contextlib import ExitStack

import numpy as np
import concourse.bass as bass
import concourse.mybir as mybir

F32 = mybir.dt.float32
BF16 = mybir.dt.bfloat16
U32 = mybir.dt.uint32
ALU = mybir.AluOpType
ACT = mybir.ActivationFunctionType
AX = mybir.AxisListType

P = 128
B, S, D = 2, 1024, 128
T = B * S
NT = T // P
NS = S // P
H, DK = 16, 8
BH = B * H
REL = 32
NREL = 2 * REL + 1
WIN = P + 2 * REL
E, HID = 8, 512
LH, LD = 16, 64
DF = 512
PROJ, NE1 = 32, 4
RANKS = [1, 2, 4, 8]
RSUM = sum(RANKS)
WARM = 3
BANK = 512
QUAD = BANK // P
BY_REL_SLOTS = 4
RING = 4
EPS = 1e-5
MASKED = -1e38
PIECES = 3
QROWS = 6 * DK
AROWS = 96
SROWS = AROWS + PIECES
VCOLS = DK + 1 + NS
RPAD = P
RROW = RPAD + BH * NREL

COLS = ["ln1_g", "ln1_b", "ln2_g", "ln2_b", "bq", "bk", "rk_first", "rk_last",
        "l1_ln1_g", "l1_ln1_b", "l1_ln2_g", "l1_ln2_b"]
COL = {name: n for n, name in enumerate(COLS)}
EXP_B1 = len(COLS)
NCOLS = EXP_B1 + E * HID // P
ROWS = {}
_at = 0
for _name, _n in [("b_o", D), ("bv", D), ("bp", D), ("gate_b", E), ("rv_first", D), ("rv_last", D),
                  ("router_b", PROJ), ("temp", 1), ("slots", E)]:
    ROWS[_name] = (_at, _n)
    _at += _n
NROWS = _at
MATS = {}
_at = 0
for _name, _n in [("r_q", D), ("r_k", D), ("r_v", D), ("r_o", D), ("c_q", D), ("c_k", D), ("c_v", D),
                  ("c_p", D), ("gate", E)]:
    MATS[_name] = (_at, _n)
    _at += _n
NMATS = _at
MATS1 = {}
_at = 0
for _name, _n in [("l_q", LH * LD), ("l_k", LH * LD), ("l_v", LH * LD), ("l_o", LH * LD), ("f1", DF),
                  ("f2", DF), ("base", D), ("router", PROJ), ("down", RSUM)]:
    MATS1[_name] = (_at, _n)
    _at += _n
NMATS1 = _at
RCH = (H * NREL + P - 1) // P
RGROUPS = [(0, 6), (6, 11), (11, 16)]


def chained(eng, sem, start=0):
    done = [0]

    def link(ins):
        done[0] += 1
        ins.then_inc(sem, 1)
        eng.wait_ge(sem, start + done[0])

    link.done = done
    return link


def warm_up(nc, out, G):
    for _ in range(WARM):
        nc.tensor.matmul(out, G.ident[:, :], G.xt[:, :, :].rearrange("p t d -> p (t d)")[:, 0:out.shape[1]],
                         start=True, stop=True)


class Named(dict):
    __getattr__ = dict.__getitem__
    __setattr__ = dict.__setitem__


def norm_stats_tensors(sb, tag):
    return Named(
        stats=sb(f"{tag}_stats", [P, NT, 6], F32), mean_var=sb(f"{tag}_mean_var", [P, NT, 2], F32),
        var=sb(f"{tag}_var", [P, NT], F32), std=sb(f"{tag}_std", [P, NT], F32),
        rstd=sb(f"{tag}_rstd", [P, NT], F32), tmp=sb(f"{tag}_tmp", [P, NT], F32))


def layer_norm(nc, dve, link, N, src, dst, var_ready, std_ready, turn, ready):
    for t in range(NT):
        last = nc.vector.bn_stats(N.stats[:, t, :], src[:, t, :])
    link(last)
    for t in range(NT):
        last = nc.vector.bn_aggr(N.mean_var[:, t, :], N.stats[:, t, :])
    link(last)
    nc.vector.tensor_scalar(N.var[:, :], N.mean_var[:, :, 1], EPS, None, ALU.add).then_inc(var_ready, 1)
    dve.wait_ge(std_ready, turn)
    link(nc.vector.reciprocal(N.rstd[:, :], N.std[:, :]))
    link(nc.vector.tensor_tensor(N.tmp[:, :], N.rstd[:, :], N.rstd[:, :], ALU.mult))
    link(nc.vector.tensor_tensor(N.tmp[:, :], N.tmp[:, :], N.var[:, :], ALU.mult))
    link(nc.vector.tensor_scalar(N.tmp[:, :], N.tmp[:, :], -0.5, 1.5, ALU.mult, ALU.add))
    link(nc.vector.tensor_tensor(N.rstd[:, :], N.rstd[:, :], N.tmp[:, :], ALU.mult))
    for t in range(NT):
        last = nc.vector.tensor_scalar(dst[:, t, :], src[:, t, :], N.mean_var[:, t, 0:1], N.rstd[:, t:t + 1],
                                       ALU.subtract, ALU.mult)
        if t % QUAD == QUAD - 1:
            last.then_inc(ready, 1)


def layer_norm_root(nc, act, N, var_ready, std_ready, turn):
    act.wait_ge(var_ready, turn)
    nc.scalar.activation(N.std[:, :], N.var[:, :], ACT.Sqrt).then_inc(std_ready, 1)


def stage_normalize(nc, G, M, tag, gain, bias, first):
    with ExitStack() as ctx:
        def sb(name, shape, dt=F32):
            return ctx.enter_context(nc.sbuf_tensor(name, shape, dt))

        def sem(name):
            return ctx.enter_context(nc.semaphore(name))

        N = norm_stats_tensors(sb, tag)
        xnn = sb(f"{tag}_xnn", [P, NT, D])
        xn_ps = [ctx.enter_context(nc.psum_tensor(f"{tag}_xn_ps{i}", [P, BANK], F32)) for i in range(2)]
        h1_ps = [ctx.enter_context(nc.psum_tensor(f"{tag}_h1_ps{i}", [P, BANK], F32)) for i in range(2)]
        x_in = sem(f"{tag}_x_in")
        par_in = sem(f"{tag}_par_in")
        chain = sem(f"{tag}_chain")
        var_ready = sem(f"{tag}_var_ready")
        std_ready = sem(f"{tag}_std_ready")
        xn_ready = sem(f"{tag}_xn_ready")
        ident0 = sem(f"{tag}_ident0")
        ident_ready = sem(f"{tag}_ident_ready")
        xn_turned = sem(f"{tag}_xn_turned")
        h1_turned = sem(f"{tag}_h1_turned")
        xn_kept = sem(f"{tag}_xn_kept")
        h1_kept = sem(f"{tag}_h1_kept")
        block = ctx.enter_context(nc.Block())

        @block.sync
        def _(sp):
            if not first:
                return
            sp.dma_start(G.xt[:, :, :], M.x.rearrange("(t p) d -> p t d", p=P)).then_inc(x_in, 16)
            sp.dma_start(G.cols[:, :], M.cols).then_inc(par_in, 16)
            sp.dma_start(G.rows[:, :], M.rows.partition_broadcast(P)).then_inc(par_in, 16)
            sp.dma_start(G.mats[:, :], M.mats).then_inc(par_in, 16)
            sp.wait_ge(par_in, 48)

        @block.gpsimd
        def _(pool):
            if not first:
                return
            nc.gpsimd.memset(G.zeros[:, :], 0.0).then_inc(ident0, 1)
            nc.gpsimd.memset(G.ident[:, :], 0.0).then_inc(ident0, 1)
            nc.gpsimd.memset(G.identb[:, :], 0.0).then_inc(ident0, 1)
            nc.gpsimd.memset(G.mask_ij[:, :], 0.0).then_inc(ident0, 1)
            nc.gpsimd.memset(G.mask_ji[:, :], 0.0).then_inc(ident0, 1)
            for m in (G.causal01[:, :], G.far_sign[:, 0:P - REL], G.before_last[:, :], G.after_first[:, :]):
                nc.gpsimd.memset(m, 1.0).then_inc(ident0, 1)
            nc.gpsimd.memset(G.far_sign[:, P - REL:P], 0.0).then_inc(ident0, 1)
            pool.wait_ge(ident0, 10)
            for m in (G.ident, G.identb):
                nc.gpsimd.affine_select(out=m[:, :], in_=m[:, :], compare_op=ALU.not_equal, fill=1.0, base=0,
                                        pattern=[[-1, P]], channel_multiplier=1).then_inc(ident_ready, 1)
            nc.gpsimd.affine_select(out=G.mask_ij[:, :], in_=G.mask_ij[:, :], compare_op=ALU.is_ge, fill=MASKED,
                                    base=0, pattern=[[-1, P]], channel_multiplier=1).then_inc(ident_ready, 1)
            nc.gpsimd.affine_select(out=G.mask_ji[:, :], in_=G.mask_ji[:, :], compare_op=ALU.is_ge, fill=MASKED,
                                    base=0, pattern=[[1, P]], channel_multiplier=-1).then_inc(ident_ready, 1)
            nc.gpsimd.affine_select(out=G.causal01[:, :], in_=G.causal01[:, :], compare_op=ALU.is_ge, fill=0.0,
                                    base=0, pattern=[[1, P]], channel_multiplier=-1).then_inc(ident_ready, 1)
            for cols, fill in ((slice(0, P - REL), 0.0), (slice(P - REL, P), -1.0)):
                nc.gpsimd.affine_select(out=G.far_sign[:, cols], in_=G.far_sign[:, cols], compare_op=ALU.is_ge,
                                        fill=fill, base=cols.start, pattern=[[1, cols.stop - cols.start]],
                                        channel_multiplier=-1).then_inc(ident_ready, 1)
            nc.gpsimd.affine_select(out=G.before_last[:, :], in_=G.before_last[:, :], compare_op=ALU.is_gt,
                                    fill=0.0, base=0, pattern=[[-1, P]],
                                    channel_multiplier=1).then_inc(ident_ready, 1)
            nc.gpsimd.affine_select(out=G.after_first[:, :], in_=G.after_first[:, :], compare_op=ALU.is_gt,
                                    fill=0.0, base=0, pattern=[[1, P]],
                                    channel_multiplier=-1).then_inc(ident_ready, 1)

        @block.vector
        def _(dve):
            link = chained(dve, chain)
            if first:
                dve.wait_ge(x_in, 16)
            layer_norm(nc, dve, link, N, G.xt, G.xn, var_ready, std_ready, 1, xn_ready)
            dve.wait_ge(xn_ready, QUAD)
            layer_norm(nc, dve, link, N, G.xn, xnn, var_ready, std_ready, 2, xn_ready)
            if first:
                dve.wait_ge(par_in, 48)
            for c in range(QUAD):
                dve.wait_ge(h1_turned, c + 1)
                nc.vector.tensor_scalar(G.h1T[:, c * BANK:(c + 1) * BANK], h1_ps[c % 2][:, :],
                                        G.col(gain), G.col(bias), ALU.mult, ALU.add).then_inc(h1_kept, 1)

        @block.scalar
        def _(act):
            layer_norm_root(nc, act, N, var_ready, std_ready, 1)
            layer_norm_root(nc, act, N, var_ready, std_ready, 2)
            for c in range(QUAD):
                act.wait_ge(xn_turned, c + 1)
                nc.scalar.copy(G.xnT[:, c * BANK:(c + 1) * BANK], xn_ps[c % 2][:, :]).then_inc(xn_kept, 1)

        @block.tensor
        def _(pe):
            if first:
                pe.wait_ge(ident_ready, 2)
            for src, ps, ready, turned, kept in ((G.xn, xn_ps, 0, xn_turned, xn_kept),
                                                 (xnn, h1_ps, QUAD, h1_turned, h1_kept)):
                if ready:
                    warm_up(nc, h1_ps[1][:, :], G)
                for c in range(QUAD):
                    pe.wait_ge(xn_ready, ready + c + 1)
                    if c >= 2:
                        pe.wait_ge(kept, c - 1)
                    for k in range(QUAD):
                        last = nc.tensor.transpose(ps[c % 2][:, k * P:(k + 1) * P], src[:, c * QUAD + k, :],
                                                   G.ident[:, :])
                    last.then_inc(turned, 1)


def load_head(sp, G, M, relative, n, u, parts=range(PIECES)):
    q_array, k_arrays = (0, (1, 2)) if relative else (3, (4,))
    loaded = (G.r_loaded if relative else G.c_loaded)[u]
    piece_size = B * P * S

    def rows(array, piece, step, count):
        return bass.AP(M.split.tensor, (array * PIECES + piece) * piece_size + n * (DK * S),
                       [[step, count], [S, DK], [1, S]])

    for piece in parts:
        r, reps = (0, 3 * DK, 5 * DK)[piece], PIECES - piece
        sp.dma_start(G.q[r:r + reps * DK, u, :], rows(q_array, 0, piece_size, reps)).then_inc(loaded, 16)
        for i, array in enumerate(k_arrays):
            sp.dma_start(G.ks[r:r + reps * DK, u, i, :], rows(array, piece, 0, reps)).then_inc(loaded, 16)


def load_rel(sp, G, M, n, u):
    sp.dma_start(G.rel[:, u, :, :],
                 bass.AP(M.rel.tensor, RPAD + n * NREL, [[RROW - 1, P], [P * RROW, NS], [1, WIN]])
                 ).then_inc(G.rel_loaded[u], 16)


def fill_far(ops, G, n, u, link):
    rel, edge = G.rel, G.rel_edge[:, u, :].unsqueeze(2)
    link(ops.tensor_copy(G.rel_edge[:, u, :], G.rel_last[:, :, :, :].rearrange(
        "p b h t -> p (b h t)")[:, bass.ds(n * NS, NS)]))
    link(ops.tensor_tensor(rel[:, u, :, 2 * REL:WIN], rel[:, u, :, 2 * REL:WIN],
                                 edge.to_broadcast([P, NS, P]), ALU.subtract))
    link(ops.tensor_tensor(rel[:, u, :, 2 * REL:WIN], rel[:, u, :, 2 * REL:WIN],
                                 G.before_last[:, :].unsqueeze(1).to_broadcast([P, NS, P]), ALU.mult))
    link(ops.tensor_tensor(rel[:, u, :, 2 * REL:REL + P], rel[:, u, :, 2 * REL:REL + P],
                                 edge.to_broadcast([P, NS, P - REL]), ALU.add))
    assert link.done[0] == 4
    return ops.tensor_tensor(rel[:, u, :, 0:P], rel[:, u, :, 0:P],
                                   G.after_first[:, :].unsqueeze(1).to_broadcast([P, NS, P]), ALU.mult)


def stage_project(nc, G, M):
    inv = 1.0 / float(np.sqrt(DK))
    with ExitStack() as ctx:
        def sb(name, shape, dt=F32):
            return ctx.enter_context(nc.sbuf_tensor(name, shape, dt))

        def sem(name):
            return ctx.enter_context(nc.semaphore(name))

        proj = G.proj
        rest = sb("rest", [P, T])
        pieces = sb("pieces", [P, 2, PIECES, T], BF16)
        bq_scaled = sb("bq_scaled", [P, 1])
        RSLOTS = 4
        rel_w = G.catt[:, :, :, :].rearrange("p n j v -> p (n j v)")[:, 0:2 * H * NREL].rearrange(
            "p (i c) -> p i c", i=2)
        rel_sb = G.att[:, :, :, :].rearrange("p n j v -> p (n j v)")[:, 0:RSLOTS * H * NREL].rearrange(
            "p (i h r) -> p i h r", i=RSLOTS, h=H)
        proj_ps = [ctx.enter_context(nc.psum_tensor(f"proj_ps{i}", [P, BANK], F32)) for i in range(2)]
        v_ps = [ctx.enter_context(nc.psum_tensor(f"v_ps{i}", [P, BANK], F32)) for i in range(2)]
        rel_ps = [ctx.enter_context(nc.psum_tensor(f"rel_ps{i}", [P, BANK], F32)) for i in range(3)]
        rel_w_in = sem("p_rel_w_in")
        rel_w_ready = sem("p_rel_w_ready")
        bias_ready = sem("p_bias_ready")
        projected = sem("p_projected")
        proj_kept = sem("p_proj_kept")
        chain = sem("p_chain")
        cut = sem("p_cut")
        pieces_stored = [sem(f"p_pieces_stored{i}") for i in range(2)]
        v_projected = sem("p_v_projected")
        v_kept = sem("p_v_kept")
        scored = sem("p_scored")
        rel_kept = sem("p_rel_kept")
        last_kept = sem("p_last_kept")
        rel_stored = [sem(f"p_rel_stored{i}") for i in range(RSLOTS)]
        pad_stored = sem("p_pad_stored")
        slot_ready = sem("p_slot_ready")
        pool_chain = sem("p_pool_chain")
        dve_chain = sem("p_dve_chain")
        columns_ready = sem("p_columns_ready")
        block = ctx.enter_context(nc.Block())
        plan = [("r_q", G.xnT, 1), ("r_k", G.xnT, 2), ("c_q", G.h1T, 1), ("c_k", G.h1T, 1)]
        STORES_AT = (3, 6, 10)
        VALUES_AT = [(12, 13, 14, 15)[v // 4] for v in range(NT)]
        REL_AT = 11
        HEAD_AT = 13
        kept_after = [4, 12, 12, 16, 20]

        @block.sync
        def _(sp):
            sp.dma_start(rel_w[:, 0, :], M.rk_block).then_inc(rel_w_in, 16)
            sp.dma_start(rel_w[:, 1, :], M.rk_block_first).then_inc(rel_w_in, 16)
            sp.dma_start(bass.AP(M.rel.tensor, 0, [[RROW, P], [P * RROW, NS], [1, RPAD]]),
                         G.zeros[:, :].unsqueeze(1).to_broadcast([P, NS, RPAD])).then_inc(pad_stored, 16)

            def store_pieces(a):
                sp.wait_ge(cut, a + 1)
                sp.dma_start(M.split[a].rearrange("c b p s -> p c b s"),
                             pieces[:, a % 2, :, :].rearrange("p c (b s) -> p c b s", b=B)
                             ).then_inc(pieces_stored[a % 2], 16)

            store_pieces(0)
            store_pieces(1)
            for t in range(NT):
                b, tile = divmod(t, NS)
                sp.wait_ge(rel_kept, (t + 1) * len(RGROUPS))
                sp.dma_start(bass.AP(M.rel.tensor, tile * P * RROW + RPAD + b * H * NREL,
                                     [[RROW, P], [1, H * NREL]]),
                             rel_sb[:, t % RSLOTS, :, :].rearrange("p h r -> p (h r)")).then_inc(
                                 rel_stored[t % RSLOTS], 16)
                if t in STORES_AT:
                    store_pieces(2 + STORES_AT.index(t))
                if t == HEAD_AT:
                    sp.wait_ge(pieces_stored[0], 32)
                    sp.wait_ge(pieces_stored[1], 16)
                    sp.wait_ge(slot_ready, 2 * RING)
                if HEAD_AT <= t < HEAD_AT + PIECES:
                    load_head(sp, G, M, True, 0, 0, [t - HEAD_AT])
                if t == REL_AT:
                    sp.wait_ge(cut, 4)
                    sp.wait_ge(pad_stored, 16)
                    for i in range(RSLOTS):
                        sp.wait_ge(rel_stored[i], 16 * (NS // RSLOTS))
                if REL_AT <= t < REL_AT + 2:
                    load_rel(sp, G, M, t - REL_AT, t - REL_AT)
            load_head(sp, G, M, True, 1, 1)
            sp.wait_ge(pieces_stored[0], 48)
            sp.wait_ge(pieces_stored[1], 32)
            for i in range(RSLOTS):
                sp.wait_ge(rel_stored[i], 16 * (NT // RSLOTS))

        @block.gpsimd
        def _(pool):
            pool.wait_ge(rel_w_in, 32)
            nc.gpsimd.tensor_tensor(rel_w[:, 0, :], rel_w[:, 0, :], rel_w[:, 1, :],
                                    ALU.subtract).then_inc(rel_w_ready, 1)

            def set_columns():
                nc.gpsimd.memset(G.vs[:, :, :, :], 0.0).then_inc(columns_ready, 1)
                pool.wait_ge(columns_ready, 1)
                nc.gpsimd.memset(G.vs[:, :, :, DK:VCOLS], 1.0).then_inc(columns_ready, 1)
                pool.wait_ge(columns_ready, 2)
                for u in range(RING):
                    nc.gpsimd.affine_select(out=G.vs[:, u, :, DK + 1:VCOLS], in_=G.vs[:, u, :, DK + 1:VCOLS],
                                            compare_op=ALU.is_ge, fill=0.0, base=-P,
                                            pattern=[[P, NS], [-P, NS]], channel_multiplier=1
                                            ).then_inc(columns_ready, 1)

            for t in range(NT):
                pool.wait_ge(rel_kept, (t + 1) * len(RGROUPS))
                nc.gpsimd.tensor_copy(G.rel_last[:, t // NS, :, t % NS], rel_sb[:, t % RSLOTS, :, NREL - 1]
                                      ).then_inc(last_kept, 1)
                if t < RING:
                    nc.gpsimd.memset(G.ks[:, t, :, :], 1.0).then_inc(slot_ready, 1)
                    nc.gpsimd.memset(G.q[:, t, :], 0.0).then_inc(slot_ready, 1)
                if t == RING:
                    set_columns()
            pool.wait_ge(G.rel_loaded[1], 16)
            fill_far(nc.gpsimd, G, 1, 1, chained(pool, pool_chain, 0))

        @block.scalar
        def _(act):
            nc.scalar.mul(bq_scaled[:, :], G.col("bq"), inv).then_inc(bias_ready, 1)
            act.wait_ge(bias_ready, 1)
            n = 0
            for i in range(4):
                for c in range(QUAD):
                    act.wait_ge(projected, n + 1)
                    ps, cols = proj_ps[n % 2], slice(c * BANK, (c + 1) * BANK)
                    n += 1
                    if i == 0:
                        nc.scalar.activation(proj[:, 0, cols], ps[:, :], ACT.Identity, scale=inv
                                             ).then_inc(proj_kept, 1)
                    elif i == 1:
                        nc.scalar.activation(proj[:, 1, cols], ps[:, :], ACT.Identity,
                                             bias=G.col("rk_first")).then_inc(proj_kept, 1)
                        nc.scalar.activation(proj[:, 2, cols], ps[:, :], ACT.Identity,
                                             bias=G.col("rk_last")).then_inc(proj_kept, 1)
                    elif i == 2:
                        nc.scalar.activation(proj[:, 3, cols], ps[:, :], ACT.Identity, bias=bq_scaled[:, :],
                                             scale=inv).then_inc(proj_kept, 1)
                    else:
                        nc.scalar.activation(proj[:, 4, cols], ps[:, :], ACT.Identity,
                                             bias=G.col("bk")).then_inc(proj_kept, 1)
            for t in range(NT):
                if t >= RSLOTS:
                    act.wait_ge(rel_stored[t % RSLOTS], 16 * (t // RSLOTS))
                    act.wait_ge(last_kept, t - RSLOTS + 1)
                for g, (h0, h1) in enumerate(RGROUPS):
                    act.wait_ge(scored, t * len(RGROUPS) + g + 1)
                    nc.scalar.copy(rel_sb[:, t % RSLOTS, h0:h1, :],
                                   rel_ps[g][:, 0:(h1 - h0) * NREL].rearrange("p (h r) -> p h r", r=NREL)
                                   ).then_inc(rel_kept, 1)

        @block.vector
        def _(dve):
            link = chained(dve, chain)
            for a in range(5):
                dve.wait_ge(proj_kept, kept_after[a])
                if a >= 2:
                    dve.wait_ge(pieces_stored[a % 2], 16 * (a // 2))
                src, hi, mid, lo = proj[:, a, :], *(pieces[:, a % 2, i, :] for i in range(PIECES))
                link(nc.vector.tensor_copy(hi, src))
                link(nc.vector.tensor_tensor(rest[:, :], src, hi, ALU.subtract))
                link(nc.vector.tensor_copy(mid, rest[:, :]))
                nc.vector.tensor_tensor(lo, rest[:, :], mid, ALU.subtract).then_inc(cut, 1)
                dve.wait_ge(cut, a + 1)
            for t in range(NT):
                b, tile = divmod(t, NS)
                heads = slice(b * H, (b + 1) * H)
                dve.wait_ge(v_projected, t + 1)
                v_rel = v_ps[t % 2][:, 0:D].rearrange("p (h d) -> p h d", d=DK)
                v_causal = v_ps[t % 2][:, D:2 * D].rearrange("p (h d) -> p h d", d=DK)
                nc.vector.tensor_tensor(G.v_rel[:, heads, tile, :], v_rel,
                                        G.row("rv_first").rearrange("p (h d) -> p h d", d=DK), ALU.add)
                nc.vector.tensor_tensor(G.v_causal[:, heads, tile, :], v_causal,
                                        G.row("bv").rearrange("p (h d) -> p h d", d=DK), ALU.add).then_inc(v_kept, 1)
            dve.wait_ge(G.rel_loaded[0], 16)
            dve.wait_ge(last_kept, NS)
            fill_far(nc.vector, G, 0, 0, chained(dve, dve_chain, 0))

        @block.tensor
        def _(pe):
            n = 0
            for name, src, _copies in plan:
                for c in range(QUAD):
                    if n >= 2:
                        pe.wait_ge(proj_kept, [1, 2, 3, 4, 6, 8, 10, 12, 13, 14, 15, 16, 17, 18, 19, 20][n - 2])
                    nc.tensor.matmul(proj_ps[n % 2][:, :], G.mat(name), src[:, c * BANK:(c + 1) * BANK],
                                     start=True, stop=True).then_inc(projected, 1)
                    n += 1

            def values(t):
                if t >= 2:
                    pe.wait_ge(v_kept, t - 1)
                nc.tensor.matmul(v_ps[t % 2][:, 0:D], G.xnT[:, t * P:(t + 1) * P], G.mat("r_v"),
                                 start=True, stop=True)
                nc.tensor.matmul(v_ps[t % 2][:, D:2 * D], G.h1T[:, t * P:(t + 1) * P], G.mat("c_v"),
                                 start=True, stop=True).then_inc(v_projected, 1)

            pe.wait_ge(rel_w_ready, 1)
            for t in range(NT):
                for g, (h0, h1) in enumerate(RGROUPS):
                    if t >= 1:
                        pe.wait_ge(rel_kept, (t - 1) * len(RGROUPS) + g + 1)
                    nc.tensor.matmul(rel_ps[g][:, 0:(h1 - h0) * NREL], proj[:, 0, t * P:(t + 1) * P],
                                     rel_w[:, 0, h0 * NREL:h1 * NREL], start=True, stop=True).then_inc(scored, 1)
                for v in range(NT):
                    if VALUES_AT[v] == t:
                        values(v)
            pe.wait_ge(proj_kept, kept_after[-1])
            for _ in range(3):
                warm_up(nc, proj_ps[0][:, :], G)




def await_count(eng, sem, value):
    if not isinstance(value, int) or value > 0:
        eng.wait_ge(sem, value)


def clear_semaphores(nc, numbers):
    with nc.Block() as block:
        @block.sync
        def _(sp):
            sp.sem_clear(numbers)


def load_by_rel(sp, G, M, t):
    b, tile = divmod(t, NS)
    sp.dma_start(G.by_rel[:, t % BY_REL_SLOTS, :, 0:NREL - 1],
                 bass.AP(M.window.tensor, b * H * S * WIN + tile * P * WIN,
                         [[WIN + 1, P], [S * WIN, H], [1, NREL - 1]])).then_inc(
                         G.by_rel_in[t % BY_REL_SLOTS], 16)


def over_heads(eng, head):
    for u in range(RING):
        head(u, 0, u, u)
    with eng.Fori(1, BH // RING - 1) as k:
        for u in range(RING):
            head(k * RING + u, k, u, RING + u)
    last = BH // RING - 1
    for u in range(RING):
        head(last * RING + u, last, u, last * RING + u)


def stage_attention(nc, G, M, relative):
    tag = "r" if relative else "c"
    LOADS = 3 * (3 if relative else 2)
    halves = [(i, hf, hf * BANK, min((hf + 1) * BANK, S if relative else (i + 1) * P))
              for i in range(NS) for hf in range(2) if relative or hf * BANK < (i + 1) * P]
    NA = len(halves)
    share = [3, 2, 2, 2, 1, 2, 2, 2] if relative else [2, 2, 2, 1, 1, 1, 2, 1]
    SPLIT = 3 if relative else 1
    EARLY = sum(share[SPLIT:])
    beside = [list(range(EARLY + sum(share[:j]), EARLY + sum(share[:j + 1]))) for j in range(SPLIT)]
    beside += [list(range(sum(share[SPLIT:j]), sum(share[SPLIT:j + 1]))) for j in range(SPLIT, NS)]
    assert sum(share) == NA
    A_BANKS = 2 if relative else 3
    MAX_AT = 4 if relative else 3
    STEPS_AFTER = ((1, 2), (3, 4))
    FIRST_TURNS = NA + EARLY + 1
    PER_HEAD = NA + 2

    def items(at):
        for j in range(NS):
            ahead = 1 if j < SPLIT else 2
            row = [("piece", x, ahead) for x in beside[j] if at + ahead < BH]
            row += [("sums", 0, -1)] if j == 2 and at >= 1 else []
            row += [("max", 0, 1)] if j == MAX_AT and at + 1 < BH else []
            yield row

    def turns(n, at):
        first = FIRST_TURNS - (1 if at >= 1 else 0) - (EARLY if at == BH - 1 else 0)
        before = sum(len(row) for row in items(at - 1)) if at else FIRST_TURNS
        out, i = [], 0
        for row in items(at):
            out.append([])
            for item in row:
                back = A_BANKS if i >= A_BANKS else i + 1 + (before - 1 - i) % A_BANKS
                out[-1].append((*item, n * PER_HEAD + first + i, i % A_BANKS,
                                n * PER_HEAD + first + i - back + 1))
                i += 1
        return out

    LAST_TURN = turns(BH - 1, BH - 1)[2][-1][3] + 1

    with ExitStack() as ctx:
        def sb(name, shape, dt=F32):
            return ctx.enter_context(nc.sbuf_tensor(f"{tag}_{name}", shape, dt))

        def sem(name):
            return ctx.enter_context(nc.semaphore(f"{tag}_{name}"))

        q, ks, vs = G.q, G.ks, G.vs
        probs = sb("probs", [P, NS, S])
        half_max = sb("half_max", [P, 2, NS, 2])
        row_max = sb("row_max", [P, NS])
        neg_rest = sb("neg_rest", [P, NS])
        neg_max = sb("neg_max", [P, PIECES, NS], BF16)
        neg_maxT = sb("neg_maxT", [PIECES * NS, 2, P], BF16)
        a_ps = [ctx.enter_context(nc.psum_tensor(f"{tag}_a_ps{i}", [P, BANK], F32))
                for i in range(A_BANKS)]
        b_ps = [ctx.enter_context(nc.psum_tensor(f"{tag}_b_ps{i}", [P, S], F32)) for i in range(2)]
        sumT = sb("sumT", [P, 2, P])
        o_ps = ctx.enter_context(nc.psum_tensor(f"{tag}_o_ps", [P, 2, P], F32))
        if relative:
            rel = G.rel
            win_ps = ctx.enter_context(nc.psum_tensor(f"{tag}_win_ps", [P, 2, WIN], F32))
            win_sb = [flat[:, :, :].rearrange("p t d -> p (t d)")[:, 0:NS * WIN].rearrange(
                "p (j w) -> p j w", j=NS) for flat in (G.mixer, G.x2)]
            far_sb = sb("far_sb", [P, NS, P])
        loaded = G.r_loaded if relative else G.c_loaded
        max_in = [sem(f"max_in{i}") for i in range(RING)]
        values_ready = sem("values_ready")
        rel_ready = sem("rel_ready")
        pool_chain = sem("pool_chain")
        chain = sem("chain")
        a_scored = sem("a_scored")
        a_used = sem("a_used")
        b_scored = sem("b_scored")
        exp_done = sem("exp_done")
        pv_done = sem("pv_done")
        sum_kept = sem("sum_kept")
        floor_ready = sem("floor_ready")
        win_kept = sem("win_kept")
        win_stored = G.win_stored
        far_masked = sem("far_masked")
        far_summed = sem("far_summed")
        block = ctx.enter_context(nc.Block())

        @block.sync
        def _(sp):
            def maxima(n, u, turn):
                sp.wait_ge(a_used, turn + 1)
                sp.dma_start(q[AROWS:SROWS, u, :], neg_maxT[:, u % 2, :]).then_inc(max_in[u], 16)

            def store_window(n, u):
                sp.wait_ge(win_kept, n * 4 + 4)
                sp.dma_start(bass.AP(M.window.tensor, n * (S * WIN), [[WIN, P], [P * WIN, NS], [1, WIN]]),
                             win_sb[u % 2][:, :, :]).then_inc(win_stored[u % 2], 16)

            def head(n, k, u, at):
                if at + 3 < BH:
                    if at >= 1:
                        sp.wait_ge(pv_done, n * NS)
                    if relative:
                        load_rel(sp, G, M, n + 3, (u + 3) % RING)
                    load_head(sp, G, M, relative, n + 3, (u + 3) % RING)
                elif relative:
                    sp.wait_ge(pv_done, n * NS)
                    load_head(sp, G, M, False, n + 3 - BH, (u + 3) % RING)
                if relative and at >= 1:
                    store_window(n - 1, (u - 1) % RING)
                if at + 1 < BH:
                    turn = [item[3] for row in turns(n, at) for item in row if item[0] == "max"][0]
                    maxima(n + 1, (u + 1) % RING, turn)

            if relative:
                load_rel(sp, G, M, 2, 2)
                load_head(sp, G, M, True, 2, 2)
            maxima(0, 0, FIRST_TURNS - 1)
            over_heads(sp, head)
            if relative:
                store_window(BH - 1, RING - 1)
            else:
                for i in range(2):
                    sp.wait_ge(win_stored[i], 16 * (BH // 2))
                for i, source in enumerate((M.rv_block, M.rv_block_first)):
                    sp.dma_start(G.rv_w[:, i, :, :], source.rearrange("p (c d) -> p c d", d=D)
                                 ).then_inc(G.rv_in, 16)
                for t in range(BY_REL_SLOTS):
                    load_by_rel(sp, G, M, t)

        @block.gpsimd
        def _(pool):
            def prepare(n, k, u, at):
                if at >= RING:
                    pool.wait_ge(pv_done, (n - RING + 1) * NS)
                values = G.v_rel if relative else G.v_causal
                nc.gpsimd.tensor_copy(vs[:, u, :, 0:DK], values[:, :, :, :].rearrange("p n j d -> p (n j d)")[
                    :, bass.ds(n * (NS * DK), NS * DK)].rearrange("p (j d) -> p j d", d=DK)
                                      ).then_inc(values_ready, 1)
                if relative and at >= 2:
                    pool.wait_ge(G.rel_loaded[u], 16 * (k + 1))
                    fill_far(nc.gpsimd, G, n, u, chained(pool, pool_chain, n * 4 - 8)).then_inc(rel_ready, 1)

            def mask_far(n, u, at):
                pool.wait_ge(win_kept, n * 4 + 4)
                if at >= 1:
                    pool.wait_ge(far_summed, n)
                nc.gpsimd.tensor_tensor(far_sb[:, :, :], win_sb[u % 2][:, :, 2 * REL:WIN],
                                        G.far_sign[:, :].unsqueeze(1).to_broadcast([P, NS, P]), ALU.mult
                                        ).then_inc(far_masked, 1)

            def head(n, k, u, at):
                if relative and at >= 1:
                    mask_far(n - 1, (u - 1) % RING, at - 1)
                if at + 3 < BH:
                    prepare(n + 3, k + (u + 3) // RING, (u + 3) % RING, at + 3)

            for n in range(3):
                prepare(n, 0, n, n)
            over_heads(pool, head)
            if not relative:
                pool.wait_ge(G.rv_in, 32)
                nc.gpsimd.tensor_tensor(G.rv_w[:, 0, :, :], G.rv_w[:, 0, :, :], G.rv_w[:, 1, :, :],
                                        ALU.subtract).then_inc(G.rv_ready, 1)

        @block.scalar
        def _(act):
            def keep_window(n, k, u, at, pair):
                act.wait_ge(pv_done, n * NS + min(2 * pair + 3, NS))
                if pair == 0 and at >= 2:
                    act.wait_ge(win_stored[u % 2], k * 32 + 16 * (u // 2))
                    act.wait_ge(far_masked, n - 1)
                nc.scalar.copy(win_sb[u % 2][:, 2 * pair:2 * pair + 2, :],
                               win_ps[:, :, :]).then_inc(win_kept, 1)

            def keep_sums(n):
                act.wait_ge(pv_done, n * NS + NS)
                nc.scalar.copy(sumT[:, :, :], o_ps[:, :, :]).then_inc(sum_kept, 1)

            def last_head(n, k, u, at):
                if relative:
                    keep_window(n, k, u, at, 3)
                keep_sums(n)

            def head(n, k, u, at):
                for j in range(NS):
                    act.wait_ge(b_scored, n * NS + j + 1)
                    if at >= 1:
                        act.wait_ge(pv_done, (n - 1) * NS + (min(j + 3, NS) if relative else j + 1))
                    lo = 0 if relative else j * P
                    nc.scalar.activation(probs[:, j, lo:S], b_ps[j % 2][:, lo:S], ACT.Exp).then_inc(exp_done, 1)
                    if relative and j in (3, 5, 7):
                        keep_window(n, k, u, at, (j - 3) // 2)
                    if j == 0 and at >= 1:
                        last_head(n - 1, k - 1 if u == 0 else k, (u - 1) % RING, at - 1)

            over_heads(act, head)
            last_head(BH - 1, BH // RING - 1, RING - 1, BH - 1)

        @block.vector
        def _(dve):
            def max_piece(u, x, turn, bank):
                i, hf, lo, hi = halves[x]
                dve.wait_ge(a_scored, turn + 1)
                nc.vector.tensor_reduce(half_max[:, u % 2, i, hf:hf + 1], a_ps[bank][:, 0:hi - lo], AX.X,
                                        ALU.max).then_inc(a_used, 1)

            def negate_max(n, u, step):
                if step:
                    dve.wait_ge(chain, n * 5 + step)
                if step == 0:
                    out = nc.vector.tensor_tensor(row_max[:, :], half_max[:, u % 2, :, 0], half_max[:, u % 2, :, 1], ALU.max)
                elif step == 1:
                    out = nc.vector.tensor_scalar(neg_max[:, 0, :], row_max[:, :], -1.0, None, ALU.mult)
                elif step == 2:
                    out = nc.vector.scalar_tensor_tensor(neg_rest[:, :], row_max[:, :], -1.0, neg_max[:, 0, :],
                                                         ALU.mult, ALU.subtract)
                elif step == 3:
                    out = nc.vector.tensor_copy(neg_max[:, 1, :], neg_rest[:, :])
                else:
                    out = nc.vector.tensor_tensor(neg_max[:, 2, :], neg_rest[:, :], neg_max[:, 1, :],
                                                  ALU.subtract)
                out.then_inc(chain, 1)

            def negate_after_piece(n, u, x):
                for step in STEPS_AFTER[x] if x < len(STEPS_AFTER) else ():
                    negate_max(n, u, step)

            def keep_turned(k, u, at, turn, bank):
                dve.wait_ge(a_scored, turn + 1)
                if at >= 2:
                    dve.wait_ge(max_in[(u + 2) % RING], 16 * k + (16 if u >= 2 else 0))
                nc.vector.tensor_copy(neg_maxT[:, u % 2, :], a_ps[bank][0:PIECES * NS, 0:P // 2].bitcast(
                    BF16)).then_inc(a_used, 1)

            def keep_out(n, turn, bank):
                dve.wait_ge(a_scored, turn + 1)
                att, w = (G.att, VCOLS) if relative else (G.catt, DK + 1)
                nc.vector.tensor_copy(
                    att[:, :, :, :].rearrange("p n t d -> p (n t d)")[:, bass.ds(n * (NS * w), NS * w)].rearrange(
                        "p (c h d) -> p c h d", c=NS // 2, h=2),
                    a_ps[bank][:, 0:2 * P].rearrange("p (h c d) -> p c h d", h=2, d=32)[:, :, :, 0:w]
                    ).then_inc(a_used, 1)

            def sum_far(n):
                dve.wait_ge(far_masked, n + 1)
                nc.vector.tensor_reduce(G.far[:, :, :].rearrange("p n t -> p (n t)")[:, bass.ds(n * NS, NS)],
                                        far_sb[:, :, :], AX.X, ALU.add).then_inc(far_summed, 1)

            def head(n, k, u, at):
                for j, row in enumerate(turns(n, at)):
                    for kind, x, ahead, turn, bank, free in row:
                        if kind == "piece":
                            max_piece(u + ahead, x, turn, bank)
                            if ahead == 2:
                                negate_after_piece(n + 1, u + 1, x)
                        elif kind == "sums":
                            keep_out(n - 1, turn, bank)
                        else:
                            keep_turned(k + (u + 1) // RING, (u + 1) % RING, at + 1, turn, bank)
                    if j == SPLIT - 1 and at + 1 < BH:
                        dve.wait_ge(a_used, row[-1][3] + 1)
                        negate_max(n + 1, u + 1, 0)
                        if at + 2 == BH:
                            for step in range(1, 5):
                                negate_max(n + 1, u + 1, step)
                    if relative and j == 4 and at >= 1:
                        sum_far(n - 1)

            if not relative:
                nc.vector.memset(half_max[:, :, :, 1], -3e38).then_inc(floor_ready, 1)
                dve.wait_ge(floor_ready, 1)
            for x in range(NA):
                max_piece(0, x, x, x % A_BANKS)
            dve.wait_ge(a_used, NA)
            negate_max(0, 0, 0)
            for x in range(EARLY):
                max_piece(1, x, NA + x, (NA + x) % A_BANKS)
                negate_after_piece(0, 0, x)
            keep_turned(0, 0, 0, FIRST_TURNS - 1, (FIRST_TURNS - 1) % A_BANKS)
            over_heads(dve, head)
            keep_out(BH - 1, LAST_TURN, 0)
            if relative:
                dve.wait_ge(win_kept, BH * 4)
                dve.wait_ge(far_summed, BH - 1)
                nc.vector.tensor_tensor(far_sb[:, :, :], win_sb[(BH - 1) % 2][:, :, 2 * REL:WIN],
                                        G.far_sign[:, :].unsqueeze(1).to_broadcast([P, NS, P]), ALU.mult
                                        ).then_inc(far_masked, 1)
                sum_far(BH - 1)

        @block.tensor
        def _(pe):
            def score_piece(u, x, bank, free):
                i, hf, lo, hi = halves[x]
                ps = a_ps[bank]
                await_count(pe, a_used, free)
                lhs = q[0:AROWS, u, i * P:(i + 1) * P]
                if relative:
                    mid = (i + 1) * P
                    parts = [(0, lo, min(hi, mid)), (1, max(lo, mid), hi)]
                else:
                    parts = [(0, lo, hi)]
                parts = [p for p in parts if p[1] < p[2]]
                for m, (kind, a, b) in enumerate(parts):
                    last = nc.tensor.matmul(ps[:, a - lo:b - lo], lhs, ks[0:AROWS, u, kind, a:b], start=(m == 0),
                                            stop=False, skip_group_check=True)
                if relative:
                    a, b = max(lo, i * P - REL), min(hi, i * P + P + REL)
                    if a < b:
                        w = a - (i * P - REL)
                        last = nc.tensor.matmul(ps[:, a - lo:b - lo], G.ident[:, :], rel[:, u, i, w:w + b - a],
                                                start=False, stop=True, skip_group_check=True)
                elif lo <= i * P < hi:
                    last = nc.tensor.matmul(ps[:, i * P - lo:(i + 1) * P - lo], G.identb[:, :], G.mask_ij[:, :],
                                            start=False, stop=True, skip_group_check=True)
                last.then_inc(a_scored, 1)

            def begin_a(n, k, u, at):
                pe.wait_ge(loaded[u], 16 * LOADS * (k + 1))
                if relative and at >= 2:
                    pe.wait_ge(rel_ready, n - 1)

            def turn_max(n, bank, free):
                pe.wait_ge(chain, n * 5 + 5)
                pe.wait_ge(a_used, free)
                nc.tensor.transpose(a_ps[bank][0:PIECES * NS, 0:P // 2].bitcast(BF16),
                                    neg_max[:, :, :].rearrange("p c t -> p (c t)"), G.identb[:, :]
                                    ).then_inc(a_scored, 1)

            def score_keys(n, k, u, at, j):
                ps = b_ps[j % 2]
                await_count(pe, exp_done, n * NS + j - 1)
                if relative:
                    parts = [(1, 0, j * P), (0, j * P, S)]
                else:
                    parts = [(0, j * P, S)]
                cuts = [(kind, max(a, c), min(b, c + BANK), c) for c in (0, BANK) for kind, a, b in parts
                        if max(a, c) < min(b, c + BANK)]
                seen = set()
                for kind, a, b, c in cuts:
                    last = nc.tensor.matmul(ps[:, a:b], ks[0:SROWS, u, kind, j * P:(j + 1) * P],
                                            q[0:SROWS, u, a:b], start=(c not in seen), stop=False,
                                            skip_group_check=True)
                    seen.add(c)
                if relative:
                    for i, w, rows, a, b in ((j, REL, slice(0, P), 0, P), (j + 1, 0, slice(P - REL, P), 0, REL),
                                             (j - 1, REL + P, slice(0, REL), P - REL, P)):
                        if 0 <= i < NS:
                            last = nc.tensor.matmul(ps[rows, i * P + a:i * P + b],
                                                    rel[:, u, i, w:w + rows.stop - rows.start], G.ident[:, a:b],
                                                    start=False, stop=True, skip_group_check=True)
                else:
                    last = nc.tensor.matmul(ps[:, j * P:(j + 1) * P], G.identb[:, :], G.mask_ji[:, :],
                                            start=False, stop=True, skip_group_check=True)
                last.then_inc(b_scored, 1)

            def weigh_values(n, u, j):
                pe.wait_ge(exp_done, n * NS + j + 1)
                if j == 0:
                    pe.wait_ge(values_ready, n + 1)
                    await_count(pe, sum_kept, n)
                for c in range(0 if relative else j // 2, NS // 2):
                    a, b = max(2 * c * P, 0 if relative else j * P), 2 * (c + 1) * P
                    last = nc.tensor.matmul(o_ps[32 * c:32 * (c + 1), :, :].rearrange("p h q -> p (h q)")[
                        :, a - 2 * c * P:2 * P], vs[:, u, j, :], probs[:, j, a:b], start=(j == 0),
                                            stop=(j == (NS - 1 if relative else 2 * c + 1)), skip_group_check=True)
                return last

            def turn_sums(n, bank, free):
                pe.wait_ge(sum_kept, n + 1)
                pe.wait_ge(a_used, free)
                for h in range(2):
                    last = nc.tensor.transpose(a_ps[bank][:, h * P:(h + 1) * P], sumT[:, h, :], G.ident[:, :])
                last.then_inc(a_scored, 1)

            def turn_window(n, i):
                if i % 2 == 0:
                    await_count(pe, win_kept, n * 4 + i // 2)
                last = nc.tensor.transpose(win_ps[:, i % 2, REL:REL + P], probs[:, i, i * P:(i + 1) * P],
                                           G.ident[:, :])
                for side, a, b, w, keys in ((i - 1, 0, REL, 0, slice(P - REL, P)),
                                            (i + 1, P - REL, P, REL + P, slice(0, REL))):
                    if 0 <= side < NS:
                        data, pick = probs[:, side, i * P + a:i * P + b], G.ident[:, keys]
                    else:
                        data, pick = G.ident[:, a:b], G.zeros[:, 0:REL]
                    last = nc.tensor.matmul(win_ps[a:b, i % 2, w:w + REL], data, pick, start=True, stop=True,
                                            skip_group_check=True)
                return last

            def use_keys(n, u, j):
                last = weigh_values(n, u, j)
                if relative:
                    for i in ([j - 1] if j else []) + ([j] if j == NS - 1 else []):
                        last = turn_window(n, i)
                last.then_inc(pv_done, 1)

            def last_keys(n, u, at, j):
                if j >= 1:
                    use_keys(n, u, j - 1)
                elif at >= 1:
                    use_keys(n - 1, (u - 1) % RING, NS - 1)

            def head(n, k, u, at):
                pe.wait_ge(max_in[u], 16 * (k + 1))
                for j, row in enumerate(turns(n, at)):
                    score_keys(n, k, u, at, j)
                    if j == SPLIT and at + 2 < BH:
                        begin_a(n + 2, k + (u + 2) // RING, (u + 2) % RING, at + 2)
                    for m, (kind, x, ahead, turn, bank, free) in enumerate(row):
                        if relative and m == 1:
                            last_keys(n, u, at, j)
                        if kind == "piece":
                            score_piece((u + ahead) % RING, x, bank, free)
                        elif kind == "sums":
                            turn_sums(n - 1, bank, free)
                        else:
                            turn_max(n + 1, bank, free)
                    if not relative or len(row) < 2:
                        last_keys(n, u, at, j)

            if relative:
                nc.tensor.matmul(win_ps[:, :, :].rearrange("p i w -> p (i w)"), G.ident[:, :], G.zeros[
                    :, 0:1].to_broadcast([P, 2 * WIN]), start=True, stop=True)
            begin_a(0, 0, 0, 0)
            for x in range(NA):
                score_piece(0, x, x % A_BANKS, x - A_BANKS + 1)
            begin_a(1, 0, 1, 1)
            for x in range(EARLY):
                score_piece(1, x, (NA + x) % A_BANKS, NA + x - A_BANKS + 1)
            turn_max(0, (FIRST_TURNS - 1) % A_BANKS, FIRST_TURNS - A_BANKS)
            warm_up(nc, b_ps[0][:, 0:BANK], G)
            over_heads(pe, head)
            use_keys(BH - 1, RING - 1, NS - 1)
            turn_sums(BH - 1, 0, LAST_TURN)


def stage_combine(nc, G, M):
    with ExitStack() as ctx:
        def sb(name, shape, dt=F32):
            return ctx.enter_context(nc.sbuf_tensor(f"o_{name}", shape, dt))

        def sem(name):
            return ctx.enter_context(nc.semaphore(f"o_{name}"))

        def ps(name, shape):
            return ctx.enter_context(nc.psum_tensor(f"o_{name}", shape, F32))

        rv_w, by_rel = G.rv_w, G.by_rel
        by_relT = sb("by_relT", [P, 2, RCH, P])
        inv_r = sb("inv_r", [P, BH, NS])
        inv_c = sb("inv_c", [P, BH, NS])
        yc = sb("yc", [P, NT, D])
        yr = sb("yr", [P, 2, D])
        yT = sb("yT", [P, 2, 2, P])
        plus = sb("plus", [P, 2, D])
        turn_ps = [ps(f"turn_ps{i}", [P, 3, P]) for i in range(3)]
        mix_ps = ps("mix_ps", [P, D])
        yT_ps = [ps(f"yT_ps{i}", [P, 2, P]) for i in range(2)]
        out_ps = [ps(f"out_ps{i}", [P, 2, D]) for i in range(2)]
        far_placed = sem("far_placed")
        turned = sem("turned")
        turn_kept = sem("turn_kept")
        mixed = sem("mixed")
        chain = sem("chain")
        inverted = sem("inverted")
        y_ready = sem("y_ready")
        y_turned = sem("y_turned")
        yT_kept = sem("yT_kept")
        out_done = sem("out_done")
        out_kept = sem("out_kept")
        block = ctx.enter_context(nc.Block())

        @block.sync
        def _(sp):
            for t in range(BY_REL_SLOTS, NT):
                sp.wait_ge(turned, (t - BY_REL_SLOTS + 1) * 3)
                load_by_rel(sp, G, M, t)

        @block.gpsimd
        def _(pool):
            for t in range(NT):
                b, tile = divmod(t, NS)
                if t >= BY_REL_SLOTS:
                    pool.wait_ge(turned, (t - BY_REL_SLOTS + 1) * 3)
                heads = slice(b * H, (b + 1) * H)
                nc.gpsimd.tensor_tensor(by_rel[:, t % BY_REL_SLOTS, :, NREL - 1], G.far[:, heads, tile],
                                        G.att[:, heads, tile, DK + 1 + tile], ALU.add).then_inc(far_placed, 1)

        @block.scalar
        def _(act):
            for t in range(NT + 2):
                if t < NT:
                    if t >= 2:
                        act.wait_ge(mixed, t - 1)
                    for g in range(3):
                        act.wait_ge(turned, t * 3 + g + 1)
                        nc.scalar.copy(by_relT[:, t % 2, 3 * g:3 * g + 3, :], turn_ps[g][:, :, :]
                                       ).then_inc(turn_kept, 1)
                if t >= 2:
                    act.wait_ge(y_turned, t - 1)
                    if t >= 4:
                        act.wait_ge(out_done, t - 3)
                    nc.scalar.copy(yT[:, t % 2, :, :], yT_ps[t % 2][:, :, :]).then_inc(yT_kept, 1)

        @block.vector
        def _(dve):
            link = chained(dve, chain)
            nc.vector.reciprocal(inv_r[:, :, :], G.att[:, :, :, DK])
            link(nc.vector.reciprocal(inv_c[:, :, :], G.catt[:, :, :, DK]))
            for b in range(B):
                heads = slice(b * H, (b + 1) * H)
                last = nc.vector.tensor_tensor(
                    yc[:, b * NS:(b + 1) * NS, :].rearrange("p t (h d) -> p h t d", d=DK), G.catt[:, heads, :, 0:DK],
                    inv_c[:, heads, :].unsqueeze(3).to_broadcast([P, H, NS, DK]), ALU.mult)
            link(last)
            for t in range(NT + 3):
                if t < NT:
                    b, tile = divmod(t, NS)
                    heads = slice(b * H, (b + 1) * H)
                    dve.wait_ge(mixed, t + 1)
                    if t >= 2:
                        dve.wait_ge(y_turned, t - 1)
                    y = yr[:, t % 2, :].rearrange("p (h d) -> p h d", d=DK)
                    link(nc.vector.tensor_tensor(y, mix_ps[:, :].rearrange("p (h d) -> p h d", d=DK),
                                                 G.att[:, heads, tile, 0:DK], ALU.add))
                    nc.vector.tensor_tensor(y, y, inv_r[:, heads, tile].unsqueeze(2).to_broadcast([P, H, DK]),
                                            ALU.mult).then_inc(y_ready, 1)
                if t >= 3:
                    s = t - 3
                    dve.wait_ge(out_done, s + 1)
                    nc.vector.tensor_tensor(G.mixer[:, s, :], out_ps[s % 2][:, 0, :], G.row("b_o"), ALU.add)
                    link(nc.vector.tensor_tensor(plus[:, s % 2, :], out_ps[s % 2][:, 1, :], G.row("bp"), ALU.add))
                    nc.vector.tensor_tensor(G.x2[:, s, :], plus[:, s % 2, :], G.xn[:, s, :], ALU.add
                                            ).then_inc(out_kept, 1)

        @block.tensor
        def _(pe):
            def turn(t):
                pe.wait_ge(G.by_rel_in[t % BY_REL_SLOTS], 16 * (t // BY_REL_SLOTS + 1))
                pe.wait_ge(far_placed, t + 1)
                flat = by_rel[:, t % BY_REL_SLOTS, :, :].rearrange("p h r -> p (h r)")
                for c in range(RCH):
                    if t and c % 3 == 0:
                        pe.wait_ge(turn_kept, (t - 1) * 3 + c // 3 + 1)
                    rows = min(P, H * NREL - c * P)
                    if rows < P:
                        nc.tensor.transpose(turn_ps[c // 3][:, c % 3, :], G.zeros[:, 0:P], G.ident[:, :])
                    last = nc.tensor.transpose(turn_ps[c // 3][0:rows, c % 3, :], flat[:, c * P:c * P + rows],
                                               G.ident[:, :])
                    if c % 3 == 2:
                        last.then_inc(turned, 1)

            def mix(t):
                pe.wait_ge(turn_kept, (t + 1) * 3)
                if t == 0:
                    pe.wait_ge(G.rv_ready, 1)
                else:
                    pe.wait_ge(y_ready, t)
                for c in range(RCH):
                    last = nc.tensor.matmul(mix_ps[:, :], by_relT[:, t % 2, c, :], rv_w[:, 0, c, :],
                                            start=(c == 0), stop=(c == RCH - 1))
                last.then_inc(mixed, 1)

            def turn_y(t):
                pe.wait_ge(y_ready, t + 1)
                if t >= 2:
                    pe.wait_ge(yT_kept, t - 1)
                nc.tensor.transpose(yT_ps[t % 2][:, 0, :], yr[:, t % 2, :], G.ident[:, :])
                nc.tensor.transpose(yT_ps[t % 2][:, 1, :], yc[:, t, :], G.ident[:, :]).then_inc(y_turned, 1)

            def project(t):
                pe.wait_ge(yT_kept, t + 1)
                if t >= 2:
                    pe.wait_ge(out_kept, t - 1)
                nc.tensor.matmul(out_ps[t % 2][:, 0, :], yT[:, t % 2, 0, :], G.mat("r_o"), start=True, stop=True)
                nc.tensor.matmul(out_ps[t % 2][:, 1, :], yT[:, t % 2, 1, :], G.mat("c_p"), start=True,
                                 stop=True).then_inc(out_done, 1)

            warm_up(nc, turn_ps[0][:, :, :].rearrange("p c q -> p (c q)"), G)
            for t in range(NT + 3):
                if t < NT:
                    turn(t)
                if 1 <= t <= NT:
                    mix(t - 1)
                if 2 <= t <= NT + 1:
                    turn_y(t - 2)
                if t >= 3:
                    project(t - 3)


def stage_experts(nc, G, M):
    UNITS = E * QUAD
    HC = HID // P
    with ExitStack() as ctx:
        def sb(name, shape, dt=F32):
            return ctx.enter_context(nc.sbuf_tensor(f"e_{name}", shape, dt))

        def sem(name):
            return ctx.enter_context(nc.semaphore(f"e_{name}"))

        def ps(name, shape):
            return ctx.enter_context(nc.psum_tensor(f"e_{name}", shape, F32))

        N = norm_stats_tensors(sb, "n")
        h2 = sb("h2", [P, NT, D])
        h2T = sb("h2T", [P, T])
        w1 = sb("w1", [P, 2, HID])
        w2 = sb("w2", [P, 2, HC, D])
        b1 = sb("b1", [P, 2, HC])
        b2 = sb("b2", [E, D])
        mid = sb("mid", [P, 2, HC, BANK])
        logits = sb("logits", [P, NT, E])
        top = sb("top", [P, NT, E])
        top_at = sb("top_at", [P, NT, E], U32)
        top_slot = sb("top_slot", [P, NT, 2])
        gap = sb("gap", [P, NT])
        ratio = sb("ratio", [P, NT])
        share = sb("share", [P, 2, NT])
        pick = sb("pick", [P, 2, NT, E])
        gates = sb("gates", [P, NT, E])
        gatesT = sb("gatesT", [E, T])
        bank = [ps(f"bank{i}", [P, BANK]) for i in range(8)]
        weights_in = [sem(f"weights_in{i}") for i in range(2)]
        b2_in = sem("b2_in")
        layer1_in = sem("layer1_in")
        chain = sem("chain")
        var_ready = sem("var_ready")
        std_ready = sem("std_ready")
        h2_ready = sem("h2_ready")
        h2_turned = sem("h2_turned")
        h2T_kept = sem("h2T_kept")
        gated = sem("gated")
        gap_ready = sem("gap_ready")
        ratio_ready = sem("ratio_ready")
        gates_ready = sem("gates_ready")
        gates_turned = sem("gates_turned")
        gatesT_kept = sem("gatesT_kept")
        biased = sem("biased")
        bias_kept = sem("bias_kept")
        hidden = sem("hidden")
        hidden_kept = sem("hidden_kept")
        expert_done = sem("expert_done")
        expert_kept = sem("expert_kept")
        silu_ready = sem("silu_ready")
        block = ctx.enter_context(nc.Block())

        def over_experts(eng, expert):
            for slot in range(2):
                expert(slot, 0, slot, slot)
            with eng.Fori(1, E // 2 - 1) as pair:
                for slot in range(2):
                    expert(pair * 2 + slot, pair, slot, 2 + slot)
            for slot in range(2):
                expert(E - 2 + slot, E // 2 - 1, slot, E - 2 + slot)

        @block.sync
        def _(sp):
            sp.dma_start(b2[:, :], M.exp_b2).then_inc(b2_in, 16)
            sp.dma_start(G.mats1[:, :], M.mats1).then_inc(layer1_in, 16)

            def expert(e, pair, slot, at):
                if at >= 2:
                    sp.wait_ge(expert_done, e * QUAD - QUAD)
                sp.dma_start(w1[:, slot, :], bass.AP(M.exp_w1.tensor, e * (P * HID), [[HID, P], [1, HID]])
                             ).then_inc(weights_in[slot], 16)
                sp.dma_start(w2[:, slot, :, :], bass.AP(M.exp_w2.tensor, e * (P * HID), [[HID, P], [1, HID]])
                             ).then_inc(weights_in[slot], 16)
                sp.dma_start(b1[:, slot, :], bass.AP(M.cols.tensor, e * HC + EXP_B1, [[NCOLS, P], [1, HC]])
                             ).then_inc(weights_in[slot], 16)

            over_experts(sp, expert)
            sp.wait_ge(layer1_in, 16)

        @block.scalar
        def _(act):
            layer_norm_root(nc, act, N, var_ready, std_ready, 1)

            def gelu(e, pair, slot, at, c):
                unit = e * QUAD + c
                if c == 0:
                    act.wait_ge(weights_in[slot], 48 * (pair + 1))
                if at * QUAD + c >= 2:
                    act.wait_ge(expert_done, unit - 1)
                for k in range(HC):
                    act.wait_ge(hidden, unit * HC + k + 1)
                    nc.scalar.activation(mid[:, c % 2, k, :], bank[k][:, :], ACT.Gelu,
                                         bias=b1[:, slot, k:k + 1]).then_inc(hidden_kept, 1)

            gelu(0, 0, 0, 0, 0)
            act.wait_ge(gap_ready, 1)
            nc.scalar.activation(ratio[:, :], gap[:, :], ACT.Exp).then_inc(ratio_ready, 1)
            gelu(0, 0, 0, 0, 1)
            for c in range(QUAD):
                act.wait_ge(gates_turned, c + 1)
                nc.scalar.copy(gatesT[:, c * BANK:(c + 1) * BANK], bank[6 + c % 2][0:E, :]).then_inc(gatesT_kept, 1)

            def expert(e, pair, slot, at):
                for c in range(0 if at else 2, QUAD):
                    gelu(e, pair, slot, at, c)

            over_experts(act, expert)
            for t in range(0, NT, QUAD):
                act.wait_ge(expert_kept, UNITS - QUAD + t // QUAD + 1)
                nc.scalar.activation(h2[:, t:t + QUAD, :], G.x2[:, t:t + QUAD, :], ACT.Silu).then_inc(silu_ready, 1)

        @block.vector
        def _(dve):
            link = chained(dve, chain)
            layer_norm(nc, dve, link, N, G.x2, h2, var_ready, std_ready, 1, h2_ready)
            for c in range(QUAD):
                dve.wait_ge(h2_turned, c + 1)
                nc.vector.tensor_scalar(h2T[:, c * BANK:(c + 1) * BANK], bank[c % 2][:, :], G.col("ln2_g"),
                                        G.col("ln2_b"), ALU.mult, ALU.add).then_inc(h2T_kept, 1)
            dve.wait_ge(gated, 1)
            link(nc.vector.tensor_tensor(logits[:, :, :], bank[6][:, 0:NT * E].rearrange("p (t e) -> p t e", e=E),
                                         G.row("gate_b").unsqueeze(1).to_broadcast([P, NT, E]), ALU.add))
            for t in range(NT):
                last = nc.vector.max(top[:, t, :], logits[:, t, :])
            link(last)
            for t in range(NT):
                last = nc.vector.max_index(top_at[:, t, :], top[:, t, :], logits[:, t, :])
            link(last)
            link(nc.vector.tensor_copy(top_slot[:, :, :], top_at[:, :, 0:2]))
            nc.vector.tensor_tensor(gap[:, :], top[:, :, 1], top[:, :, 0], ALU.subtract).then_inc(gap_ready, 1)
            dve.wait_ge(ratio_ready, 1)
            link(nc.vector.tensor_scalar(share[:, 1, :], ratio[:, :], 1.0, None, ALU.add))
            link(nc.vector.reciprocal(share[:, 0, :], share[:, 1, :]))
            link(nc.vector.tensor_tensor(share[:, 1, :], ratio[:, :], share[:, 0, :], ALU.mult))
            slots = G.row("slots").unsqueeze(1).to_broadcast([P, NT, E])
            for i in range(2):
                link(nc.vector.tensor_tensor(pick[:, i, :, :], slots,
                                             top_slot[:, :, i].unsqueeze(2).to_broadcast([P, NT, E]), ALU.is_equal))
                link(nc.vector.tensor_tensor(pick[:, i, :, :], pick[:, i, :, :],
                                             share[:, i, :].unsqueeze(2).to_broadcast([P, NT, E]), ALU.mult))
            nc.vector.tensor_tensor(gates[:, :, :], pick[:, 0, :, :], pick[:, 1, :, :], ALU.add
                                    ).then_inc(gates_ready, 1)
            for c in range(QUAD):
                dve.wait_ge(biased, c + 1)
                tiles = G.x2[:, c * QUAD:(c + 1) * QUAD, :]
                nc.vector.tensor_tensor(tiles, tiles, bank[6 + c % 2][:, :].rearrange("p (t d) -> p t d", d=D), ALU.add
                                        ).then_inc(bias_kept, 1)

            def finish(i):
                tiles = slice(i * QUAD, (i + 1) * QUAD)
                dve.wait_ge(silu_ready, i + 1)
                link(nc.vector.tensor_tensor(h2[:, tiles, :], h2[:, tiles, :], G.mixer[:, tiles, :], ALU.mult))
                return nc.vector.tensor_tensor(G.xt[:, tiles, :], G.xt[:, tiles, :], h2[:, tiles, :], ALU.add)

            def expert(e, pair, slot, at):
                for c in range(QUAD):
                    unit = e * QUAD + c
                    dve.wait_ge(expert_done, unit + 1)
                    if at == 0:
                        dve.wait_ge(bias_kept, c + 1)
                    else:
                        dve.wait_ge(expert_kept, unit - QUAD + 1)
                    for t in range(QUAD):
                        tile = G.x2[:, c * QUAD + t, :]
                        gate = gates[:, c * QUAD + t, :]
                        last = nc.vector.scalar_tensor_tensor(tile, bank[4 + c % 2][:, t * D:(t + 1) * D],
                                                              gate[:, bass.ds(e, 1)], tile, ALU.mult, ALU.add)
                    last.then_inc(expert_kept, 1)
                    if at == E - 1 and c >= 1:
                        finish(c - 1)

            over_experts(dve, expert)
            link(finish(QUAD - 1))

        @block.tensor
        def _(pe):
            pe.wait_ge(var_ready, 1)
            warm_up(nc, bank[1][:, :], G)
            for c in range(QUAD):
                pe.wait_ge(h2_ready, c + 1)
                if c >= 2:
                    pe.wait_ge(h2T_kept, c - 1)
                for k in range(QUAD):
                    last = nc.tensor.transpose(bank[c % 2][:, k * P:(k + 1) * P], h2[:, c * QUAD + k, :],
                                               G.ident[:, :])
                last.then_inc(h2_turned, 1)
            pe.wait_ge(h2T_kept, QUAD)
            for t in range(NT):
                last = nc.tensor.matmul(bank[6][:, t * E:(t + 1) * E], h2T[:, t * P:(t + 1) * P], G.mat("gate"),
                                        start=True, stop=True)
            last.then_inc(gated, 1)

            def hidden_layer(e, pair, slot, at, c):
                unit = e * QUAD + c
                if c == 0:
                    pe.wait_ge(weights_in[slot], 48 * (pair + 1))
                for k in range(HC):
                    if at * QUAD + c >= 1:
                        pe.wait_ge(hidden_kept, unit * HC + k - 3)
                    nc.tensor.matmul(bank[k][:, :], w1[:, slot, k * P:(k + 1) * P],
                                     h2T[:, c * BANK:(c + 1) * BANK], start=True, stop=True).then_inc(hidden, 1)

            def output_layer(e, pair, slot, at, c):
                unit = e * QUAD + c
                pe.wait_ge(hidden_kept, (unit + 1) * HC)
                if at * QUAD + c >= 2:
                    pe.wait_ge(expert_kept, unit - 1)
                for t in range(QUAD):
                    for k in range(HC):
                        last = nc.tensor.matmul(bank[4 + c % 2][:, t * D:(t + 1) * D],
                                                mid[:, c % 2, k, t * P:(t + 1) * P], w2[:, slot, k, :],
                                                start=(k == 0), stop=(k == HC - 1))
                last.then_inc(expert_done, 1)

            hidden_layer(0, 0, 0, 0, 0)
            hidden_layer(0, 0, 0, 0, 1)
            output_layer(0, 0, 0, 0, 0)
            pe.wait_ge(gates_ready, 1)
            for c in range(QUAD):
                if c >= 2:
                    pe.wait_ge(gatesT_kept, c - 1)
                for k in range(QUAD):
                    last = nc.tensor.transpose(bank[6 + c % 2][0:E, k * P:(k + 1) * P],
                                               gates[:, c * QUAD + k, :], G.ident[:, :])
                last.then_inc(gates_turned, 1)
            pe.wait_ge(b2_in, 16)
            pe.wait_ge(gatesT_kept, QUAD)
            for c in range(QUAD):
                if c >= 2:
                    pe.wait_ge(bias_kept, c - 1)
                for k in range(QUAD):
                    t = c * QUAD + k
                    last = nc.tensor.matmul(bank[6 + c % 2][:, k * D:(k + 1) * D], gatesT[:, t * P:(t + 1) * P],
                                            b2[:, :], start=True, stop=True)
                last.then_inc(biased, 1)

            def expert(e, pair, slot, at):
                for c in range(QUAD):
                    if at == 0 and c == 0:
                        continue
                    if c + 1 < QUAD:
                        hidden_layer(e, pair, slot, at, c + 1)
                    elif at + 1 < E:
                        hidden_layer(e + 1, pair + slot, 1 - slot, at + 1, 0)
                    output_layer(e, pair, slot, at, c)

            over_experts(pe, expert)


def stage_linear_attention(nc, G, M):
    EPS_DEN = 1e-6
    NB = 7
    PAIRS = LH // 2
    VA = LD + 1
    PAIR_GROUPS = [range(0, 3), range(3, 6), range(6, 8)]
    NAMES = ["q0", "q1", "k0", "k1", "v0", "v1", "turn0", "turn1", "s0", "s1", "out", "s2", "s3",
             "kt0", "kt1", "num0", "num1", "num2", "st0", "st1", "st2"]
    LATE = ["turn0", "turn1", "out"]
    ACT_JOBS = [n for n in NAMES if n[:-1] in ("v", "turn", "kt")]
    DVE_JOBS = [n for n in NAMES if n not in ACT_JOBS]
    NJ = len(NAMES)
    assert NJ % NB == 0

    def count(names, t, name):
        late = sum(n in names for n in LATE)
        if isinstance(t, int) and t == 0:
            return [n for n in names if n not in LATE].index(name) + 1
        return t * len(names) + (names.index(name) + 1 - late)

    def count_tail(names, name):
        late = [n for n in LATE if n in names]
        return NT * len(names) - len(late) + late.index(name) + 1

    with ExitStack() as ctx:
        def sb(name, shape, dt=F32):
            return ctx.enter_context(nc.sbuf_tensor(f"l_{name}", shape, dt))

        def sem(name):
            return ctx.enter_context(nc.semaphore(f"l_{name}"))

        h = sb("h", [P, P])
        exps = sb("exps", [P, 4, BANK])
        qk = sb("qk", [P, 2, PAIRS, P])
        k_tok = sb("k_tok", [P, PAIRS * P])
        v = sb("v", [P, LH, VA])
        scores = sb("scores", [P, LH, P])
        state = sb("state", [P, PAIRS, 2 * VA])
        den = sb("den", [P, 3, 6])
        inv_den = sb("inv_den", [P, 3, 6])
        att = sb("att", [P, LH * LD])
        attT = sb("attT", [P, PAIRS, P])
        bank = [ctx.enter_context(nc.psum_tensor(f"l_bank{i}", [P, BANK], F32)) for i in range(NB)]
        h_in = sem("h_in")
        ones_ready = sem("ones_ready")
        state_zero = sem("state_zero")
        done = sem("done")
        exp_ready = sem("exp_ready")
        act_kept = sem("act_kept")
        dve_kept = sem("dve_kept")
        chain = sem("chain")
        block = ctx.enter_context(nc.Block())

        def over_tiles(eng, tile):
            for b in range(B):
                peeled = 2 if b == 0 else 1
                for t in range(b * NS, b * NS + peeled):
                    tile(t, t)
                with eng.Fori(b * NS + peeled, (b + 1) * NS) as t:
                    tile(t, b * NS + peeled)

        def bank_of(name):
            return bank[NAMES.index(name) % NB]

        @block.gpsimd
        def _(pool):
            nc.gpsimd.memset(v[:, :, LD:VA], 1.0).then_inc(ones_ready, 1)

            def tile(t, at):
                if at >= 1:
                    pool.wait_ge(done, count(NAMES, t - 1, "v1"))
                nc.gpsimd.tensor_copy(h[:, :], G.h1T[:, bass.ds(t * P, P)]).then_inc(h_in, 1)

            over_tiles(pool, tile)

        @block.scalar
        def _(act):
            def turned(wait_for, g):
                act.wait_ge(done, wait_for)
                nc.scalar.copy(attT[:, 4 * g:4 * g + 4, :], bank_of(f"turn{g}")[:, :].rearrange(
                    "p (c t) -> p c t", t=P)).then_inc(act_kept, 1)

            def tile(t, at):
                for i, name in enumerate(("q0", "q1", "k0", "k1")):
                    act.wait_ge(done, count(NAMES, t, name))
                    if at >= 1:
                        act.wait_ge(dve_kept, count(DVE_JOBS, t - 1, name))
                    nc.scalar.activation(exps[:, i, :], bank_of(name)[:, :], ACT.Exp).then_inc(exp_ready, 1)
                if at == 0:
                    act.wait_ge(ones_ready, 1)
                for g in range(2):
                    act.wait_ge(done, count(NAMES, t, f"v{g}"))
                    nc.scalar.copy(v[:, 8 * g:8 * g + 8, 0:LD], bank_of(f"v{g}")[:, :].rearrange(
                        "p (h d) -> p h d", d=LD)).then_inc(act_kept, 1)
                if at >= 1:
                    for g in range(2):
                        turned(count(NAMES, t, f"turn{g}"), g)
                for g in range(2):
                    act.wait_ge(done, count(NAMES, t, f"kt{g}"))
                    nc.scalar.copy(k_tok[:, g * BANK:(g + 1) * BANK], bank_of(f"kt{g}")[:, :]).then_inc(act_kept, 1)

            over_tiles(act, tile)
            for g in range(2):
                turned(count_tail(NAMES, f"turn{g}"), g)

        @block.vector
        def _(dve):
            def residual(wait_for, t):
                dve.wait_ge(done, wait_for)
                nc.vector.tensor_tensor(G.x2[:, :, :].rearrange("p t d -> p (t d)")[:, bass.ds(t * P, P)],
                                        bank_of("out")[:, 0:D],
                                        G.xn[:, :, :].rearrange("p t d -> p (t d)")[:, bass.ds(t * P, P)],
                                        ALU.add).then_inc(dve_kept, 1)

            def tile(t, at):
                link = chained(dve, chain, t * 10)
                if at in (0, NS):
                    if at:
                        dve.wait_ge(dve_kept, count(DVE_JOBS, t - 1, "st2"))
                    nc.vector.memset(state[:, :, :], 0.0).then_inc(state_zero, 1)
                    dve.wait_ge(state_zero, at // NS + 1)
                for i, name in enumerate(("q0", "q1", "k0", "k1")):
                    dve.wait_ge(exp_ready, t * 4 + i + 1)
                    link(nc.vector.tensor_scalar(exps[:, i, :], exps[:, i, :], 1.0, None, ALU.min))
                    nc.vector.scalar_tensor_tensor(
                        qk[:, i // 2, 4 * (i % 2):4 * (i % 2) + 4, :].rearrange("p c t -> p (c t)"),
                        bank_of(name)[:, :], 1.0, exps[:, i, :], ALU.add, ALU.max).then_inc(dve_kept, 1)
                for i in range(4):
                    if i == 2 and at >= 1:
                        residual(count(NAMES, t, "out"), t - 1)
                    dve.wait_ge(done, count(NAMES, t, f"s{i}"))
                    first = 8 * (i // 2) + i % 2
                    nc.vector.tensor_tensor(scores[:, first:first + 7:2, :], bank_of(f"s{i}")[:, :].rearrange(
                        "p (h t) -> p h t", t=P), G.causal01[:, :].unsqueeze(1).to_broadcast([P, 4, P]),
                        ALU.mult).then_inc(dve_kept, 1)
                for g, pairs in enumerate(PAIR_GROUPS):
                    n = 2 * len(pairs)
                    dve.wait_ge(done, count(NAMES, t, f"num{g}"))
                    sums = bank_of(f"num{g}")[:, 0:n * VA].rearrange("p (h d) -> p h d", d=VA)
                    link(nc.vector.tensor_scalar(den[:, g, 0:n], sums[:, :, LD], EPS_DEN, None, ALU.max))
                    link(nc.vector.reciprocal(inv_den[:, g, 0:n], den[:, g, 0:n]))
                    first = 2 * pairs[0] * LD
                    nc.vector.tensor_tensor(att[:, first:first + n * LD].rearrange("p (h d) -> p h d", d=LD),
                                            sums[:, :, 0:LD], inv_den[:, g, 0:n].unsqueeze(2).to_broadcast(
                                                [P, n, LD]), ALU.mult).then_inc(dve_kept, 1)
                for g, pairs in enumerate(PAIR_GROUPS):
                    dve.wait_ge(done, count(NAMES, t, f"st{g}"))
                    some = slice(pairs[0], pairs[-1] + 1)
                    part = bank_of(f"st{g}")[:, 0:len(pairs) * 2 * VA].rearrange("p (c d) -> p c d", d=2 * VA)
                    for rows, cols in ((slice(0, LD), slice(0, VA)), (slice(LD, P), slice(VA, 2 * VA))):
                        last = nc.vector.tensor_tensor(state[rows, some, cols], part[rows, :, cols],
                                                       state[rows, some, cols], ALU.add)
                    last.then_inc(dve_kept, 1)
                assert link.done[0] == 10

            over_tiles(dve, tile)
            residual(count_tail(NAMES, "out"), NT - 1)

        @block.tensor
        def _(pe):
            def free(t, at, name):
                p = NAMES.index(name) - NB
                if at == 0:
                    while p >= 0 and NAMES[p] in LATE:
                        p -= NB
                    if p < 0:
                        return
                if at == NT and p >= 0:
                    p -= NB
                before = t if p >= 0 else t - 1
                owner = NAMES[p % NJ]
                if at == 1 and p < 0 and owner in LATE:
                    owner = NAMES[p % NJ - NB]
                if owner in ACT_JOBS:
                    pe.wait_ge(act_kept, count(ACT_JOBS, before, owner))
                else:
                    pe.wait_ge(dve_kept, count(DVE_JOBS, before, owner))

            def turn_att(g):
                for c in range(4):
                    last = nc.tensor.transpose(bank_of(f"turn{g}")[:, c * P:(c + 1) * P],
                                               att[:, (4 * g + c) * P:(4 * g + c + 1) * P], G.ident[:, :])
                last.then_inc(done, 1)

            def project():
                w = G.mat1("l_o")
                for c in range(PAIRS):
                    last = nc.tensor.matmul(bank_of("out")[:, 0:D], attT[:, c, :], w[:, c * D:(c + 1) * D],
                                            start=(c == 0), stop=(c == PAIRS - 1))
                last.then_inc(done, 1)

            def tile(t, at):
                pe.wait_ge(h_in, t + 1)
                for i, name in enumerate(("q0", "q1", "k0", "k1")):
                    free(t, at, name)
                    w = G.mat1("l_q" if i < 2 else "l_k")
                    for c in range(4):
                        f = (4 * (i % 2) + c) * P
                        last = nc.tensor.matmul(bank_of(name)[:, c * P:(c + 1) * P], w[:, f:f + P], h[:, :],
                                                start=True, stop=True)
                    last.then_inc(done, 1)
                for g in range(2):
                    free(t, at, f"v{g}")
                    nc.tensor.matmul(bank_of(f"v{g}")[:, :], h[:, :], G.mat1("l_v")[:, g * BANK:(g + 1) * BANK],
                                     start=True, stop=True).then_inc(done, 1)
                if at >= 1:
                    pe.wait_ge(dve_kept, count(DVE_JOBS, t - 1, "num2"))
                    for g in range(2):
                        free(t, at, f"turn{g}")
                        turn_att(g)
                pe.wait_ge(dve_kept, count(DVE_JOBS, t, "k1"))
                for i in range(4):
                    if i == 2 and at >= 1:
                        free(t, at, "out")
                        pe.wait_ge(act_kept, count(ACT_JOBS, t, "turn1"))
                        project()
                    free(t, at, f"s{i}")
                    rows = slice(0, LD) if i % 2 == 0 else slice(LD, P)
                    for c in range(4):
                        pair = 4 * (i // 2) + c
                        last = nc.tensor.matmul(bank_of(f"s{i}")[:, c * P:(c + 1) * P], qk[rows, 1, pair, :],
                                                qk[rows, 0, pair, :], start=True, stop=True)
                    last.then_inc(done, 1)
                for g in range(2):
                    free(t, at, f"kt{g}")
                    for c in range(4):
                        last = nc.tensor.transpose(bank_of(f"kt{g}")[:, c * P:(c + 1) * P],
                                                   qk[:, 1, 4 * g + c, :], G.ident[:, :])
                    last.then_inc(done, 1)
                pe.wait_ge(act_kept, count(ACT_JOBS, t, "v1"))
                for g, pairs in enumerate(PAIR_GROUPS):
                    free(t, at, f"num{g}")
                    pe.wait_ge(dve_kept, count(DVE_JOBS, t, "s1" if pairs[-1] < 4 else "s3"))
                    for m, c in enumerate(pairs):
                        out = bank_of(f"num{g}")[:, m * 2 * VA:(m + 1) * 2 * VA]
                        nc.tensor.matmul(out, qk[:, 0, c, :], state[:, c, :], start=(m == 0), stop=False,
                                         skip_group_check=True)
                        for i in range(2):
                            last = nc.tensor.matmul(out[:, i * VA:(i + 1) * VA], scores[:, 2 * c + i, :],
                                                    v[:, 2 * c + i, :], start=False, stop=True,
                                                    skip_group_check=True)
                    last.then_inc(done, 1)
                for g, pairs in enumerate(PAIR_GROUPS):
                    free(t, at, f"st{g}")
                    pe.wait_ge(act_kept, count(ACT_JOBS, t, "kt0" if pairs[-1] < 4 else "kt1"))
                    for m, c in enumerate(pairs):
                        last = nc.tensor.matmul(bank_of(f"st{g}")[:, m * 2 * VA:(m + 1) * 2 * VA],
                                                k_tok[:, c * P:(c + 1) * P],
                                                v[:, 2 * c:2 * c + 2, :].rearrange("p h d -> p (h d)"),
                                                start=True, stop=True)
                    last.then_inc(done, 1)

            over_tiles(pe, tile)
            pe.wait_ge(dve_kept, count(DVE_JOBS, NT - 1, "num2"))
            for g in range(2):
                free(NT, NT, f"turn{g}")
                turn_att(g)
            free(NT, NT, "out")
            pe.wait_ge(act_kept, count_tail(ACT_JOBS, "turn1"))
            project()


def stage_adapters(nc, G, M):
    CLAMP_MAX = float(np.log(1.0 / 0.01))
    EPS_NORM = 1e-12
    ZW = D + PROJ + RSUM
    FC = DF // P
    with ExitStack() as ctx:
        def sb(name, shape, dt=F32):
            return ctx.enter_context(nc.sbuf_tensor(f"a_{name}", shape, dt))

        used = []

        def sem(name):
            s = ctx.enter_context(nc.semaphore(f"a_{name}"))
            used.append(s.num)
            return s

        N = norm_stats_tensors(sb, "n")
        h = sb("h", [P, NT, D])
        hT = sb("hT", [P, T])
        mid = sb("mid", [P, 2, FC, BANK])
        z = sb("z", [P, NT, ZW])
        sim = sb("sim", [PROJ, 4, NE1])
        ones = sb("ones", [PROJ, PROJ])
        up = sb("up", [RSUM, D])
        proj = sb("proj", [P, NT, PROJ])
        proj_sq = sb("proj_sq", [P, NT, PROJ])
        norms = sb("norms", [P, 4, NT])
        temp = sb("temp", [P, 2])
        projT = sb("projT", [PROJ, T])
        logits = sb("logits", [P, NT, 8])
        top = sb("top", [P, NT, 8])
        top_at = sb("top_at", [P, NT, 8], U32)
        top_slot = sb("top_slot", [P, NT])
        exps = sb("exps", [P, NT, NE1])
        total = sb("total", [P, 2, NT])
        pick = sb("pick", [P, NT, NE1])
        low = sb("low", [P, NT, RSUM])
        lowT = sb("lowT", [RSUM, T])
        gate = sb("gate", [P, NT, D])
        result = sb("result", [P, NT, D])
        bank = [ctx.enter_context(nc.psum_tensor(f"a_bank{i}", [P, BANK], F32)) for i in range(8)]
        small_in = sem("small_in")
        chain = sem("chain")
        pool_ready = sem("pool_ready")
        var_ready = sem("var_ready")
        std_ready = sem("std_ready")
        z_done = sem("z_done")
        z_kept = sem("z_kept")
        h_ready = sem("h_ready")
        h_turned = sem("h_turned")
        hT_kept = sem("hT_kept")
        hidden = sem("hidden")
        hidden_kept = sem("hidden_kept")
        ffn_done = sem("ffn_done")
        ffn_kept = sem("ffn_kept")
        sim_summed = sem("sim_summed")
        squares_ready = sem("squares_ready")
        roots_ready = sem("roots_ready")
        temp_ready = sem("temp_ready")
        temp_exp = sem("temp_exp")
        sim_ready = sem("sim_ready")
        proj_ready = sem("proj_ready")
        proj_turned = sem("proj_turned")
        projT_kept = sem("projT_kept")
        logits_done = sem("logits_done")
        margin_ready = sem("margin_ready")
        exps_ready = sem("exps_ready")
        low_ready = sem("low_ready")
        low_turned = sem("low_turned")
        lowT_kept = sem("lowT_kept")
        gate_done = sem("gate_done")
        gate_kept = sem("gate_kept")
        silu_ready = sem("silu_ready")
        result_ready = sem("result_ready")
        stored = sem("stored")
        clear_semaphores(nc, range(min(used), max(used) + 1))
        block = ctx.enter_context(nc.Block())

        @block.sync
        def _(sp):
            sp.dma_start(sim[:, 0, :], M.sim).then_inc(small_in, 16)
            sp.dma_start(up[:, :], M.up).then_inc(small_in, 16)
            out = M.out.rearrange("b (t p) d -> p (b t) d", p=P)
            for c in range(QUAD):
                sp.wait_ge(result_ready, c + 1)
                sp.dma_start(out[:, c * QUAD:(c + 1) * QUAD, :], result[:, c * QUAD:(c + 1) * QUAD, :]
                             ).then_inc(stored, 16)
            sp.wait_ge(stored, 16 * QUAD)

        @block.gpsimd
        def _(pool):
            nc.gpsimd.memset(ones[:, :], 1.0).then_inc(pool_ready, 1)
            pool.wait_ge(pool_ready, 1)
            nc.gpsimd.memset(logits[:, :, :], -3e38).then_inc(pool_ready, 1)

        @block.scalar
        def _(act):
            for i in range(NT // 2):
                act.wait_ge(z_done, i + 1)
                nc.scalar.copy(z[:, 2 * i:2 * i + 2, :], bank[6 + i % 2][:, 0:2 * ZW].rearrange(
                    "p (t w) -> p t w", w=ZW)).then_inc(z_kept, 1)
            layer_norm_root(nc, act, N, var_ready, std_ready, 1)
            act.wait_ge(sim_summed, 1)
            nc.scalar.activation(sim[:, 2, :], bank[5][0:PROJ, 0:NE1], ACT.Sqrt).then_inc(roots_ready, 1)
            act.wait_ge(squares_ready, 1)
            nc.scalar.activation(norms[:, 1, :], norms[:, 0, :], ACT.Sqrt).then_inc(roots_ready, 1)
            act.wait_ge(temp_ready, 1)
            nc.scalar.activation(temp[:, 1:2], temp[:, 0:1], ACT.Exp).then_inc(temp_exp, 1)
            for c in range(QUAD):
                act.wait_ge(proj_turned, c + 1)
                nc.scalar.copy(projT[:, c * BANK:(c + 1) * BANK], bank[6 + c % 2][0:PROJ, :]).then_inc(projT_kept, 1)

            def gelu(c):
                if c >= 2:
                    act.wait_ge(ffn_done, c - 1)
                for k in range(FC):
                    act.wait_ge(hidden, c * FC + k + 1)
                    nc.scalar.activation(mid[:, c % 2, k, :], bank[k][:, :], ACT.Gelu).then_inc(hidden_kept, 1)

            gelu(0)
            act.wait_ge(margin_ready, 1)
            nc.scalar.activation(exps[:, :, :], exps[:, :, :], ACT.Exp).then_inc(exps_ready, 1)
            gelu(1)
            gelu(2)
            for c in range(QUAD):
                act.wait_ge(low_turned, c + 1)
                nc.scalar.copy(lowT[:, c * BANK:(c + 1) * BANK], bank[6 + c % 2][0:RSUM, :]).then_inc(lowT_kept, 1)
            for c in range(QUAD):
                act.wait_ge(gate_kept, c + 1)
                tiles = slice(c * QUAD, (c + 1) * QUAD)
                nc.scalar.activation(result[:, tiles, :], gate[:, tiles, :], ACT.Silu).then_inc(silu_ready, 1)
            gelu(3)

        @block.vector
        def _(dve):
            link = chained(dve, chain)
            layer_norm(nc, dve, link, N, G.x2, h, var_ready, std_ready, 1, h_ready)
            dve.wait_ge(small_in, 32)
            nc.vector.tensor_tensor(sim[:, 1, :], sim[:, 0, :], sim[:, 0, :], ALU.mult).then_inc(h_ready, 1)
            nc.vector.tensor_scalar(temp[:, 0:1], G.row("temp"), CLAMP_MAX, None, ALU.min).then_inc(temp_ready, 1)
            dve.wait_ge(z_kept, NT // 2)
            nc.vector.tensor_tensor(proj[:, :, :], z[:, :, D:D + PROJ], G.row("router_b").unsqueeze(1).to_broadcast(
                [P, NT, PROJ]), ALU.add).then_inc(proj_ready, 1)
            for c in range(QUAD):
                dve.wait_ge(h_turned, c + 1)
                nc.vector.tensor_scalar(hT[:, c * BANK:(c + 1) * BANK], bank[c][:, :], G.col("l1_ln2_g"),
                                        G.col("l1_ln2_b"), ALU.mult, ALU.add).then_inc(hT_kept, 1)
            dve.wait_ge(proj_ready, 1)
            link(nc.vector.tensor_tensor(proj_sq[:, :, :], proj[:, :, :], proj[:, :, :], ALU.mult))
            nc.vector.tensor_reduce(norms[:, 0, :], proj_sq[:, :, :], AX.X, ALU.add).then_inc(squares_ready, 1)
            dve.wait_ge(roots_ready, 2)
            link(nc.vector.tensor_scalar(sim[:, 2, :], sim[:, 2, :], EPS_NORM, None, ALU.max))
            link(nc.vector.reciprocal(sim[:, 1, :], sim[:, 2, :]))
            nc.vector.tensor_tensor(sim[:, 3, :], sim[:, 0, :], sim[:, 1, :], ALU.mult).then_inc(sim_ready, 1)
            link(nc.vector.tensor_scalar(norms[:, 2, :], norms[:, 1, :], EPS_NORM, None, ALU.max))
            link(nc.vector.reciprocal(norms[:, 3, :], norms[:, 2, :]))
            dve.wait_ge(temp_exp, 1)
            link(nc.vector.tensor_scalar(norms[:, 3, :], norms[:, 3, :], temp[:, 1:2], None, ALU.mult))
            dve.wait_ge(pool_ready, 2)
            dve.wait_ge(logits_done, 1)
            link(nc.vector.tensor_tensor(logits[:, :, 0:NE1], bank[4][:, 0:NT * NE1].rearrange(
                "p (t e) -> p t e", e=NE1), norms[:, 3, :].unsqueeze(2).to_broadcast([P, NT, NE1]), ALU.mult))
            for t in range(NT):
                last = nc.vector.max(top[:, t, :], logits[:, t, :])
            link(last)
            nc.vector.tensor_tensor(exps[:, :, :], logits[:, :, 0:NE1], top[:, :, 0].unsqueeze(2).to_broadcast(
                [P, NT, NE1]), ALU.subtract).then_inc(margin_ready, 1)
            for t in range(NT):
                last = nc.vector.max_index(top_at[:, t, :], top[:, t, :], logits[:, t, :])
            link(last)
            link(nc.vector.tensor_copy(top_slot[:, :], top_at[:, :, 0]))
            link(nc.vector.tensor_tensor(pick[:, :, :], G.row("slots")[:, 0:NE1].unsqueeze(1).to_broadcast(
                [P, NT, NE1]), top_slot[:, :].unsqueeze(2).to_broadcast([P, NT, NE1]), ALU.is_equal))
            dve.wait_ge(exps_ready, 1)
            link(nc.vector.tensor_reduce(total[:, 0, :], exps[:, :, :], AX.X, ALU.add))
            link(nc.vector.reciprocal(total[:, 1, :], total[:, 0, :]))
            link(nc.vector.tensor_tensor(pick[:, :, :], pick[:, :, :], total[:, 1, :].unsqueeze(2).to_broadcast(
                [P, NT, NE1]), ALU.mult))
            at = 0
            for e, rank in enumerate(RANKS):
                last = nc.vector.tensor_tensor(low[:, :, at:at + rank], z[:, :, D + PROJ + at:D + PROJ + at + rank],
                                               pick[:, :, e].unsqueeze(2).to_broadcast([P, NT, rank]), ALU.mult)
                at += rank
            last.then_inc(low_ready, 1)

            def keep_ffn(c):
                tiles = slice(c * QUAD, (c + 1) * QUAD)
                dve.wait_ge(ffn_done, c + 1)
                nc.vector.tensor_tensor(G.mixer[:, tiles, :], bank[6 + c % 2][:, :].rearrange(
                    "p (t d) -> p t d", d=D), G.x2[:, tiles, :], ALU.add).then_inc(ffn_kept, 1)

            keep_ffn(0)
            keep_ffn(1)
            for c in range(QUAD):
                tiles = slice(c * QUAD, (c + 1) * QUAD)
                dve.wait_ge(gate_done, c + 1)
                nc.vector.tensor_tensor(gate[:, tiles, :], bank[4 + c % 2][:, :].rearrange("p (t d) -> p t d", d=D),
                                        z[:, tiles, 0:D], ALU.add).then_inc(gate_kept, 1)

            def finish(c):
                tiles = slice(c * QUAD, (c + 1) * QUAD)
                dve.wait_ge(silu_ready, c + 1)
                dve.wait_ge(ffn_kept, c + 1)
                link(nc.vector.tensor_tensor(result[:, tiles, :], result[:, tiles, :], G.mixer[:, tiles, :],
                                             ALU.mult))
                nc.vector.tensor_tensor(result[:, tiles, :], result[:, tiles, :], G.xt[:, tiles, :], ALU.add
                                        ).then_inc(result_ready, 1)

            finish(0)
            finish(1)
            keep_ffn(2)
            finish(2)
            keep_ffn(3)
            finish(3)

        @block.tensor
        def _(pe):
            w = G.mats1[:, MATS1["base"][0]:MATS1["base"][0] + ZW]
            for i in range(NT // 2):
                if i >= 2:
                    pe.wait_ge(z_kept, i - 1)
                for k in range(2):
                    t = 2 * i + k
                    last = nc.tensor.matmul(bank[6 + i % 2][:, k * ZW:(k + 1) * ZW], G.xnT[:, t * P:(t + 1) * P], w,
                                            start=True, stop=True)
                last.then_inc(z_done, 1)
            for c in range(QUAD):
                pe.wait_ge(h_ready, c + 1)
                for k in range(QUAD):
                    last = nc.tensor.transpose(bank[c][:, k * P:(k + 1) * P], h[:, c * QUAD + k, :], G.ident[:, :])
                last.then_inc(h_turned, 1)
            pe.wait_ge(h_ready, QUAD + 1)
            pe.wait_ge(pool_ready, 1)
            nc.tensor.matmul(bank[5][0:PROJ, 0:NE1], ones[:, :], sim[:, 1, :], start=True, stop=True
                             ).then_inc(sim_summed, 1)
            pe.wait_ge(proj_ready, 1)
            pe.wait_ge(z_kept, NT // 2)
            for c in range(QUAD):
                if c >= 2:
                    pe.wait_ge(projT_kept, c - 1)
                for k in range(QUAD):
                    last = nc.tensor.transpose(bank[6 + c % 2][0:PROJ, k * P:(k + 1) * P],
                                               proj[:, c * QUAD + k, :], G.ident[:, :])
                last.then_inc(proj_turned, 1)

            def hidden_layer(c):
                pe.wait_ge(hT_kept, QUAD)
                for k in range(FC):
                    if c >= 1:
                        pe.wait_ge(hidden_kept, (c - 1) * FC + k + 1)
                    nc.tensor.matmul(bank[k][:, :], G.mat1("f1")[:, k * P:(k + 1) * P],
                                     hT[:, c * BANK:(c + 1) * BANK], start=True, stop=True).then_inc(hidden, 1)

            def output_layer(c):
                pe.wait_ge(hidden_kept, (c + 1) * FC)
                if c >= 2:
                    pe.wait_ge(ffn_kept, c - 1)
                for k in range(QUAD):
                    for m in range(FC):
                        last = nc.tensor.matmul(bank[6 + c % 2][:, k * D:(k + 1) * D],
                                                mid[:, c % 2, m, k * P:(k + 1) * P],
                                                G.mat1("f2")[:, m * D:(m + 1) * D], start=(m == 0),
                                                stop=(m == FC - 1))
                last.then_inc(ffn_done, 1)

            hidden_layer(0)
            pe.wait_ge(projT_kept, QUAD)
            pe.wait_ge(sim_ready, 1)
            for t in range(NT):
                last = nc.tensor.matmul(bank[4][:, t * NE1:(t + 1) * NE1], projT[:, t * P:(t + 1) * P],
                                        sim[:, 3, :], start=True, stop=True)
            last.then_inc(logits_done, 1)
            hidden_layer(1)
            output_layer(0)
            hidden_layer(2)
            output_layer(1)
            pe.wait_ge(low_ready, 1)
            for c in range(QUAD):
                if c >= 2:
                    pe.wait_ge(lowT_kept, c - 1)
                else:
                    pe.wait_ge(ffn_kept, c + 1)
                for k in range(QUAD):
                    last = nc.tensor.transpose(bank[6 + c % 2][0:RSUM, k * P:(k + 1) * P], low[:, c * QUAD + k, :],
                                               G.ident[:, :])
                last.then_inc(low_turned, 1)
            for c in range(QUAD):
                pe.wait_ge(lowT_kept, c + 1)
                if c >= 2:
                    pe.wait_ge(gate_kept, c - 1)
                for k in range(QUAD):
                    t = c * QUAD + k
                    last = nc.tensor.matmul(bank[4 + c % 2][:, k * D:(k + 1) * D], lowT[:, t * P:(t + 1) * P],
                                            up[:, :], start=True, stop=True)
                last.then_inc(gate_done, 1)
            hidden_layer(3)
            output_layer(2)
            output_layer(3)


def recurrent_block_kernel(nc, out, **ins):
    def scratch(name, shape, dt=F32):
        return nc.dram_tensor(name, shape, dt).ap()

    M = Named(**ins)
    M.out = out
    M.split = scratch("split", [5, PIECES, B, P, S], BF16)
    M.rel = scratch("rel", [S, RROW])
    M.window = scratch("window", [BH, S, WIN])
    with ExitStack() as ctx:
        def sb(name, shape, dt=F32):
            return ctx.enter_context(nc.sbuf_tensor(name, shape, dt))

        G = Named()
        G.xt = sb("xt", [P, NT, D])
        G.xn = sb("xn", [P, NT, D])
        G.cols = sb("cols", [P, NCOLS])
        G.rows = sb("rows", [P, NROWS])
        G.mats = sb("mats", [P, NMATS])
        G.ident = sb("ident", [P, P])
        G.identb = sb("identb", [P, P], BF16)
        G.mask_ij = sb("mask_ij", [P, P], BF16)
        G.mask_ji = sb("mask_ji", [P, P], BF16)
        G.causal01 = sb("causal01", [P, P])
        G.far_sign = sb("far_sign", [P, P])
        G.before_last = sb("before_last", [P, P])
        G.after_first = sb("after_first", [P, P])
        G.zeros = sb("zeros", [P, P])
        G.col = lambda name: G.cols[:, COL[name]:COL[name] + 1]
        G.row = lambda name: G.rows[:, ROWS[name][0]:ROWS[name][0] + ROWS[name][1]]
        G.mat = lambda name: G.mats[:, MATS[name][0]:MATS[name][0] + MATS[name][1]]
        G.mixer = sb("mixer", [P, NT, D])
        G.x2 = sb("x2", [P, NT, D])
        with ExitStack() as layer0:
            def sb0(name, shape, dt=F32):
                return layer0.enter_context(nc.sbuf_tensor(name, shape, dt))

            G.att = sb0("att", [P, BH, NS, VCOLS])
            G.catt = sb0("catt", [P, BH, NS, DK + 1])
            G.far = sb0("far", [P, BH, NS])
            G.v_rel = sb0("v_rel", [P, BH, NS, DK])
            G.v_causal = sb0("v_causal", [P, BH, NS, DK])
            G.rel_last = sb0("rel_last", [P, B, H, NS])
            G.q = sb0("q", [SROWS, RING, S], BF16)
            G.ks = sb0("ks", [SROWS, RING, 2, S], BF16)
            G.vs = sb0("vs", [P, RING, NS, 32])
            G.r_loaded = [layer0.enter_context(nc.semaphore(f"r_loaded{i}")) for i in range(RING)]
            G.win_stored = [layer0.enter_context(nc.semaphore(f"win_stored{i}")) for i in range(2)]
            G.c_loaded = [layer0.enter_context(nc.semaphore(f"c_loaded{i}")) for i in range(RING)]
            with ExitStack() as scored:
                G.proj = scored.enter_context(nc.sbuf_tensor("proj", [P, 5, T], F32))
                G.rel = G.proj[:, 1:4, :].rearrange("p a t -> p (a t)").rearrange(
                    "p (u j w) -> p u j w", u=RING, j=NS)
                G.rel_edge = scored.enter_context(nc.sbuf_tensor("rel_edge", [P, RING, NS], F32))
                G.rel_loaded = [scored.enter_context(nc.semaphore(f"rel_loaded{i}")) for i in range(RING)]
                with ExitStack() as turned:
                    G.xnT = turned.enter_context(nc.sbuf_tensor("xnT", [P, T], F32))
                    G.h1T = turned.enter_context(nc.sbuf_tensor("h1T", [P, T], F32))
                    stage_normalize(nc, G, M, "n0", "ln1_g", "ln1_b", True)
                    stage_project(nc, G, M)
                stage_attention(nc, G, M, True)
            with ExitStack() as combined:
                G.rv_w = combined.enter_context(nc.sbuf_tensor("rv_w", [P, 2, RCH, D], F32))
                G.by_rel = combined.enter_context(nc.sbuf_tensor("by_rel", [P, BY_REL_SLOTS, H, NREL], F32))
                G.rv_in = combined.enter_context(nc.semaphore("rv_in"))
                G.rv_ready = combined.enter_context(nc.semaphore("rv_ready"))
                G.by_rel_in = [combined.enter_context(nc.semaphore(f"by_rel_in{i}"))
                               for i in range(BY_REL_SLOTS)]
                stage_attention(nc, G, M, False)
                stage_combine(nc, G, M)
        with ExitStack() as layer1:
            G.mats1 = layer1.enter_context(nc.sbuf_tensor("mats1", [P, NMATS1], F32))
            G.mat1 = lambda name: G.mats1[:, MATS1[name][0]:MATS1[name][0] + MATS1[name][1]]
            stage_experts(nc, G, M)
            G.xnT = layer1.enter_context(nc.sbuf_tensor("xnT1", [P, T], F32))
            with ExitStack() as turned:
                G.h1T = turned.enter_context(nc.sbuf_tensor("h1T1", [P, T], F32))
                stage_normalize(nc, G, M, "n1", "l1_ln1_g", "l1_ln1_b", False)
                stage_linear_attention(nc, G, M)
            stage_adapters(nc, G, M)


def layout(inputs):
    f = lambda name: np.asarray(inputs[name])
    chunks = lambda w: w.reshape(-1, P, w.shape[-1]).transpose(1, 0, 2).reshape(P, -1)
    rk, rv = f("L0_attn_rel_k_emb"), f("L0_attn_rel_v_emb")
    cols = [f("L0_ffn_ln1_g"), f("L0_ffn_ln1_b"), f("L0_ffn_ln2_g"), f("L0_ffn_ln2_b"), f("L0_ffn_bq"),
            f("L0_ffn_bk"), np.tile(rk[0], H), np.tile(rk[-1], H), f("L1_attn_ln1_g"), f("L1_attn_ln1_b"),
            f("L1_attn_ln2_g"), f("L1_attn_ln2_b"), *f("L0_ffn_exp_b1").reshape(-1, P)]
    rows = [f("L0_attn_b_o"), f("L0_ffn_bv"), f("L0_ffn_bp"), f("L0_ffn_gate_b"), np.tile(rv[0], H),
            np.tile(rv[-1], H), f("L1_ffn_bp"), f("L1_ffn_temp"), np.arange(E, dtype=np.float32)]
    mats = [f("L0_attn_Wq").T, f("L0_attn_Wk").T, f("L0_attn_Wv").T, f("L0_attn_Wo").T, f("L0_ffn_Wq"),
            f("L0_ffn_Wk"), f("L0_ffn_Wv"), f("L0_ffn_Wp"), f("L0_ffn_gate_W")]
    mats1 = [f("L1_attn_Wq"), f("L1_attn_Wk"), f("L1_attn_Wv"), chunks(f("L1_attn_Wo")), f("L1_attn_Wf1"),
             chunks(f("L1_attn_Wf2")), f("L1_ffn_W").T, f("L1_ffn_Wp").T,
             np.concatenate([f(f"L1_ffn_Wd{i}") for i in range(NE1)], 0).T]
    rk_block = np.zeros((H, DK, H, NREL), np.float32)
    rk_block_first = np.zeros((H, DK, H, NREL), np.float32)
    rv_block = np.zeros((H, NREL, H, DK), np.float32)
    rv_block_first = np.zeros((H, NREL, H, DK), np.float32)
    for h in range(H):
        rk_block[h, :, h, :] = rk.T
        rk_block_first[h, :, h, :] = np.broadcast_to(rk[0][:, None], (DK, NREL))
        rv_block[h, :, h, :] = rv
        rv_block_first[h, :, h, :] = np.broadcast_to(rv[0], (NREL, DK))
    fill = lambda w: np.concatenate([w.reshape(H * NREL, D), np.zeros((RCH * P - H * NREL, D), np.float32)], 0)
    return {
        "x": f("L0_attn_x").reshape(T, D),
        "cols": np.stack(cols, 1), "rows": np.concatenate(rows), "mats": np.concatenate(mats, 1),
        "mats1": np.concatenate(mats1, 1),
        "rk_block": rk_block.reshape(D, H * NREL), "rk_block_first": rk_block_first.reshape(D, H * NREL),
        "rv_block": chunks(fill(rv_block)), "rv_block_first": chunks(fill(rv_block_first)),
        "exp_w1": f("L0_ffn_exp_W1"), "exp_w2": f("L0_ffn_exp_W2").reshape(E, HID // P, P, D).transpose(0, 2, 1, 3),
        "exp_b2": f("L0_ffn_exp_b2"), "sim": f("L1_ffn_sim"),
        "up": np.concatenate([f(f"L1_ffn_Wu{i}").T for i in range(NE1)], 0),
    }


def kernel(**inputs):
    import concourse.bacc as bacc
    from concourse.bass_utils import run_bass_kernel_spmd

    nc = bacc.Bacc("TRN2", target_bir_lowering=False, num_devices=1)
    arrays, args = {}, {}
    for name, a in layout(inputs).items():
        arrays[f"in_{name}"] = a = np.ascontiguousarray(a)
        args[name] = nc.dram_tensor(f"in_{name}", a.shape, mybir.dt.from_np(a.dtype), kind="ExternalInput").ap()
    out = nc.dram_tensor("out", (B, S, D), F32, kind="ExternalOutput").ap()
    recurrent_block_kernel(nc, out, **args)
    result = run_bass_kernel_spmd(nc, [arrays], core_ids=[0])
    return result.results[0]["out"]
```
